# Optimizing a Trainium2 kernel written in Bass

```python
import numpy as np
import jax
import jax.numpy as jnp

def _softmax(x, axis=-1):
    return jax.nn.softmax(x, axis=axis)

def _gelu(x):
    return jax.nn.gelu(x, approximate=True)

def _silu(x):
    return jax.nn.silu(x)

def _sigmoid(x):
    return jax.nn.sigmoid(x)

def _layernorm(x, axis=-1, eps=1e-05):
    m = jnp.mean(x, axis=axis, keepdims=True)
    v = jnp.var(x, axis=axis, keepdims=True)
    return (x - m) / jnp.sqrt(v + eps)

def _scatter_add(tgt, idx, src, axis=0):
    return tgt.at[idx].add(src)

def _segment_sum(src, seg, n):
    return jax.ops.segment_sum(src, seg, n)
kernel_name = 'mk_gnn_resnorm_d4_gnn_r32_392477'

def setup_inputs(seed: int=0):
    np.random.seed(seed)
    _w = jnp.asarray

    def _rec_inputs():
        import jax
        import jax.numpy as jnp
        _gk = jax.random.key(seed)
        x = -0.000202 + 1 * jax.random.normal(jax.random.fold_in(_gk, 1), (3125, 64), jnp.float32)
        _s = jax.random.randint(jax.random.fold_in(_gk, 2), (25000,), 0, 3125, jnp.int32)
        _d = jax.random.randint(jax.random.fold_in(_gk, 3), (25000,), 0, 3125, jnp.int32)
        _loop = jnp.arange(3125, dtype=jnp.int32)
        src = jnp.concatenate([_s, _d, _loop])
        dst = jnp.concatenate([_d, _s, _loop])
        _o = jnp.argsort(dst, stable=True)
        src = src[_o]
        dst = dst[_o]
        edge_attr_16 = 0.000283511 + 1.00007 * jax.random.normal(jax.random.fold_in(_gk, 11), (53125, 16), jnp.float32)
        return (x, src, dst, edge_attr_16)
    x, src, dst, edge_attr_16 = _rec_inputs()

    def _L0_gnn_setup():
        import jax, jax.numpy as jnp
        import numpy as np
        N_NODES = 3125
        N_EDGES = 31250
        IN_DIM = 64
        OUT_DIM = 64
        BN_EPS = 1e-05
        key = jax.random.key(seed)
        ks = jax.random.split(key, 8)
        x = jax.random.normal(ks[0], (N_NODES, IN_DIM), dtype=jnp.float32)
        edge_index = jax.random.randint(ks[1], (2, N_EDGES), 0, N_NODES, dtype=jnp.int64)
        s1 = 1.0 / np.sqrt(IN_DIM)
        s2 = 1.0 / np.sqrt(OUT_DIM)
        W1 = jax.random.uniform(ks[2], (IN_DIM, OUT_DIM), jnp.float32, -s1, s1)
        b1 = jax.random.uniform(ks[3], (OUT_DIM,), jnp.float32, -s1, s1)
        W2 = jax.random.uniform(ks[4], (OUT_DIM, OUT_DIM), jnp.float32, -s2, s2)
        b2 = jax.random.uniform(ks[5], (OUT_DIM,), jnp.float32, -s2, s2)
        gamma = jnp.ones((OUT_DIM,), jnp.float32)
        beta = jnp.zeros((OUT_DIM,), jnp.float32)
        return {'x': x, 'edge_index': edge_index, 'W1': W1, 'b1': b1, 'W2': W2, 'b2': b2, 'gamma': gamma, 'beta': beta}
    _L0_gnn_all = _L0_gnn_setup()
    _L0_gnn_in = {k: v for k, v in _L0_gnn_all.items() if k in ('W1', 'b1', 'W2', 'b2', 'gamma', 'beta')}
    del _L0_gnn_all

    def _L1_gnn_setup():
        import jax, jax.numpy as jnp
        import numpy as np
        N = 3125
        E = 50000
        IN, HID, OUT = (64, 256, 64)
        key = jax.random.key(seed)
        ks = jax.random.split(key, 8)
        x = jax.random.normal(ks[0], (N, IN), dtype=jnp.float32)
        edge_index = jax.random.randint(ks[1], (2, E), 0, N, dtype=jnp.int64)

        def lin(k, fan_in, fan_out):
            bound = 1.0 / np.sqrt(fan_in)
            kw, kb = jax.random.split(k)
            W = jax.random.uniform(kw, (fan_in, fan_out), minval=-bound, maxval=bound, dtype=jnp.float32)
            b = jax.random.uniform(kb, (fan_out,), minval=-bound, maxval=bound, dtype=jnp.float32)
            return (W, b)
        W1, b1 = lin(ks[2], IN, HID)
        W2, b2 = lin(ks[3], HID, HID)
        W3, b3 = lin(ks[4], HID, OUT)
        return {'x': x, 'edge_index': edge_index, 'W1': W1, 'b1': b1, 'W2': W2, 'b2': b2, 'W3': W3, 'b3': b3}
    _L1_gnn_all = _L1_gnn_setup()
    _L1_gnn_in = {k: v for k, v in _L1_gnn_all.items() if k in ('W1', 'b1', 'W2', 'b2', 'W3', 'b3')}
    del _L1_gnn_all

    def _L2_gnn_setup():
        import jax, jax.numpy as jnp
        import numpy as np
        N_NODES = 3125
        N_EDGES = 37500
        HID = 64
        EDGE_DIM = 16
        N_LAYERS = 3

        def _gru_cell(x, h, Wih, Whh, bih, bhh):
            gi = x @ Wih + bih
            gh = h @ Whh + bhh
            gi_r, gi_z, gi_n = jnp.split(gi, 3, axis=-1)
            gh_r, gh_z, gh_n = jnp.split(gh, 3, axis=-1)
            r = jax.nn.sigmoid(gi_r + gh_r)
            z = jax.nn.sigmoid(gi_z + gh_z)
            n = jnp.tanh(gi_n + r * gh_n)
            return (1.0 - z) * n + z * h
        key = jax.random.key(seed)
        ks = jax.random.split(key, 16)
        s = 0.1
        return {'node_features': jax.random.normal(ks[0], (N_NODES, HID), jnp.float32), 'edge_index': jax.random.randint(ks[1], (2, N_EDGES), 0, N_NODES, jnp.int32), 'edge_features': jax.random.normal(ks[2], (N_EDGES, EDGE_DIM), jnp.float32), 'enc_W': jax.random.normal(ks[3], (HID, HID), jnp.float32) * s, 'enc_b': jnp.zeros((HID,), jnp.float32), 'msg_W1': jax.random.normal(ks[4], (N_LAYERS, 2 * HID + EDGE_DIM, HID), jnp.float32) * s, 'msg_b1': jnp.zeros((N_LAYERS, HID), jnp.float32), 'msg_W2': jax.random.normal(ks[5], (N_LAYERS, HID, HID), jnp.float32) * s, 'msg_b2': jnp.zeros((N_LAYERS, HID), jnp.float32), 'gru_Wih': jax.random.normal(ks[6], (N_LAYERS, HID, 3 * HID), jnp.float32) * s, 'gru_Whh': jax.random.normal(ks[7], (N_LAYERS, HID, 3 * HID), jnp.float32) * s, 'gru_bih': jnp.zeros((N_LAYERS, 3 * HID), jnp.float32), 'gru_bhh': jnp.zeros((N_LAYERS, 3 * HID), jnp.float32), 'ro_W1': jax.random.normal(ks[8], (HID, HID), jnp.float32) * s, 'ro_b1': jnp.zeros((HID,), jnp.float32), 'ro_W2': jax.random.normal(ks[9], (HID, HID), jnp.float32) * s, 'ro_b2': jnp.zeros((HID,), jnp.float32)}
    _L2_gnn_all = _L2_gnn_setup()
    _L2_gnn_in = {k: v for k, v in _L2_gnn_all.items() if k in ('enc_W', 'enc_b', 'msg_W1', 'msg_b1', 'msg_W2', 'msg_b2', 'gru_Wih', 'gru_Whh', 'gru_bih', 'gru_bhh', 'ro_W1', 'ro_b1', 'ro_W2', 'ro_b2')}
    del _L2_gnn_all

    def _L3_gnn_setup():
        import jax, jax.numpy as jnp
        import numpy as np
        NEG_SLOPE = 0.2

        def _gat_layer(x, src, dst, n_nodes, W, a_src, a_dst, b):
            h = x @ W
            alpha_s = h @ a_src
            alpha_d = h @ a_dst
            e = jax.nn.leaky_relu(alpha_s[src] + alpha_d[dst], NEG_SLOPE)
            m = jax.ops.segment_max(e, dst, num_segments=n_nodes)
            w = jnp.exp(e - m[dst])
            z = jax.ops.segment_sum(w, dst, num_segments=n_nodes)
            alpha = w / (z[dst] + 1e-16)
            out = jax.ops.segment_sum(alpha[:, None] * h[src], dst, num_segments=n_nodes)
            return out + b
        key = jax.random.key(seed)
        N, E, D_IN, D_H, D_OUT = (50000, 25000, 64, 64, 64)
        ks = jax.random.split(key, 12)
        x = jax.random.normal(ks[0], (N, D_IN), dtype=jnp.float32)
        edge_index = jax.random.randint(ks[1], (2, E), 0, N, dtype=jnp.int64)
        s = 1.0 / np.sqrt(D_IN)
        W1 = jax.random.normal(ks[2], (D_IN, D_H), dtype=jnp.float32) * s
        a_src1 = jax.random.normal(ks[3], (D_H,), dtype=jnp.float32) * s
        a_dst1 = jax.random.normal(ks[4], (D_H,), dtype=jnp.float32) * s
        b1 = jnp.zeros((D_H,), dtype=jnp.float32)
        s2 = 1.0 / np.sqrt(D_H)
        W2 = jax.random.normal(ks[5], (D_H, D_OUT), dtype=jnp.float32) * s2
        a_src2 = jax.random.normal(ks[6], (D_OUT,), dtype=jnp.float32) * s2
        a_dst2 = jax.random.normal(ks[7], (D_OUT,), dtype=jnp.float32) * s2
        b2 = jnp.zeros((D_OUT,), dtype=jnp.float32)
        return {'x': x, 'edge_index': edge_index, 'W1': W1, 'a_src1': a_src1, 'a_dst1': a_dst1, 'b1': b1, 'W2': W2, 'a_src2': a_src2, 'a_dst2': a_dst2, 'b2': b2}
    _L3_gnn_all = _L3_gnn_setup()
    _L3_gnn_in = {k: v for k, v in _L3_gnn_all.items() if k in ('W1', 'a_src1', 'a_dst1', 'b1', 'W2', 'a_src2', 'a_dst2', 'b2')}
    del _L3_gnn_all
    return {'x': x, 'src': src, 'dst': dst, 'edge_attr_16': edge_attr_16, 'L0_gnn_W1': _L0_gnn_in['W1'], 'L0_gnn_b1': _L0_gnn_in['b1'], 'L0_gnn_W2': _L0_gnn_in['W2'], 'L0_gnn_b2': _L0_gnn_in['b2'], 'L0_gnn_gamma': _L0_gnn_in['gamma'], 'L0_gnn_beta': _L0_gnn_in['beta'], 'L1_gnn_W1': _L1_gnn_in['W1'], 'L1_gnn_b1': _L1_gnn_in['b1'], 'L1_gnn_W2': _L1_gnn_in['W2'], 'L1_gnn_b2': _L1_gnn_in['b2'], 'L1_gnn_W3': _L1_gnn_in['W3'], 'L1_gnn_b3': _L1_gnn_in['b3'], 'L2_gnn_enc_W': _L2_gnn_in['enc_W'], 'L2_gnn_enc_b': _L2_gnn_in['enc_b'], 'L2_gnn_msg_W1': _L2_gnn_in['msg_W1'], 'L2_gnn_msg_b1': _L2_gnn_in['msg_b1'], 'L2_gnn_msg_W2': _L2_gnn_in['msg_W2'], 'L2_gnn_msg_b2': _L2_gnn_in['msg_b2'], 'L2_gnn_gru_Wih': _L2_gnn_in['gru_Wih'], 'L2_gnn_gru_Whh': _L2_gnn_in['gru_Whh'], 'L2_gnn_gru_bih': _L2_gnn_in['gru_bih'], 'L2_gnn_gru_bhh': _L2_gnn_in['gru_bhh'], 'L2_gnn_ro_W1': _L2_gnn_in['ro_W1'], 'L2_gnn_ro_b1': _L2_gnn_in['ro_b1'], 'L2_gnn_ro_W2': _L2_gnn_in['ro_W2'], 'L2_gnn_ro_b2': _L2_gnn_in['ro_b2'], 'L3_gnn_W1': _L3_gnn_in['W1'], 'L3_gnn_a_src1': _L3_gnn_in['a_src1'], 'L3_gnn_a_dst1': _L3_gnn_in['a_dst1'], 'L3_gnn_b1': _L3_gnn_in['b1'], 'L3_gnn_W2': _L3_gnn_in['W2'], 'L3_gnn_a_src2': _L3_gnn_in['a_src2'], 'L3_gnn_a_dst2': _L3_gnn_in['a_dst2'], 'L3_gnn_b2': _L3_gnn_in['b2']}

def reference(x, src, dst, edge_attr_16, L0_gnn_W1, L0_gnn_b1, L0_gnn_W2, L0_gnn_b2, L0_gnn_gamma, L0_gnn_beta, L1_gnn_W1, L1_gnn_b1, L1_gnn_W2, L1_gnn_b2, L1_gnn_W3, L1_gnn_b3, L2_gnn_enc_W, L2_gnn_enc_b, L2_gnn_msg_W1, L2_gnn_msg_b1, L2_gnn_msg_W2, L2_gnn_msg_b2, L2_gnn_gru_Wih, L2_gnn_gru_Whh, L2_gnn_gru_bih, L2_gnn_gru_bhh, L2_gnn_ro_W1, L2_gnn_ro_b1, L2_gnn_ro_W2, L2_gnn_ro_b2, L3_gnn_W1, L3_gnn_a_src1, L3_gnn_a_dst1, L3_gnn_b1, L3_gnn_W2, L3_gnn_a_src2, L3_gnn_a_dst2, L3_gnn_b2):
    import jax
    import jax.numpy as jnp

    def _L0_gnn_ref(x, edge_index, W1, b1, W2, b2, gamma, beta):
        import jax, jax.numpy as jnp
        import numpy as np
        N_NODES = 3125
        N_EDGES = 31250
        IN_DIM = 64
        OUT_DIM = 64
        BN_EPS = 1e-05
        src, dst = (edge_index[0], edge_index[1])
        agg = jax.ops.segment_sum(x[src], dst, num_segments=N_NODES)
        h = x + agg
        h = jax.nn.relu(h @ W1 + b1) @ W2 + b2
        mean = jnp.mean(h, axis=0)
        var = jnp.var(h, axis=0)
        h = (h - mean) * jax.lax.rsqrt(var + BN_EPS) * gamma + beta
        return jax.nn.relu(h)

    def _L1_gnn_ref(x, edge_index, W1, b1, W2, b2, W3, b3):
        import jax, jax.numpy as jnp
        import numpy as np
        N = 3125
        E = 50000
        IN, HID, OUT = (64, 256, 64)
        src, dst = (edge_index[0], edge_index[1])
        agg = jax.ops.segment_sum(x[src], dst, num_segments=x.shape[0])
        h = x + agg
        h = jax.nn.relu(h @ W1 + b1)
        h = jax.nn.relu(h @ W2 + b2)
        return h @ W3 + b3

    def _L2_gnn_ref(node_features, edge_index, edge_features, enc_W, enc_b, msg_W1, msg_b1, msg_W2, msg_b2, gru_Wih, gru_Whh, gru_bih, gru_bhh, ro_W1, ro_b1, ro_W2, ro_b2):
        import jax, jax.numpy as jnp
        import numpy as np
        N_NODES = 3125
        N_EDGES = 37500
        HID = 64
        EDGE_DIM = 16
        N_LAYERS = 3

        def _gru_cell(x, h, Wih, Whh, bih, bhh):
            gi = x @ Wih + bih
            gh = h @ Whh + bhh
            gi_r, gi_z, gi_n = jnp.split(gi, 3, axis=-1)
            gh_r, gh_z, gh_n = jnp.split(gh, 3, axis=-1)
            r = jax.nn.sigmoid(gi_r + gh_r)
            z = jax.nn.sigmoid(gi_z + gh_z)
            n = jnp.tanh(gi_n + r * gh_n)
            return (1.0 - z) * n + z * h
        src, dst = (edge_index[0], edge_index[1])
        n_nodes = node_features.shape[0]
        h = node_features @ enc_W + enc_b
        for l in range(N_LAYERS):
            cat = jnp.concatenate([h[src], h[dst], edge_features], axis=-1)
            m = jax.nn.relu(cat @ msg_W1[l] + msg_b1[l]) @ msg_W2[l] + msg_b2[l]
            agg = jax.ops.segment_sum(m, dst, num_segments=n_nodes)
            h = _gru_cell(agg, h, gru_Wih[l], gru_Whh[l], gru_bih[l], gru_bhh[l])
        return jax.nn.relu(h @ ro_W1 + ro_b1) @ ro_W2 + ro_b2

    def _L3_gnn_ref(x, edge_index, W1, a_src1, a_dst1, b1, W2, a_src2, a_dst2, b2):
        import jax, jax.numpy as jnp
        import numpy as np
        NEG_SLOPE = 0.2

        def _gat_layer(x, src, dst, n_nodes, W, a_src, a_dst, b):
            h = x @ W
            alpha_s = h @ a_src
            alpha_d = h @ a_dst
            e = jax.nn.leaky_relu(alpha_s[src] + alpha_d[dst], NEG_SLOPE)
            m = jax.ops.segment_max(e, dst, num_segments=n_nodes)
            w = jnp.exp(e - m[dst])
            z = jax.ops.segment_sum(w, dst, num_segments=n_nodes)
            alpha = w / (z[dst] + 1e-16)
            out = jax.ops.segment_sum(alpha[:, None] * h[src], dst, num_segments=n_nodes)
            return out + b
        n_nodes = x.shape[0]
        loops = jnp.arange(n_nodes, dtype=edge_index.dtype)
        src = jnp.concatenate([edge_index[0], loops])
        dst = jnp.concatenate([edge_index[1], loops])
        h = _gat_layer(x, src, dst, n_nodes, W1, a_src1, a_dst1, b1)
        h = jax.nn.relu(h)
        out = _gat_layer(h, src, dst, n_nodes, W2, a_src2, a_dst2, b2)
        return out
    edge_index = jnp.stack([src, dst])
    x = _layernorm(x + _L0_gnn_ref(x, edge_index, L0_gnn_W1, L0_gnn_b1, L0_gnn_W2, L0_gnn_b2, L0_gnn_gamma, L0_gnn_beta), axis=-1)
    x = _layernorm(x + _L1_gnn_ref(x, edge_index, L1_gnn_W1, L1_gnn_b1, L1_gnn_W2, L1_gnn_b2, L1_gnn_W3, L1_gnn_b3), axis=-1)
    x = _layernorm(x + _L2_gnn_ref(x, edge_index, edge_attr_16, L2_gnn_enc_W, L2_gnn_enc_b, L2_gnn_msg_W1, L2_gnn_msg_b1, L2_gnn_msg_W2, L2_gnn_msg_b2, L2_gnn_gru_Wih, L2_gnn_gru_Whh, L2_gnn_gru_bih, L2_gnn_gru_bhh, L2_gnn_ro_W1, L2_gnn_ro_b1, L2_gnn_ro_W2, L2_gnn_ro_b2), axis=-1)
    x = _layernorm(x + _L3_gnn_ref(x, edge_index, L3_gnn_W1, L3_gnn_a_src1, L3_gnn_a_dst1, L3_gnn_b1, L3_gnn_W2, L3_gnn_a_src2, L3_gnn_a_dst2, L3_gnn_b2), axis=-1)
    return x

_drawn_inputs = setup_inputs


def setup_inputs(seed=0):
    import zlib

    import numpy as np

    out = dict(_drawn_inputs(seed))
    spreads = {'L0_gnn_gamma': (1.0, 0.2),
     'L0_gnn_beta': (0.0, 0.1),
     'L2_gnn_enc_b': (0.0, 0.1),
     'L2_gnn_msg_b1': (0.0, 0.1),
     'L2_gnn_msg_b2': (0.0, 0.1),
     'L2_gnn_gru_bih': (0.0, 0.302),
     'L2_gnn_gru_bhh': (0.0, 0.365),
     'L2_gnn_ro_b1': (0.0, 0.1),
     'L2_gnn_ro_b2': (0.0, 0.1),
     'L3_gnn_b1': (0.0, 0.1),
     'L3_gnn_b2': (0.0, 0.1)}
    factors = {'L0_gnn_b2': 8.0,
     'L1_gnn_b1': 3.453,
     'L3_gnn_a_dst1': 3.891,
     'L3_gnn_a_src2': 3.719,
     'L3_gnn_a_dst2': 8.0}
    for name, (base, spread) in spreads.items():
        noise = np.random.default_rng([zlib.crc32(name.encode()), seed]).standard_normal(out[name].shape)
        drawn = base * np.exp(spread * noise) if base else spread * noise
        out[name] = jnp.asarray(drawn.astype(out[name].dtype))
    for name, factor in factors.items():
        out[name] = (out[name] * factor).astype(out[name].dtype)
    return out
```

```python
from contextlib import ExitStack

import concourse.bass as bass
from concourse import mybir

F32 = mybir.dt.float32
I32 = mybir.dt.int32
ALU = mybir.AluOpType
ACT = mybir.ActivationFunctionType
AX = mybir.AxisListType

P = 128
N, E, D = 3125, 53125, 64
NT = -(-N // P)
NP = NT * P
L = -(-E // P)
COLS, SLOTS = 8, 2
L = -(-L // (COLS * SLOTS)) * COLS * SLOTS
EP = P * L
NG = L // COLS
TRIPS = NG // SLOTS
W = D + 1
WG = D + 2
HID = 256
EF = 16
CH = 512
NC = -(-NP // CH)
BN_EPS = LN_EPS = 1e-5
SLOPE = 0.2
BIG = 1e30
NLAYER = 3
ZERO_STORES = -(-L * D // NP) + 1
PARTS = 4
LP = L // PARTS
UNROLL = 5
SKIP = 1 << 20

STAGES = [("l0_carry", "V"), ("l0_T", "A"), ("l0_w1", "A"), ("l0_w2", "A"), ("l0_back", "V"),
          ("l1_carry", "V"), ("l1_T", "A"), ("l1_w1a", "A"), ("l1_w1b", "A"), ("l1_w2a", "A"), ("l1_w2b", "A"),
          ("l1_w3", "A"), ("l1_back", "V"), ("l2_T", "A"), ("l2_enc", "A")]
for _l in range(NLAYER):
    STAGES += [(f"pq{_l}", "V"), (f"carry{_l}", "V"), (f"T{_l}", "A"), (f"agg{_l}", "A"), (f"r{_l}", "A"),
               (f"z{_l}", "A"), (f"gh{_l}", "V"), (f"gi{_l}", "V")]
STAGES += [("ro1", "A"), ("ro2", "A"), ("l2_back", "V")]
for _l in range(2):
    STAGES += [(f"gT{_l}", "A"), (f"gh_w{_l}", "V"), (f"gcarry{_l}", "V")]
INDEX = {name: k for k, (name, _) in enumerate(STAGES)}


def tiles(c):
    return range(c * CH // P, min(NT, (c + 1) * CH // P))


def cols(c):
    return slice(c * CH, min(NP, (c + 1) * CH))


class Chain:

    def __init__(self, eng, sem):
        self.eng, self.sem, self.n, self.base = eng, sem, 0, None

    def value(self):
        return self.n if self.base is None else self.base + self.n

    def link(self, ins):
        ins.then_inc(self.sem, 1)
        self.n += 1
        self.eng.wait_ge(self.sem, self.value())

    def loop(self, i, per_trip):
        self.start, self.per_trip = self.n, per_trip
        self.base, self.n = i * per_trip, self.start

    def end(self, trips):
        assert self.n == self.start + self.per_trip, self.n - self.start
        self.base, self.n = None, self.start + trips * self.per_trip


def build(nc, a, out):
    with ExitStack() as ctx:
        ctx.enter_context(nc.allow_non_contiguous_dma(reason="a few columns of one value per partition"))

        def sb(name, shape, dt=F32):
            return ctx.enter_context(nc.sbuf_tensor(name, shape, dt))

        def sem(name):
            return ctx.enter_context(nc.semaphore(name))

        def dram(name, shape, dt=F32):
            return nc.dram_tensor(name, shape, dt, kind="Internal").ap()

        tab = [dram(f"tab{k}", (NP, WG if k >= 5 else D)) for k in range(7)]
        qtab = [dram(f"qtab{l}", (NP, D)) for l in range(NLAYER)]
        adtab = [dram(f"adtab{l}", (NP, 2)) for l in range(2)]
        q_at_start = dram("q_at_start", (EP, D))
        ad_at_start = dram("ad_at_start", (EP, 2))
        sums = dram("sums", (EP, D))
        sums_w = dram("sums_w", (EP, WG))
        first_d = dram("first_d", (NP + 1, 1))

        big = sb("big", [P, L * WG])
        FM = [big[:, k * NP:(k + 1) * NP] for k in range(8)]
        spans = sb("spans", [P, NP])
        src_i = sb("src_i", [P, L], I32)
        dst_i = sb("dst_i", [P, L], I32)
        dst_f = sb("dst_f", [P, L])
        same = sb("same", [P, L])
        pen_f = sb("pen_f", [P, L])
        pen_b = sb("pen_b", [P, L])
        logit = sb("logit", [P, L])
        ad_e = sb("ad_e", [P, L, 2])
        mx_f = sb("mx_f", [P, L])
        mx_b = sb("mx_b", [P, L])
        wgt = sb("wgt", [P, L])
        xN = sb("xN", [P, NT, D])
        yN = sb("yN", [P, NT, W])
        gN = sb("gN", [P, NT, WG])
        ringG = sb("ringG", [P, SLOTS, COLS * WG])
        ringQ = sb("ringQ", [P, SLOTS, COLS * D])
        ringE = sb("ringE", [EF, SLOTS, COLS * P])
        idx_s = sb("idx_s", [P, SLOTS, COLS], I32)
        carry = sb("carry", [P, D])
        carry_q = sb("carry_q", [P, D])
        q_row = sb("q_row", [P, NLAYER, D])
        ad_row = sb("ad_row", [P, 2, 2])
        ident = sb("ident", [P, P])
        ones = sb("ones", [P, 1])
        node_i = sb("node_i", [P, NT], I32)
        node_f = sb("node_f", [P, NT])
        edge_row_i = sb("edge_row_i", [P, NT], I32)
        edge_row = sb("edge_row", [P, NT])
        count = sb("count", [P, NT])
        first = sb("first", [P, NT])
        nxt = sb("nxt", [P, NT])
        has = sb("has", [P, NT])
        deg = sb("deg", [P, NT])
        tmp = sb("tmp", [P, NT])
        start_i = sb("start_i", [P, NT], I32)
        end_i = sb("end_i", [P, NT], I32)
        tail = sb("tail", [P, 2])
        tail_i = sb("tail_i", [P, 2], I32)
        beside_i = sb("beside_i", [P, 2], I32)
        beside = sb("beside", [P, 2])
        flag = sb("flag", [P, 6])
        stat = sb("stat", [P, NT])
        rstd = sb("rstd", [P, NT])
        adN = sb("adN", [P, NT, 2])
        self_w = sb("self_w", [P, NT])
        self_s = sb("self_s", [P, NT])
        edge_carry = sb("edge_carry", [P, 2])
        pen_row = sb("pen_row", [1, 2, P])
        val_row = sb("val_row", [1, 2, P])
        car_row = sb("car_row", [1, 2, P + 1])
        edge_end = sb("edge_end", [1, 1])
        bn = sb("bn", [D, 6])
        w01, w02 = sb("w01", [D, D]), sb("w02", [D, D])
        c0 = sb("c0", [D, 4])
        w11 = sb("w11", [D, HID])
        w12 = sb("w12", [P, 2, HID])
        w13 = sb("w13", [P, 2, D])
        c1 = sb("c1", [P, 4])
        c13 = sb("c13", [D, 1])
        enc_w, enc_b = sb("enc_w", [D, D]), sb("enc_b", [D, 1])
        w_pq = sb("w_pq", [D, NLAYER, 2 * D])
        w_e = sb("w_e", [EF, NLAYER, D])
        b_pq = sb("b_pq", [P, NLAYER, 2 * D])
        w_m2 = sb("w_m2", [W, NLAYER, D])
        w_ih, w_hh = sb("w_ih", [D, NLAYER, 3 * D]), sb("w_hh", [D, NLAYER, 3 * D])
        b_ih, b_hh = sb("b_ih", [D, NLAYER, 3]), sb("b_hh", [D, NLAYER, 3])
        b_rz = sb("b_rz", [D, NLAYER, 3])
        ro1, ro2, c_ro = sb("ro1", [D, D]), sb("ro2", [D, D]), sb("c_ro", [D, 2])
        gw = sb("gw", [D, 2, D])
        g_src, g_dst, g_b = sb("g_src", [P, 2, D]), sb("g_dst", [P, 2, D]), sb("g_b", [P, 2, D])

        ps = ctx.enter_context(nc.psum_tensor("ps", [P, 8, 512], F32))

        edges_in, x_in, weights_in = sem("edges_in"), sem("x_in"), sem("weights_in")
        consts_made = sem("consts_made")
        zero_made, zeros_out = sem("zero_made"), sem("zeros_out")
        act_slots_open = sem("act_slots_open")
        rows_before = sem("rows_before")
        counts_ready = sem("counts_ready")
        edge_rows_ready, edge_rows_in = sem("edge_rows_ready"), sem("edge_rows_in")
        first_ready, first_out, first_in = sem("first_ready"), sem("first_out"), sem("first_in")
        prep_done = sem("prep_done")
        pens_ready, pens_turned = sem("pens_ready"), sem("pens_turned")
        filled, drained_a, drained_v = sem("filled"), sem("drained_a"), sem("drained_v")
        vchain = sem("vchain")
        staged = sem("staged")
        turn, turn_a = sem("turn"), sem("turn_a")
        gathered = [sem(f"gathered{s}") for s in range(SLOTS)]
        slot_open = [sem(f"slot_open{s}") for s in range(SLOTS)]
        q_in = [sem(f"q_in{s}") for s in range(SLOTS)]
        ef_in = [sem(f"ef_in{s}") for s in range(SLOTS)]
        edge_product = sem("edge_product")
        edge_summed = sem("edge_summed")
        summed = sem("summed")
        weighted_out = sem("weighted_out")
        multiplied, scanned = sem("multiplied"), sem("scanned")
        self_ready, self_done = sem("self_ready"), sem("self_done")
        sums_in = sem("sums_in")
        table_ready, table_out, qtable_out = sem("table_ready"), sem("table_out"), sem("qtable_out")
        q_scattered, q_row_in, q_row_out = sem("q_scattered"), sem("q_row_in"), sem("q_row_out")
        ad_ready, adtab_out, ad_scattered = sem("ad_ready"), sem("adtab_out"), sem("ad_scattered")
        ad_row_in, ad_in = sem("ad_row_in"), sem("ad_in")
        maxima_ready, maxima_turned = sem("maxima_ready"), sem("maxima_turned")
        carries_ready, carries_turned = sem("carries_ready"), sem("carries_turned")
        gap_ready, weights_ready = sem("gap_ready"), sem("weights_ready")
        var_ready, std_ready = sem("var_ready"), sem("std_ready")
        bn_scale_ready, bn_done = sem("bn_scale_ready"), sem("bn_done")
        node_ready = sem("node_ready")
        gate_ready, cell_in, state_ready = sem("gate_ready"), sem("cell_in"), sem("state_ready")
        out_ready, out_done = sem("out_ready"), sem("out_done")

        def fill_count(name, c):
            return NC * INDEX[name] + c + 1

        def drained(name, c):
            k = INDEX[name]
            who = STAGES[k][1]
            before = sum(1 for _, w in STAGES[:k] if w == who)
            return (drained_a if who == "A" else drained_v), NC * before + c + 1

        src_d, dst_d, x_d, ef_d = a["src"], a["dst"], a["x"], a["edge_attr_16"]
        table_x = lambda k: tab[k].rearrange("(t p) d -> p t d", p=P)
        sums_g = sums.rearrange("(p l) d -> p (l d)", p=P)
        sums_wg = sums_w.rearrange("(p l) d -> p (l d)", p=P)
        q_g = q_at_start.rearrange("(p l) d -> p (l d)", p=P)
        every = big[:].rearrange("p (b w) -> p b w", w=WG)
        ad_g = ad_at_start.rearrange("(p l) d -> p (l d)", p=P)

        weight_loads = [
            (w01[:], a["L0_gnn_W1"]), (w02[:], a["L0_gnn_W2"]),
            (c0[:, 0:1], a["L0_gnn_b1"].unsqueeze(1)), (c0[:, 1:2], a["L0_gnn_b2"].unsqueeze(1)),
            (c0[:, 2:3], a["L0_gnn_gamma"].unsqueeze(1)), (c0[:, 3:4], a["L0_gnn_beta"].unsqueeze(1)),
            (w11[:], a["L1_gnn_W1"]), (w12[:], a["L1_gnn_W2"].rearrange("(k p) n -> p k n", p=P)),
            (w13[:], a["L1_gnn_W3"].rearrange("(k p) n -> p k n", p=P)),
            (c1[:, 0:1], a["L1_gnn_b1"][0:P].unsqueeze(1)), (c1[:, 1:2], a["L1_gnn_b1"][P:HID].unsqueeze(1)),
            (c1[:, 2:3], a["L1_gnn_b2"][0:P].unsqueeze(1)), (c1[:, 3:4], a["L1_gnn_b2"][P:HID].unsqueeze(1)),
            (c13[:], a["L1_gnn_b3"].unsqueeze(1)),
            (enc_w[:], a["L2_gnn_enc_W"]), (enc_b[:], a["L2_gnn_enc_b"].unsqueeze(1)),
            (w_pq[:, :, 0:D], a["L2_gnn_msg_W1"][:, 0:D, :].rearrange("l k n -> k l n")),
            (w_pq[:, :, D:2 * D], a["L2_gnn_msg_W1"][:, D:2 * D, :].rearrange("l k n -> k l n")),
            (w_e[:], a["L2_gnn_msg_W1"][:, 2 * D:, :].rearrange("l k n -> k l n")),
            (w_m2[0:D], a["L2_gnn_msg_W2"].rearrange("l k n -> k l n")),
            (w_m2[D:W], a["L2_gnn_msg_b2"].unsqueeze(0)),
            (w_ih[:], a["L2_gnn_gru_Wih"].rearrange("l k n -> k l n")),
            (w_hh[:], a["L2_gnn_gru_Whh"].rearrange("l k n -> k l n")),
            (b_ih[:], a["L2_gnn_gru_bih"].rearrange("l (g d) -> d l g", g=3)),
            (b_hh[:], a["L2_gnn_gru_bhh"].rearrange("l (g d) -> d l g", g=3)),
            (ro1[:], a["L2_gnn_ro_W1"]), (ro2[:], a["L2_gnn_ro_W2"]),
            (c_ro[:, 0:1], a["L2_gnn_ro_b1"].unsqueeze(1)), (c_ro[:, 1:2], a["L2_gnn_ro_b2"].unsqueeze(1)),
            (b_pq[:, :, D:2 * D], a["L2_gnn_msg_b1"].partition_broadcast(P)),
        ]
        for l in range(2):
            weight_loads += [
                (gw[:, l, :], a[f"L3_gnn_W{l + 1}"]),
                (g_src[:, l, :], a[f"L3_gnn_a_src{l + 1}"].partition_broadcast(P)),
                (g_dst[:, l, :], a[f"L3_gnn_a_dst{l + 1}"].partition_broadcast(P)),
                (g_b[:, l, :], a[f"L3_gnn_b{l + 1}"].partition_broadcast(P))]

        block = ctx.enter_context(nc.Block())

        @block.sync
        def _(sp):
            sp.dma_start(src_i[:], src_d).then_inc(edges_in, 16)
            sp.dma_start(dst_i[:], dst_d).then_inc(edges_in, 16)
            flat = dst_d.rearrange("p l -> (p l)")
            sp.dma_start(beside_i[1:P, 0:1], dst_d[0:P - 1, L - 1:L]).then_inc(edges_in, 16)
            sp.dma_start(beside_i[0:P - 1, 1:2], dst_d[1:P, 0:1]).then_inc(edges_in, 16)
            sp.dma_start(beside_i[0:1, 0:1], a["none"]).then_inc(edges_in, 16)
            sp.dma_start(beside_i[P - 1:P, 1:2], a["none"]).then_inc(edges_in, 16)
            sp.dma_start(xN[:], x_d.rearrange("(t p) d -> p t d", p=P)).then_inc(x_in, 16)
            for dst, s in weight_loads:
                sp.dma_start(dst, s).then_inc(weights_in, 16)
            sp.wait_ge(zero_made, 1)
            width = NP
            for k in range(0, L * D, width):
                n = min(width, L * D - k)
                sp.dma_start(q_g[:, k:k + n], FM[0][:, 0:n]).then_inc(zeros_out, 16)
            sp.dma_start(ad_g, FM[0][:, 0:2 * L]).then_inc(zeros_out, 16)
            sp.wait_ge(first_ready, 1)
            sp.dma_start(first_d[0:NP].rearrange("(t p) o -> p (t o)", p=P), first[:]).then_inc(first_out, 16)
            sp.dma_start(first_d[NP:NP + 1], tail[P - 1:P, 1:2]).then_inc(first_out, 16)
            sp.wait_ge(first_out, 32)
            sp.dma_start(nxt[:], first_d[1:NP + 1].rearrange("(t p) o -> p (t o)", p=P)).then_inc(first_in, 16)
            row = first_d.rearrange("n o -> (n o)")
            sp.dma_start(FM[1], row[0:NP].partition_broadcast(P)).then_inc(first_in, 16)
            sp.dma_start(FM[2], row[1:NP + 1].partition_broadcast(P)).then_inc(first_in, 16)

            def store_sums(k):
                with sp.Fori(0, TRIPS) as i:
                    for s in range(SLOTS):
                        sp.wait_ge(summed, i * SLOTS + k * NG + s + 1)
                        sp.dma_start(sums_g[:, bass.ds((i * SLOTS + s) * COLS * D, COLS * D)],
                                     ringG[:, s, 0:COLS * D]).then_inc(slot_open[s], 16)

            store_sums(0)
            sp.wait_ge(table_ready, 1)
            sp.dma_start(table_x(1), xN[:]).then_inc(table_out, 16)
            store_sums(1)
            pq = FM[6].rearrange("p (t d) -> p t d", t=NT)
            for l in range(NLAYER):
                sp.wait_ge(table_ready, 2 + l)
                sp.dma_start(table_x(2 + l), pq[:, :, 0:D]).then_inc(table_out, 16)
                sp.dma_start(qtab[l].rearrange("(t p) d -> p t d", p=P), pq[:, :, D:2 * D]).then_inc(qtable_out, 16)
                sp.wait_ge(q_row_in, 16 * (l + 1))
                sp.wait_ge(q_scattered, 16 * NT * (l + 1))
                sp.dma_start(q_at_start.rearrange("(p l) d -> p l d", p=P)[:, 0, :], q_row[:, l, :]).then_inc(q_row_out, 16)
                store_sums(2 + l)
            for l in range(2):
                sp.wait_ge(table_ready, 5 + l)
                sp.dma_start(table_x(5 + l), gN[:]).then_inc(table_out, 16)
                sp.wait_ge(ad_ready, l + 1)
                sp.dma_start(adtab[l].rearrange("(t p) o -> p t o", p=P), adN[:]).then_inc(adtab_out, 16)
                sp.wait_ge(ad_scattered, 16 * NT * (l + 1))
                sp.dma_start(ad_e[:].rearrange("p l o -> p (l o)"), ad_g).then_inc(ad_in, 16)
                for q in range(PARTS):
                    sp.wait_ge(scanned, W * (l * PARTS + q + 1))
                    at = slice(q * LP * WG, (q + 1) * LP * WG)
                    sp.dma_start(sums_wg[:, at], big[:, at]).then_inc(weighted_out, 16)
            sp.wait_ge(out_ready, 1)
            full = N // P
            sp.dma_start(out[0:full * P].rearrange("(t p) d -> p t d", p=P), yN[:, 0:full, 0:D]).then_inc(out_done, 16)
            sp.dma_start(out[full * P:N], yN[0:N - full * P, full, 0:D]).then_inc(out_done, 16)
            sp.wait_ge(out_done, 32)

        @block.gpsimd
        def _(pool):
            def made(ins, n):
                ins.then_inc(consts_made, 1)
                pool.wait_ge(consts_made, n)

            pool.memset(FM[0], 0.0).then_inc(zero_made, 1)
            made(pool.memset(ident[:], 0.0), 1)
            made(pool.affine_select(out=ident[:], in_=ident[:], compare_op=ALU.not_equal, fill=1.0, base=0,
                                    pattern=[[-1, P]], channel_multiplier=1), 2)
            made(pool.memset(ones[:], 1.0), 3)
            made(pool.iota(node_i[:], pattern=[[P, NT]], base=0, channel_multiplier=1), 4)
            made(pool.iota(tail_i[:], pattern=[[1, 2]], base=L - 1, channel_multiplier=L), 5)
            made(pool.iota(FM[1].bitcast(I32), pattern=[[1, NP]], base=0, channel_multiplier=0), 6)

            def gather(out_ap, table, index):
                return pool.indirect_dma_start(out=out_ap, out_offset=None, in_=table,
                                               in_offset=bass.IndirectOffsetOnAxis(ap=index, axis=0))

            def scatter(table, index, in_ap):
                return pool.indirect_dma_start(out=table, out_offset=bass.IndirectOffsetOnAxis(ap=index, axis=0),
                                               in_=in_ap, in_offset=None, bounds_check=EP - 1, oob_is_err=False)

            edge_rows = big[:, 3 * NP:3 * NP + NT * L].bitcast(I32)
            pool.wait_ge(edge_rows_ready, 1)
            for t in range(NT):
                gather(edge_rows[:, t * L:(t + 1) * L], dst_d, edge_row_i[:, t:t + 1]).then_inc(edge_rows_in, 16)

            def gather_pass(k, width):
                table = x_d if k == 0 else tab[k][:, :]
                if k:
                    pool.wait_ge(table_out, 16 * k)
                with pool.Fori(0, TRIPS) as i:
                    for s in range(SLOTS):
                        pool.wait_ge(staged, i * SLOTS + k * NG + s + 1)
                        pool.sem_inc(turn, 1)
                        for u in range(COLS):
                            gather(ringG[:, s, u * width:(u + 1) * width], table,
                                   idx_s[:, s, u:u + 1]).then_inc(gathered[s], 16)

            def gather_sums(k):
                if k < 5:
                    for s in range(SLOTS):
                        pool.wait_ge(slot_open[s], 16 * ((k + 1) * TRIPS + 1))
                else:
                    pool.wait_ge(weighted_out, 16 * PARTS * (k - 4))
                source, width = (sums, D) if k < 5 else (sums_w, WG)
                if k == 0:
                    pool.wait_ge(prep_done, 1)
                for t in range(NT):
                    gather(gN[:, t, 0:width], source[:, :], end_i[:, t:t + 1]).then_inc(sums_in, 16)

            gather_pass(0, D)
            gather_sums(0)
            gather_pass(1, D)
            gather_sums(1)
            pool.wait_ge(zeros_out, 16 * ZERO_STORES)
            for l in range(NLAYER):
                pool.wait_ge(table_ready, 2 + l)
                for t in range(NT):
                    scatter(q_at_start[:, :], start_i[:, t:t + 1],
                            FM[6][:, t * 2 * D + D:(t + 1) * 2 * D]).then_inc(q_scattered, 16)
                pool.wait_ge(qtable_out, 16 * (l + 1))
                gather(q_row[:, l, :], qtab[l][:, :], dst_i[:, 0:1]).then_inc(q_row_in, 16)
                gather_pass(2 + l, D)
                gather_sums(2 + l)
            for l in range(2):
                pool.wait_ge(ad_ready, l + 1)
                if l:
                    pool.wait_ge(ad_in, 16 * l)
                for t in range(NT):
                    scatter(ad_at_start[:, :], start_i[:, t:t + 1], adN[:, t, :]).then_inc(ad_scattered, 16)
                pool.wait_ge(adtab_out, 16 * (l + 1))
                gather(ad_row[:, l, :], adtab[l][:, :], dst_i[:, 0:1]).then_inc(ad_row_in, 16)
                gather_pass(5 + l, WG)
                pool.wait_ge(weights_ready, l + 1)
                for q in range(1, PARTS):
                    part = every[:, q * LP:(q + 1) * LP, 1:WG]
                    nc.gpsimd.tensor_tensor(part, part, wgt[:, q * LP:(q + 1) * LP].unsqueeze(2).to_broadcast(
                        [P, LP, W]), ALU.mult).then_inc(multiplied, 1)
                gather_sums(5 + l)

        @block.scalar
        def _(act):
            def stage_indices(k, edges_too=None):
                with act.Fori(0, TRIPS) as i:
                    for s in range(SLOTS):
                        act.wait_ge(slot_open[s], (i + (k * TRIPS + 1)) * 16)
                        act.sem_inc(turn_a, 1)
                        nc.scalar.copy(idx_s[:, s, :], src_i[:, bass.ds((i * SLOTS + s) * COLS, COLS)]
                                       ).then_inc(staged, 1)
                        if edges_too is not None:
                            l = edges_too
                            act.wait_ge(edge_summed, i * SLOTS + l * NG + s + 1)
                            act.dma_start(ringQ[:, s, :], q_g[:, bass.ds((i * SLOTS + s) * COLS * D, COLS * D)]
                                          ).then_inc(q_in[s], 16)
                            act.dma_start(ringE[:, s, :], ef_d[:, bass.ds((i * SLOTS + s) * COLS * P, COLS * P)]
                                          ).then_inc(ef_in[s], 16)

            def drain(name, out_of, fn, bias=0.0, rows=D, after=None):
                for c in range(NC):
                    act.wait_ge(filled, fill_count(name, c))
                    if after is not None:
                        after(c)
                    n = cols(c)
                    nc.scalar.activation(out_of[0:rows, n], ps[0:rows, c, 0:n.stop - n.start], fn,
                                         bias=bias).then_inc(drained_a, 1)

            def root(m):
                act.wait_ge(var_ready, m)
                nc.scalar.activation(rstd[:], stat[:], ACT.Sqrt).then_inc(std_ready, 1)

            for s in range(SLOTS):
                act.sem_inc(slot_open[s], 16)
            for s in range(SLOTS):
                act.sem_inc(edge_summed, 1)
            act.wait_ge(edges_in, 6 * 16)
            stage_indices(0)
            act.wait_ge(weights_in, 16 * len(weight_loads))
            act.wait_ge(zeros_out, 16 * ZERO_STORES)
            drain("l0_T", FM[0], ACT.Copy)
            drain("l0_w1", FM[1], ACT.Relu, bias=c0[:, 0:1])
            drain("l0_w2", FM[2], ACT.Identity, bias=c0[:, 1:2])
            act.wait_ge(bn_scale_ready, 1)
            nc.scalar.activation(bn[:, 3:4], bn[:, 2:3], ACT.Sqrt).then_inc(bn_done, 1)
            act.wait_ge(bn_scale_ready, 2)
            nc.scalar.activation(FM[1][0:D, :], FM[2][0:D, :], ACT.Relu, bias=c0[:, 3:4],
                                 scale=bn[:, 5:6]).then_inc(bn_done, 1)
            root(1)
            stage_indices(1)
            drain("l1_T", FM[0], ACT.Copy)
            drain("l1_w1a", FM[1], ACT.Relu, bias=c1[:, 0:1], rows=P)
            drain("l1_w1b", FM[2], ACT.Relu, bias=c1[:, 1:2], rows=P)
            drain("l1_w2a", FM[3], ACT.Relu, bias=c1[:, 2:3], rows=P)
            drain("l1_w2b", FM[4], ACT.Relu, bias=c1[:, 3:4], rows=P)
            drain("l1_w3", FM[5], ACT.Identity, bias=c13[:])
            root(2)
            drain("l2_T", FM[0], ACT.Copy)
            drain("l2_enc", FM[1], ACT.Identity, bias=enc_b[:])
            for l in range(NLAYER):
                act.wait_ge(q_row_out, 16 * (l + 1))
                stage_indices(2 + l, edges_too=l)
                drain(f"T{l}", FM[0], ACT.Copy, rows=W)
                drain(f"agg{l}", FM[2], ACT.Copy)
                drain(f"r{l}", FM[3], ACT.Sigmoid, bias=b_rz[:, l, 0:1])
                drain(f"z{l}", FM[4], ACT.Sigmoid, bias=b_rz[:, l, 1:2])
                for c in range(NC):
                    act.wait_ge(cell_in, NC * l + c + 1)
                    nc.scalar.activation(FM[5][0:D, cols(c)], FM[5][0:D, cols(c)], ACT.Tanh,
                                         bias=b_ih[:, l, 2:3]).then_inc(gate_ready, 1)
            drain("ro1", FM[2], ACT.Relu, bias=c_ro[:, 0:1])
            drain("ro2", FM[3], ACT.Identity, bias=c_ro[:, 1:2])
            root(3)
            for l in range(2):
                drain(f"gT{l}", FM[0], ACT.Copy)
                stage_indices(5 + l)
                act.wait_ge(gap_ready, l + 1)
                nc.scalar.activation(wgt[:], wgt[:], ACT.Exp).then_inc(weights_ready, 1)
                act.wait_ge(self_ready, l + 1)
                nc.scalar.activation(self_w[:], self_w[:], ACT.Exp).then_inc(self_done, 1)
            root(4)

        @block.vector
        def _(v):
            chain = Chain(v, vchain)
            link = chain.link

            def drained_here(ins, name, c):
                s, n = drained(name, c)
                ins.then_inc(s, 1)
                v.wait_ge(s, n)

            v.wait_ge(edges_in, 6 * 16)
            link(v.memset(carry[:], 0.0))
            link(v.memset(carry_q[:], 0.0))
            link(v.memset(b_pq[:, :, 0:D], 0.0))
            link(v.tensor_copy(dst_f[:], dst_i[:]))
            link(v.tensor_copy(beside[:], beside_i[:]))
            link(v.memset(same[:, 0:1], 0.0))
            link(v.tensor_tensor(same[:, 1:L], dst_f[:, 1:L], dst_f[:, 0:L - 1], ALU.is_equal))
            v.wait_ge(consts_made, 6)
            link(v.tensor_copy(node_f[:], node_i[:]))
            link(v.tensor_copy(tail[:], tail_i[:]))
            link(v.tensor_copy(FM[2], FM[1].bitcast(I32)))
            v.tensor_scalar(spans[:], FM[2], dst_f[:, 0:1], None, ALU.is_gt).then_inc(rows_before, 1)

            def sum_columns(k, s, width, i, rows):
                for u in range(COLS):
                    now = rows[:, u * width:(u + 1) * width]
                    prev = carry[:, 0:width] if u == 0 else rows[:, (u - 1) * width:u * width]
                    link(v.scalar_tensor_tensor(now, prev, same[:, bass.ds((i * SLOTS + s) * COLS + u, 1)], now,
                                                ALU.mult, ALU.add))

            def sum_pass(k):
                with v.Fori(0, TRIPS) as i:
                    chain.loop(i, SLOTS * COLS)
                    for s in range(SLOTS):
                        v.wait_ge(gathered[s], (i + (k * TRIPS + 1)) * 16 * COLS)
                        rows = ringG[:, s, 0:COLS * D]
                        sum_columns(k, s, D, i, rows)
                        v.tensor_copy(carry[:, 0:D], rows[:, (COLS - 1) * D:]).then_inc(summed, 1)
                        v.wait_ge(summed, i * SLOTS + k * NG + s + 1)
                    chain.end(TRIPS)

            def message_pass(k, l):
                with v.Fori(0, TRIPS) as i:
                    chain.loop(i, SLOTS * (2 * COLS + 3))
                    for s in range(SLOTS):
                        v.wait_ge(q_in[s], (i + (l * TRIPS + 1)) * 16)
                        q, rows = ringQ[:, s, :], ringG[:, s, 0:COLS * D]
                        for u in range(COLS):
                            now = q[:, u * D:(u + 1) * D]
                            prev = carry_q[:] if u == 0 else q[:, (u - 1) * D:u * D]
                            link(v.scalar_tensor_tensor(now, prev, same[:, bass.ds((i * SLOTS + s) * COLS + u, 1)],
                                                        now, ALU.mult, ALU.add))
                        link(v.tensor_copy(carry_q[:], q[:, (COLS - 1) * D:]))
                        v.wait_ge(edge_product, i * SLOTS + l * NG + s + 1)
                        link(v.tensor_tensor(q, ps[:, 6 + s, :], q, ALU.add))
                        v.wait_ge(gathered[s], (i + (k * TRIPS + 1)) * 16 * COLS)
                        v.tensor_tensor(rows, rows, q, ALU.add).then_inc(edge_summed, 1)
                        v.wait_ge(edge_summed, i * SLOTS + l * NG + SLOTS + s + 1)
                        link(v.tensor_scalar(rows, rows, 0.0, None, ALU.max))
                        sum_columns(k, s, D, i, rows)
                        v.tensor_copy(carry[:, 0:D], rows[:, (COLS - 1) * D:]).then_inc(summed, 1)
                        v.wait_ge(summed, i * SLOTS + k * NG + s + 1)
                    chain.end(TRIPS)

            def node_sums(name, k, width):
                v.wait_ge(sums_in, 16 * NT * (k + 1))
                link(v.tensor_tensor(gN[:, :, 0:width], gN[:, :, 0:width],
                                     has[:].unsqueeze(2).to_broadcast([P, NT, width]), ALU.mult))
                for c in range(NC):
                    v.wait_ge(filled, fill_count(name, c))
                    t = tiles(c)
                    part = ps[:, c, :].rearrange("p (t d) -> p t d", d=P)[:, 0:len(t), 0:width]
                    drained_here(v.tensor_tensor(yN[:, t.start:t.stop, 0:width], gN[:, t.start:t.stop, 0:width], part,
                                                 ALU.add), name, c)

            def layer_norm(src, dst, m):
                y, sq = src[:, :, 0:D], FM[7][:, 0:NT * D].rearrange("p (t d) -> p t d", d=D)

                def wide(s):
                    return s[:].unsqueeze(2).to_broadcast([P, NT, D])

                link(v.tensor_reduce(stat[:], y, AX.X, ALU.add))
                link(v.tensor_scalar(stat[:], stat[:], 1.0 / D, None, ALU.mult))
                link(v.tensor_tensor(y, y, wide(stat), ALU.subtract))
                link(v.tensor_tensor(sq, y, y, ALU.mult))
                link(v.tensor_reduce(stat[:], sq, AX.X, ALU.add))
                v.tensor_scalar(stat[:], stat[:], 1.0 / D, LN_EPS, ALU.mult, ALU.add).then_inc(var_ready, 1)
                v.wait_ge(std_ready, m)
                link(v.reciprocal(rstd[:], rstd[:]))
                link(v.tensor_tensor(dst[:, :, 0:D], y, wide(rstd), ALU.mult))

            def residual(name):
                for c in range(NC):
                    v.wait_ge(filled, fill_count(name, c))
                    t = tiles(c)
                    part = ps[:, c, :].rearrange("p (t d) -> p t d", d=P)[:, 0:len(t), 0:D]
                    drained_here(v.tensor_tensor(yN[:, t.start:t.stop, 0:D], xN[:, t.start:t.stop, :], part,
                                                 ALU.add), name, c)

            v.wait_ge(counts_ready, 1)
            link(v.tensor_scalar(edge_row[:], ps[:, 7, 0:NT], -1.0, 0.0, ALU.add, ALU.max))
            v.tensor_copy(edge_row_i[:], edge_row[:]).then_inc(edge_rows_ready, 1)
            v.wait_ge(edge_rows_in, 16 * NT)
            edge_rows = big[:, 3 * NP:3 * NP + NT * L].bitcast(I32)
            for t in range(NT):
                link(v.tensor_copy(logit[:], edge_rows[:, t * L:(t + 1) * L]))
                link(v.tensor_scalar(wgt[:], logit[:], node_f[:, t:t + 1], 0.0, ALU.is_lt, ALU.add,
                                     accum_out=count[:, t:t + 1]))
            v.scalar_tensor_tensor(first[:], edge_row[:], float(L), count[:], ALU.mult, ALU.add).then_inc(first_ready, 1)
            v.wait_ge(first_in, 48)
            link(v.tensor_tensor(has[:], nxt[:], first[:], ALU.is_gt))
            link(v.tensor_tensor(deg[:], nxt[:], first[:], ALU.subtract))
            link(v.tensor_scalar(tmp[:], nxt[:], -1.0, 0.0, ALU.add, ALU.max))
            link(v.tensor_copy(end_i[:], tmp[:]))
            link(v.tensor_scalar(tmp[:], has[:], float(-SKIP), float(SKIP), ALU.mult, ALU.add))
            link(v.tensor_tensor(tmp[:], tmp[:], first[:], ALU.add))
            link(v.tensor_copy(start_i[:], tmp[:]))
            link(v.tensor_scalar(FM[1], FM[1], tail[:, 0:1], None, ALU.is_le))
            link(v.scalar_tensor_tensor(spans[:], FM[2], tail[:, 1:2], FM[1], ALU.is_gt, ALU.mult))
            link(v.tensor_scalar(pen_f[:, 1:L], same[:, 1:L], BIG, -BIG, ALU.mult, ALU.add))
            link(v.tensor_scalar(pen_b[:, 0:L - 1], same[:, 1:L], BIG, -BIG, ALU.mult, ALU.add))
            link(v.tensor_tensor(flag[:, 0:1], beside[:, 0:1], dst_f[:, 0:1], ALU.is_equal))
            link(v.tensor_tensor(flag[:, 1:2], beside[:, 1:2], dst_f[:, L - 1:L], ALU.is_equal))
            link(v.tensor_scalar(pen_f[:, 0:1], flag[:, 0:1], BIG, -BIG, ALU.mult, ALU.add))
            link(v.tensor_scalar(pen_b[:, L - 1:L], flag[:, 1:2], BIG, -BIG, ALU.mult, ALU.add))
            link(v.tensor_tensor(flag[:, 2:3], dst_f[:, 0:1], dst_f[:, L - 1:L], ALU.is_equal))
            link(v.tensor_scalar(flag[:, 0:2], flag[:, 0:2], flag[:, 2:3], None, ALU.mult))
            v.tensor_scalar(flag[:, 4:6], flag[:, 0:2], BIG, -BIG, ALU.mult, ALU.add).then_inc(pens_ready, 1)
            v.wait_ge(pens_turned, 1)
            link(v.tensor_copy(pen_row[:], ps[0:1, 7, 0:2 * P].rearrange("p (a b) -> p a b", a=2)))
            link(v.memset(car_row[:], -BIG))
            v.wait_ge(weights_in, 16 * len(weight_loads))
            link(v.tensor_tensor(b_rz[:], b_ih[:], b_hh[:], ALU.add))
            v.engine_nop().then_inc(prep_done, 1)

            sum_pass(0)
            node_sums("l0_carry", 0, D)
            v.wait_ge(x_in, 16)
            v.tensor_tensor(yN[:, :, 0:D], yN[:, :, 0:D], xN[:], ALU.add).then_inc(node_ready, 1)
            for c in range(NC):
                v.wait_ge(*drained("l0_w2", c))
            h = FM[2][0:D, 0:N]
            link(v.tensor_reduce(bn[:, 0:1], h, AX.X, ALU.add))
            link(v.tensor_scalar(bn[:, 0:1], bn[:, 0:1], 1.0 / N, None, ALU.mult))
            link(v.tensor_scalar(FM[2][0:D, :], FM[2][0:D, :], bn[:, 0:1], None, ALU.subtract))
            link(v.tensor_tensor(FM[3][0:D, 0:N], h, h, ALU.mult))
            link(v.tensor_reduce(bn[:, 1:2], FM[3][0:D, 0:N], AX.X, ALU.add))
            v.tensor_scalar(bn[:, 2:3], bn[:, 1:2], 1.0 / N, BN_EPS, ALU.mult, ALU.add).then_inc(bn_scale_ready, 1)
            v.wait_ge(bn_done, 1)
            link(v.reciprocal(bn[:, 4:5], bn[:, 3:4]))
            v.tensor_tensor(bn[:, 5:6], bn[:, 4:5], c0[:, 2:3], ALU.mult).then_inc(bn_scale_ready, 1)
            residual("l0_back")
            layer_norm(yN, xN, 1)
            v.engine_nop().then_inc(table_ready, 1)

            sum_pass(1)
            node_sums("l1_carry", 1, D)
            v.wait_ge(table_out, 16)
            v.tensor_tensor(yN[:, :, 0:D], yN[:, :, 0:D], xN[:], ALU.add).then_inc(node_ready, 1)
            residual("l1_back")
            layer_norm(yN, xN, 2)
            v.engine_nop().then_inc(node_ready, 1)

            for l in range(NLAYER):
                for c in range(NC):
                    v.wait_ge(filled, fill_count(f"pq{l}", c))
                    t = tiles(c)
                    pq = FM[6][:, t.start * P:t.stop * P].rearrange("p (t d) -> p t d", d=P)
                    part = ps[:, c, 0:len(t) * P].rearrange("p (t d) -> p t d", d=P)
                    drained_here(v.tensor_tensor(pq, part, b_pq[:, l, :].unsqueeze(1).to_broadcast([P, len(t), P]),
                                                 ALU.add), f"pq{l}", c)
                v.engine_nop().then_inc(table_ready, 1)
                message_pass(2 + l, l)
                node_sums(f"carry{l}", 2 + l, D)
                v.tensor_copy(yN[:, :, D], deg[:]).then_inc(node_ready, 1)
                for c in range(NC):
                    v.wait_ge(filled, fill_count(f"gh{l}", c))
                    v.wait_ge(*drained(f"z{l}", c))
                    n = cols(c)
                    drained_here(v.scalar_tensor_tensor(FM[5][0:D, n], ps[0:D, c, 0:n.stop - n.start], b_hh[:, l, 2:3],
                                                        FM[3][0:D, n], ALU.add, ALU.mult), f"gh{l}", c)
                for c in range(NC):
                    v.wait_ge(filled, fill_count(f"gi{l}", c))
                    n = cols(c)
                    drained_here(v.tensor_tensor(FM[5][0:D, n], FM[5][0:D, n], ps[0:D, c, 0:n.stop - n.start],
                                                 ALU.add), f"gi{l}", c)
                    v.engine_nop().then_inc(cell_in, 1)
                for c in range(NC):
                    v.wait_ge(gate_ready, NC * l + c + 1)
                    n = cols(c)
                    link(v.tensor_tensor(FM[1][0:D, n], FM[1][0:D, n], FM[5][0:D, n], ALU.subtract))
                    link(v.tensor_tensor(FM[1][0:D, n], FM[1][0:D, n], FM[4][0:D, n], ALU.mult))
                    link(v.tensor_tensor(FM[1][0:D, n], FM[1][0:D, n], FM[5][0:D, n], ALU.add))
                    v.engine_nop().then_inc(state_ready, 1)
            residual("l2_back")
            layer_norm(yN, xN, 3)
            v.engine_nop().then_inc(node_ready, 1)

            def wide(value, width=D):
                return value.unsqueeze(2).to_broadcast([P, NT, width])

            def leaky(out_ap, in_ap):
                return v.scalar_tensor_tensor(out_ap, in_ap, SLOPE, in_ap, ALU.mult, ALU.max)

            y = yN[:, :, 0:D]
            for l in range(2):
                for c in range(NC):
                    v.wait_ge(filled, fill_count(f"gh_w{l}", c))
                    t = tiles(c)
                    part = ps[:, c, :].rearrange("p (t d) -> p t d", d=P)[:, 0:len(t), 0:D]
                    drained_here(v.tensor_copy(yN[:, t.start:t.stop, 0:D], part), f"gh_w{l}", c)
                prod = FM[7][:, 0:NT * D].rearrange("p (t d) -> p t d", d=D)
                link(v.tensor_copy(gN[:, :, 1:W], y))
                link(v.memset(gN[:, :, W], 1.0))
                for o, vec in ((1, g_src), (0, g_dst)):
                    link(v.tensor_tensor(prod, y, vec[:, l, :].unsqueeze(1).to_broadcast([P, NT, D]), ALU.mult))
                    link(v.tensor_reduce(adN[:, :, o], prod, AX.X, ALU.add))
                v.engine_nop().then_inc(ad_ready, 1)
                v.tensor_copy(gN[:, :, 0], adN[:, :, 1]).then_inc(table_ready, 1)
                k = 5 + l
                with v.Fori(0, TRIPS) as i:
                    for s in range(SLOTS):
                        v.wait_ge(gathered[s], (i + (k * TRIPS + 1)) * 16 * COLS)
                        v.tensor_scalar(big[:, bass.ds((i * SLOTS + s) * COLS * WG, COLS * WG)], ringG[:, s, :], 1.0,
                                        None, ALU.mult).then_inc(slot_open[s], 16)
                for s in range(SLOTS):
                    v.wait_ge(slot_open[s], 16 * ((k + 1) * TRIPS + 1))
                link(v.tensor_copy(logit[:], every[:, :, 0]))
                v.wait_ge(ad_in, 16 * (l + 1))
                v.wait_ge(ad_row_in, 16 * (l + 1))
                link(v.tensor_copy(ad_e[:, 0, :], ad_row[:, l, :]))
                for o in range(2):
                    link(v.tensor_tensor_scan(ad_e[:, :, o], same[:], ad_e[:, :, o], 0.0, ALU.mult, ALU.add))
                link(v.tensor_tensor_scan(mx_f[:], pen_f[:], logit[:], -BIG, ALU.add, ALU.max))
                v.tensor_tensor_scan(mx_b[:, ::-1], pen_b[:, ::-1], logit[:, ::-1], -BIG, ALU.add,
                                     ALU.max).then_inc(maxima_ready, 1)
                v.wait_ge(maxima_turned, l + 1)
                link(v.tensor_copy(val_row[:], ps[0:1, 7, 0:2 * P].rearrange("p (a b) -> p a b", a=2)))
                link(v.tensor_tensor_scan(car_row[:, 0, 1:P + 1], pen_row[:, 0, :], val_row[:, 0, :], -BIG,
                                          ALU.add, ALU.max))
                v.tensor_tensor_scan(car_row[:, 1, 0:P][:, ::-1], pen_row[:, 1, ::-1], val_row[:, 1, ::-1], -BIG,
                                     ALU.add, ALU.max).then_inc(carries_ready, 1)
                v.wait_ge(carries_turned, l + 1)
                link(v.tensor_copy(edge_carry[:], ps[:, 7, 0:2]))
                link(v.tensor_tensor_scan(mx_f[:], pen_f[:], logit[:], edge_carry[:, 0:1], ALU.add, ALU.max))
                link(v.tensor_tensor_scan(mx_b[:, ::-1], pen_b[:, ::-1], logit[:, ::-1], edge_carry[:, 1:2],
                                          ALU.add, ALU.max))
                link(v.tensor_tensor(mx_f[:], mx_f[:], mx_b[:], ALU.max))
                link(v.tensor_tensor(mx_f[:], mx_f[:], ad_e[:, :, 1], ALU.max))
                link(v.tensor_tensor(mx_f[:], mx_f[:], ad_e[:, :, 0], ALU.add))
                link(leaky(mx_f[:], mx_f[:]))
                link(v.tensor_tensor(logit[:], logit[:], ad_e[:, :, 0], ALU.add))
                link(leaky(logit[:], logit[:]))
                v.tensor_tensor(wgt[:], logit[:], mx_f[:], ALU.subtract).then_inc(gap_ready, 1)
                link(v.tensor_copy(every[:, :, 0], mx_f[:]))
                v.wait_ge(weights_ready, l + 1)
                part = every[:, 0:LP, 1:WG]
                link(v.tensor_tensor(part, part, wgt[:, 0:LP].unsqueeze(2).to_broadcast([P, LP, W]), ALU.mult))
                for q in range(PARTS):
                    if q:
                        v.wait_ge(multiplied, l * (PARTS - 1) + q)
                    b = slice(q * LP, (q + 1) * LP)
                    with v.Fori(0, W // UNROLL) as i:
                        for u in range(UNROLL):
                            f = i * UNROLL + u + 1
                            one = big[:, bass.ds(f + q * LP * WG, LP, WG)]
                            start = big[:, bass.ds(f + (q * LP - 1) * WG, 1)] if q else 0.0
                            v.tensor_tensor_scan(one, same[:, b], one, start, ALU.mult, ALU.add).then_inc(scanned, 1)
                    v.wait_ge(scanned, W * (l * PARTS + q + 1))
                link(v.tensor_tensor(self_s[:], adN[:, :, 0], adN[:, :, 1], ALU.add))
                link(leaky(self_s[:], self_s[:]))
                v.wait_ge(sums_in, 16 * NT * (k + 1))
                link(v.tensor_tensor(gN[:], gN[:], wide(has[:], WG), ALU.mult))
                link(v.tensor_scalar(tmp[:], has[:], BIG, -BIG, ALU.mult, ALU.add))
                link(v.tensor_tensor(tmp[:], tmp[:], gN[:, :, 0], ALU.add))
                link(v.tensor_tensor(tmp[:], tmp[:], self_s[:], ALU.max))
                v.tensor_tensor(self_w[:], self_s[:], tmp[:], ALU.subtract).then_inc(self_ready, 1)
                for c in range(NC):
                    v.wait_ge(filled, fill_count(f"gcarry{l}", c))
                    t = tiles(c)
                    part = ps[:, c, :].rearrange("p (t d) -> p t d", d=P)[:, 0:len(t), 0:W]
                    rows = gN[:, t.start:t.stop, 1:WG]
                    drained_here(v.tensor_tensor(rows, rows, part, ALU.add), f"gcarry{l}", c)
                v.wait_ge(self_done, l + 1)
                link(v.tensor_tensor(y, y, wide(self_w[:]), ALU.mult))
                link(v.tensor_tensor(y, y, gN[:, :, 1:W], ALU.add))
                link(v.tensor_tensor(tmp[:], gN[:, :, W], self_w[:], ALU.add))
                link(v.tensor_scalar(tmp[:], tmp[:], 1e-16, None, ALU.add))
                link(v.reciprocal(tmp[:], tmp[:]))
                link(v.tensor_tensor(y, y, wide(tmp[:]), ALU.mult))
                link(v.tensor_tensor(y, y, g_b[:, l, :].unsqueeze(1).to_broadcast([P, NT, D]), ALU.add))
                if l == 0:
                    v.tensor_scalar(y, y, 0.0, None, ALU.max).then_inc(node_ready, 1)
            link(v.tensor_tensor(y, y, xN[:], ALU.add))
            layer_norm(yN, yN, 4)
            v.engine_nop().then_inc(out_ready, 1)

        @block.tensor
        def _(pe):
            pe.wait_ge(consts_made, 6)
            pe.wait_ge(rows_before, 1)
            for t in range(NT):
                mm = pe.matmul(ps[:, 7, t:t + 1], spans[:, t * P:(t + 1) * P], ones[:], start=True, stop=True)
            mm.then_inc(counts_ready, 1)
            pe.wait_ge(pens_ready, 1)
            pe.transpose(ps[0:1, 7, 0:P], flag[:, 4:5], ident[:])
            pe.transpose(ps[0:1, 7, P:2 * P], flag[:, 5:6], ident[:]).then_inc(pens_turned, 1)
            pe.wait_ge(weights_in, 16 * len(weight_loads))

            def fill(name, body, ready=None, first=None):
                k = INDEX[name]
                if first is not None:
                    pe.wait_ge(*first)
                for c in range(NC):
                    if k:
                        pe.wait_ge(*drained(STAGES[k - 1][0], c))
                    if ready is not None:
                        ready(c)
                    body(c).then_inc(filled, 1)

            def carries(name, width, k, last, tails=carry[:]):
                def body(c):
                    for j, t in enumerate(tiles(c)):
                        mm = pe.matmul(ps[:, c, j * P:j * P + width], spans[:, t * P:(t + 1) * P], tails,
                                       start=True, stop=True)
                    return mm
                fill(name, body, first=(last, k))

            def turn_nodes(name, source, width, count):
                def body(c):
                    for j, t in enumerate(tiles(c)):
                        mm = pe.transpose(ps[0:width, c, j * P:(j + 1) * P], source[:, t, 0:width], ident[:])
                    return mm
                fill(name, body, first=(node_ready, count))

            def turn_back(name, source, first=None):
                def body(c):
                    for j, t in enumerate(tiles(c)):
                        mm = pe.transpose(ps[:, c, j * P:j * P + D], source[0:D, t * P:(t + 1) * P], ident[0:D, 0:D])
                    return mm
                fill(name, body, first=first)

            def product(name, pairs, rows=D, ready=None, first=None):
                def body(c):
                    n = cols(c)
                    for q, (wt, x) in enumerate(pairs):
                        mm = pe.matmul(ps[0:rows, c, 0:n.stop - n.start], wt, x[:, n], start=(q == 0),
                                       stop=(q == len(pairs) - 1))
                    return mm
                fill(name, body, ready, first)

            def node_product(name, x, wt, width, ready=None):
                def body(c):
                    for j, t in enumerate(tiles(c)):
                        mm = pe.matmul(ps[:, c, j * P:j * P + width], x[0:D, t * P:(t + 1) * P], wt, start=True,
                                       stop=True)
                    return mm
                fill(name, body, ready)

            def also(*names):
                def ready(c):
                    for name in names:
                        pe.wait_ge(*drained(name, c))
                return ready

            carries("l0_carry", D, NG, summed)
            turn_nodes("l0_T", yN, D, 1)
            product("l0_w1", [(w01[:], FM[0][0:D])])
            product("l0_w2", [(w02[:], FM[1][0:D])])
            turn_back("l0_back", FM[1], first=(bn_done, 2))

            carries("l1_carry", D, 2 * NG, summed)
            turn_nodes("l1_T", yN, D, 2)
            product("l1_w1a", [(w11[:, 0:P], FM[0][0:D])], rows=P)
            product("l1_w1b", [(w11[:, P:HID], FM[0][0:D])], rows=P)
            product("l1_w2a", [(w12[:, 0, 0:P], FM[1]), (w12[:, 1, 0:P], FM[2])], rows=P)
            product("l1_w2b", [(w12[:, 0, P:HID], FM[1]), (w12[:, 1, P:HID], FM[2])], rows=P)
            product("l1_w3", [(w13[:, 0, :], FM[3]), (w13[:, 1, :], FM[4])])
            turn_back("l1_back", FM[5])

            turn_nodes("l2_T", xN, D, 3)
            product("l2_enc", [(enc_w[:], FM[0][0:D])])
            for l in range(NLAYER):
                def state(c, l=l):
                    if l:
                        pe.wait_ge(state_ready, NC * (l - 1) + c + 1)
                node_product(f"pq{l}", FM[1], w_pq[:, l, :], 2 * D, ready=state)
                for s in range(SLOTS):
                    pe.wait_ge(*drained(f"pq{l}", NC - 1))
                with pe.Fori(0, TRIPS) as i:
                    for s in range(SLOTS):
                        pe.wait_ge(ef_in[s], (i + (l * TRIPS + 1)) * 16)
                        for u in range(COLS):
                            mm = pe.matmul(ps[:, 6 + s, u * D:(u + 1) * D], ringE[:, s, u * P:(u + 1) * P],
                                           w_e[:, l, :], start=True, stop=True)
                        mm.then_inc(edge_product, 1)
                carries(f"carry{l}", D, (3 + l) * NG, summed)
                turn_nodes(f"T{l}", yN, W, 4 + l)
                product(f"agg{l}", [(w_m2[:, l, :], FM[0][0:W])])
                product(f"r{l}", [(w_ih[:, l, 0:D], FM[2][0:D]), (w_hh[:, l, 0:D], FM[1][0:D])])
                product(f"z{l}", [(w_ih[:, l, D:2 * D], FM[2][0:D]), (w_hh[:, l, D:2 * D], FM[1][0:D])])
                product(f"gh{l}", [(w_hh[:, l, 2 * D:3 * D], FM[1][0:D])])
                product(f"gi{l}", [(w_ih[:, l, 2 * D:3 * D], FM[2][0:D])])

            def last_state(c):
                pe.wait_ge(state_ready, NC * (NLAYER - 1) + c + 1)
            product("ro1", [(ro1[:], FM[1][0:D])], ready=last_state)
            product("ro2", [(ro2[:], FM[2][0:D])])
            turn_back("l2_back", FM[3])

            for l in range(2):
                turn_nodes(f"gT{l}", yN if l else xN, D, 4 + NLAYER + l)
                node_product(f"gh_w{l}", FM[0], gw[:, l, :], D)
                pe.wait_ge(maxima_ready, l + 1)
                pe.transpose(ps[0:1, 7, 0:P], mx_f[:, L - 1:L], ident[:])
                pe.transpose(ps[0:1, 7, P:2 * P], mx_b[:, 0:1], ident[:]).then_inc(maxima_turned, 1)
                pe.wait_ge(carries_ready, l + 1)
                pe.transpose(ps[:, 7, 0:1], car_row[:, 0, 0:P], ones[0:1, :])
                pe.transpose(ps[:, 7, 1:2], car_row[:, 1, 1:P + 1], ones[0:1, :]).then_inc(carries_turned, 1)
                carries(f"gcarry{l}", W, (l + 1) * PARTS * W, scanned, every[:, L - 1, 1:WG])


_LAID_OUT = ("x", "src", "dst", "edge_attr_16")


def kernel(**inputs):
    import numpy as np
    import concourse.bacc as bacc
    from concourse.bass_utils import run_bass_kernel_spmd as run

    nc = bacc.Bacc("TRN2", target_bir_lowering=False, num_devices=1)
    arrays = {k: np.ascontiguousarray(v) for k, v in inputs.items() if k not in _LAID_OUT}
    x, src, dst, ef = (np.asarray(inputs[k]) for k in _LAID_OUT)
    arrays["x"] = np.concatenate([x, np.zeros((NP - N, D), x.dtype)])
    arrays["src"] = np.concatenate([src, np.zeros(EP - E, src.dtype)]).reshape(P, L)
    arrays["dst"] = np.concatenate([dst, np.full(EP - E, N, dst.dtype)]).reshape(P, L)
    arrays["none"] = np.full((1, 1), -1, dst.dtype)
    padded = np.concatenate([ef, np.zeros((EP - E, EF), ef.dtype)]).reshape(P, L, EF)
    arrays["edge_attr_16"] = np.ascontiguousarray(padded.transpose(2, 1, 0)).reshape(EF, L * P)
    aps = {k: nc.dram_tensor(f"in_{k}", v.shape, mybir.dt.from_np(v.dtype), kind="ExternalInput").ap()
           for k, v in arrays.items()}
    out = nc.dram_tensor("out_nodes", (N, D), F32, kind="ExternalOutput").ap()
    build(nc, aps, out)
    r = run(nc, [{f"in_{k}": v for k, v in arrays.items()}], core_ids=[0])
    return r.results[0]["out_nodes"]
```

```python
from contextlib import ExitStack

import concourse.bass as bass
from concourse import mybir

F32 = mybir.dt.float32
I32 = mybir.dt.int32
ALU = mybir.AluOpType
ACT = mybir.ActivationFunctionType
AX = mybir.AxisListType

P = 128
N, E, D = 3125, 53125, 64
NT = -(-N // P)
NP = NT * P
L = -(-E // P)
COLS, SLOTS = 8, 2
L = -(-L // (COLS * SLOTS)) * COLS * SLOTS
EP = P * L
NG = L // COLS
TRIPS = NG // SLOTS
COUNT_FROM = 6
COUNT_TO = COUNT_FROM + -(-NT // 2)
NTP = -(-NT // 2) * 2
W = D + 1
WG = D + 2
HID = 256
EF = 16
CH = 512
NC = -(-NP // CH)
BN_EPS = LN_EPS = 1e-5
SLOPE = 0.2
BIG = 1e30
NLAYER = 3
ZERO_W = L * D // TRIPS
ZERO_STORES = TRIPS + 3
PARTS = 4
LP = L // PARTS
UNROLL = 5
SKIP = 1 << 20

NORM = [("std", "A"), ("norm", "V")]
PHASES = {
    "gin0": [("l0_carry", "V"), ("l0_T", "A"), ("l0_w1", "A"), ("l0_w2", "A")],
    "gin0_end": [("l0_back", "V")] + [("l0_" + n, w) for n, w in NORM],
    "gin1": [("l1_carry", "V"), ("l1_T", "A"), ("l1_w1a", "A"), ("l1_w1b", "A"), ("l1_w2a", "A"), ("l1_w2b", "A"),
             ("l1_w3", "A"), ("l1_back", "V")] + [("l1_" + n, w) for n, w in NORM]
            + [("l2_T", "A"), ("enc", "A"), ("pq0", "V")],
}
for _l in range(NLAYER):
    PHASES[f"gru{_l}"] = [(f"carry{_l}", "V"), (f"T{_l}", "A"), (f"agg{_l}", "A"), (f"rz{_l}", "A"),
                          (f"cell{_l}", "V"), (f"tanh{_l}", "A"), (f"state{_l}", "V")]
    PHASES[f"gru{_l}"] += ([(f"pq{_l + 1}", "V")] if _l < NLAYER - 1 else
                           [("ro1", "A"), ("ro2", "A"), ("l2_back", "V")] + [("l2_" + n, w) for n, w in NORM]
                           + [("gT0", "A"), ("gh0", "V")])
PHASES["gat0"] = [("gself0", "V"), ("gexp0", "A"), ("gcarry0", "V"), ("gT1", "A"), ("gh1", "V")]
PHASES["gat1"] = [("gself1", "V"), ("gexp1", "A"), ("gcarry1", "V")] + [("l3_" + n, w) for n, w in NORM]
UNFILLED = ("std", "norm", "tanh", "state", "gself", "gexp")


def is_filled(name):
    return not any(u in name for u in UNFILLED)


def wave(phase):
    names = [name for name, _ in PHASES[phase]]
    return [(names[k], step - k) for step in range(NC + len(names) - 1) for k in reversed(range(len(names)))
            if 0 <= step - k < NC]


ORDER = [item for phase in PHASES for item in wave(phase)]
WHO = {name: who for stages in PHASES.values() for name, who in stages}
FILLED_AT, DONE_AT, _count = {}, {}, {"A": 0, "V": 0, "P": 0}
for _name, _c in ORDER:
    if is_filled(_name):
        _count["P"] += 1
        FILLED_AT[_name, _c] = _count["P"]
    _count[WHO[_name]] += 1
    DONE_AT[_name, _c] = _count[WHO[_name]]


def tiles(c):
    return range(c * CH // P, min(NT, (c + 1) * CH // P))


def cols(c):
    return slice(c * CH, min(NP, (c + 1) * CH))


class Chain:

    def __init__(self, eng, sem):
        self.eng, self.sem, self.n, self.base = eng, sem, 0, None

    def value(self):
        return self.n if self.base is None else self.base + self.n

    def link(self, ins):
        ins.then_inc(self.sem, 1)
        self.n += 1
        self.eng.wait_ge(self.sem, self.value())

    def loop(self, i, per_trip):
        self.start, self.per_trip = self.n, per_trip
        self.base, self.n = i * per_trip, self.start

    def end(self, trips):
        assert self.n == self.start + self.per_trip, self.n - self.start
        self.base, self.n = None, self.start + trips * self.per_trip


def build(nc, a, out):
    with ExitStack() as ctx:
        ctx.enter_context(nc.allow_non_contiguous_dma(reason="a few columns of one value per partition"))

        def sb(name, shape, dt=F32):
            return ctx.enter_context(nc.sbuf_tensor(name, shape, dt))

        def sem(name):
            return ctx.enter_context(nc.semaphore(name))

        def dram(name, shape, dt=F32):
            return nc.dram_tensor(name, shape, dt, kind="Internal").ap()

        tab = [dram(f"tab{k}", (NP, WG if k >= 5 else D)) for k in range(7)]
        qtab = [dram(f"qtab{l}", (NP, D)) for l in range(NLAYER)]
        adtab = [dram(f"adtab{l}", (NP, 2)) for l in range(2)]
        q_at_start = dram("q_at_start", (EP, D))
        ad_at_start = dram("ad_at_start", (EP, 2))
        sums = dram("sums", (EP + 1, D))
        sums_w = dram("sums_w", (EP + 1, WG))
        first_d = dram("first_d", (NP + 1, 1))

        big = sb("big", [P, L * WG])
        FM = [big[:, k * NP:(k + 1) * NP] for k in range(8)]
        spans = sb("spans", [P, NP])
        src_i = sb("src_i", [P, L], I32)
        dst_i = sb("dst_i", [P, L], I32)
        dst_f = sb("dst_f", [P, L])
        same = sb("same", [P, L])
        pen_f = sb("pen_f", [P, L])
        pen_b = sb("pen_b", [P, L])
        logit = sb("logit", [P, L])
        ad_e = sb("ad_e", [P, L, 2])
        mx_f = sb("mx_f", [P, L])
        mx_b = sb("mx_b", [P, L])
        wgt = sb("wgt", [P, L])
        xN = sb("xN", [P, NT, D])
        yN = sb("yN", [P, NT, W])
        gN = sb("gN", [P, NT, WG])
        ringG = sb("ringG", [P, SLOTS, COLS * WG])
        ringQ = sb("ringQ", [P, SLOTS, COLS * D])
        ringE = sb("ringE", [EF, SLOTS, COLS * P])
        idx_s = sb("idx_s", [P, SLOTS, COLS], I32)
        carry = sb("carry", [P, D])
        carry_q = sb("carry_q", [P, D])
        q_row = sb("q_row", [P, NLAYER, D])
        ad_row = sb("ad_row", [P, 2, 2])
        ident = sb("ident", [P, P])
        ones = sb("ones", [P, 1])
        node_i = sb("node_i", [P, NTP], I32)
        node_f = sb("node_f", [P, NTP])
        edge_row_i = sb("edge_row_i", [P, NTP], I32)
        edge_row = sb("edge_row", [P, NTP])
        count = sb("count", [P, NTP])
        first = sb("first", [P, NT])
        nxt = sb("nxt", [P, NT])
        has = sb("has", [P, NT])
        deg = sb("deg", [P, NT])
        tmp = sb("tmp", [P, NT])
        start_i = sb("start_i", [P, NT], I32)
        end_i = sb("end_i", [P, NT], I32)
        tail = sb("tail", [P, 2])
        tail_i = sb("tail_i", [P, 2], I32)
        beside_i = sb("beside_i", [P, 2], I32)
        beside = sb("beside", [P, 2])
        flag = sb("flag", [P, 6])
        stat = sb("stat", [P, NT])
        rstd = sb("rstd", [P, NT])
        adN = sb("adN", [P, NT, 2])
        self_w = sb("self_w", [P, NT])
        self_s = sb("self_s", [P, NT])
        edge_carry = sb("edge_carry", [P, 2])
        pen_row = sb("pen_row", [1, 2, P])
        val_row = sb("val_row", [1, 2, P])
        car_row = sb("car_row", [1, 2, P + 1])
        edge_end = sb("edge_end", [1, 1])
        bn = sb("bn", [D, 6])
        w01, w02 = sb("w01", [D, D]), sb("w02", [D, D])
        c0 = sb("c0", [D, 4])
        w11 = sb("w11", [D, HID])
        w12 = sb("w12", [P, 2, HID])
        w13 = sb("w13", [P, 2, D])
        c1 = sb("c1", [P, 4])
        c13 = sb("c13", [D, 1])
        enc_w, enc_b = sb("enc_w", [D, P]), sb("enc_b", [P, 1])
        w_pq = sb("w_pq", [P, NLAYER, 2 * D])
        w_e = sb("w_e", [EF, NLAYER, D])
        b_pq = sb("b_pq", [P, NLAYER, 2 * D])
        w_m2 = sb("w_m2", [W, NLAYER, D])
        w_rz = sb("w_rz", [P, NLAYER, P])
        w_n = sb("w_n", [P, NLAYER, P])
        b_z, b_r = sb("b_z", [P, NLAYER, 2]), sb("b_r", [P, NLAYER, 2])
        b_n = sb("b_n", [P, NLAYER, 2])
        ro1, ro2, c_ro = sb("ro1", [P, D]), sb("ro2", [D, D]), sb("c_ro", [D, 2])
        gw = sb("gw", [D, 2, D])
        g_src, g_dst, g_b = sb("g_src", [P, 2, D]), sb("g_dst", [P, 2, D]), sb("g_b", [P, 2, D])

        ps = ctx.enter_context(nc.psum_tensor("ps", [P, 8, 512], F32))

        src_in, edges_in, x_in, weights_in = sem("src_in"), sem("edges_in"), sem("x_in"), sem("weights_in")
        consts_made = sem("consts_made")
        zero_made, zeros_out = sem("zero_made"), sem("zeros_out")
        act_slots_open = sem("act_slots_open")
        rows_before = sem("rows_before")
        counts_ready = sem("counts_ready")
        edge_rows_ready, edge_rows_in = sem("edge_rows_ready"), sem("edge_rows_in")
        first_ready, first_out, first_in = sem("first_ready"), sem("first_out"), sem("first_in")
        prep_done = sem("prep_done")
        pens_ready, pens_turned = sem("pens_ready"), sem("pens_turned")
        filled, done_a, done_v = sem("filled"), sem("done_a"), sem("done_v")
        vchain = sem("vchain")
        staged = sem("staged")
        turn, turn_a = sem("turn"), sem("turn_a")
        gathered = [sem(f"gathered{s}") for s in range(SLOTS)]
        slot_open = [sem(f"slot_open{s}") for s in range(SLOTS)]
        q_in = [sem(f"q_in{s}") for s in range(SLOTS)]
        ef_in = [sem(f"ef_in{s}") for s in range(SLOTS)]
        edge_product = sem("edge_product")
        edge_summed = sem("edge_summed")
        summed = sem("summed")
        weighted_out = sem("weighted_out")
        multiplied, scanned = sem("multiplied"), sem("scanned")
        sums_in = [sem(f"sums_in{c}") for c in range(NC)]
        table_out, qtable_out = sem("table_out"), sem("qtable_out")
        q_scattered, q_row_in, q_row_out = sem("q_scattered"), sem("q_row_in"), sem("q_row_out")
        adtab_out, ad_scattered = sem("adtab_out"), sem("ad_scattered")
        ad_row_in, ad_in = sem("ad_row_in"), sem("ad_in")
        maxima_ready, maxima_turned = sem("maxima_ready"), sem("maxima_turned")
        carries_ready, carries_turned = sem("carries_ready"), sem("carries_turned")
        gap_ready, weights_ready = sem("gap_ready"), sem("weights_ready")
        bn_scale_ready, bn_done = sem("bn_scale_ready"), sem("bn_done")
        out_done = sem("out_done")

        def done(name, c):
            return (done_a if WHO[name] == "A" else done_v), DONE_AT[name, c]

        src_d, dst_d, x_d, ef_d = a["src"], a["dst"], a["x"], a["edge_attr_16"]

        FILL = lambda name, c: (filled, FILLED_AT[name, c])
        STATE = FM[1][D:P]
        pq = FM[6].rearrange("p (t d) -> p t d", t=NT)
        edge_rows = big[:, 3 * NP:3 * NP + NTP * L].bitcast(I32)

        def chunk_of(table, c):
            return table.rearrange("(t p) d -> p t d", p=P)[:, tiles(c).start:tiles(c).stop]

        def chunk(x, c, width=D):
            return x[:, tiles(c).start:tiles(c).stop, 0:width]

        sums_g = sums[0:EP].rearrange("(p l) d -> p (l d)", p=P)
        sums_wg = sums_w[0:EP].rearrange("(p l) d -> p (l d)", p=P)
        q_g = q_at_start.rearrange("(p l) d -> p (l d)", p=P)
        every = big[:].rearrange("p (b w) -> p b w", w=WG)
        ad_g = ad_at_start.rearrange("(p l) d -> p (l d)", p=P)

        wih, whh = (a[f"L2_gnn_gru_W{n}"].rearrange("l k n -> k l n") for n in ("ih", "hh"))
        bih, bhh = (a[f"L2_gnn_gru_b{n}"].rearrange("l (g d) -> d l g", g=3) for n in ("ih", "hh"))
        weight_loads = [
            (w01[:], a["L0_gnn_W1"]), (w02[:], a["L0_gnn_W2"]),
            (c0[:, 0:1], a["L0_gnn_b1"].unsqueeze(1)), (c0[:, 1:2], a["L0_gnn_b2"].unsqueeze(1)),
            (c0[:, 2:3], a["L0_gnn_gamma"].unsqueeze(1)), (c0[:, 3:4], a["L0_gnn_beta"].unsqueeze(1)),
            (w11[:], a["L1_gnn_W1"]), (w12[:], a["L1_gnn_W2"].rearrange("(k p) n -> p k n", p=P)),
            (w13[:], a["L1_gnn_W3"].rearrange("(k p) n -> p k n", p=P)),
            (c1[:, 0:1], a["L1_gnn_b1"][0:P].unsqueeze(1)), (c1[:, 1:2], a["L1_gnn_b1"][P:HID].unsqueeze(1)),
            (c1[:, 2:3], a["L1_gnn_b2"][0:P].unsqueeze(1)), (c1[:, 3:4], a["L1_gnn_b2"][P:HID].unsqueeze(1)),
            (c13[:], a["L1_gnn_b3"].unsqueeze(1)),
            (enc_w[:, D:P], a["L2_gnn_enc_W"]), (enc_b[D:P], a["L2_gnn_enc_b"].unsqueeze(1)),
            (w_pq[D:P, :, 0:D], a["L2_gnn_msg_W1"][:, 0:D, :].rearrange("l k n -> k l n")),
            (w_pq[D:P, :, D:2 * D], a["L2_gnn_msg_W1"][:, D:2 * D, :].rearrange("l k n -> k l n")),
            (w_e[:], a["L2_gnn_msg_W1"][:, 2 * D:, :].rearrange("l k n -> k l n")),
            (w_m2[0:D], a["L2_gnn_msg_W2"].rearrange("l k n -> k l n")),
            (w_m2[D:W], a["L2_gnn_msg_b2"].unsqueeze(0)),
            (w_rz[0:D, :, 0:D], wih[:, :, D:2 * D]), (w_rz[0:D, :, D:P], wih[:, :, 0:D]),
            (w_rz[D:P, :, 0:D], whh[:, :, D:2 * D]), (w_rz[D:P, :, D:P], whh[:, :, 0:D]),
            (w_n[0:D, :, 0:D], wih[:, :, 2 * D:]), (w_n[D:P, :, D:P], whh[:, :, 2 * D:]),
            (b_r[D:P, :, 0], bih[:, :, 0]), (b_r[D:P, :, 1], bhh[:, :, 0]),
            (b_z[0:D, :, 0], bih[:, :, 1]), (b_z[0:D, :, 1], bhh[:, :, 1]),
            (b_n[D:P, :, 0], bih[:, :, 2]), (b_n[D:P, :, 1], bhh[:, :, 2]),
            (ro1[D:P], a["L2_gnn_ro_W1"]), (ro2[:], a["L2_gnn_ro_W2"]),
            (c_ro[:, 0:1], a["L2_gnn_ro_b1"].unsqueeze(1)), (c_ro[:, 1:2], a["L2_gnn_ro_b2"].unsqueeze(1)),
            (b_pq[:, :, D:2 * D], a["L2_gnn_msg_b1"].partition_broadcast(P)),
        ]
        for l in range(2):
            weight_loads += [
                (gw[:, l, :], a[f"L3_gnn_W{l + 1}"]),
                (g_src[:, l, :], a[f"L3_gnn_a_src{l + 1}"].partition_broadcast(P)),
                (g_dst[:, l, :], a[f"L3_gnn_a_dst{l + 1}"].partition_broadcast(P)),
                (g_b[:, l, :], a[f"L3_gnn_b{l + 1}"].partition_broadcast(P))]

        block = ctx.enter_context(nc.Block())

        @block.sync
        def _(sp):
            sp.dma_start(src_i[:], src_d).then_inc(src_in, 16)
            sp.dma_start(dst_i[:], dst_d).then_inc(edges_in, 16)
            sp.dma_start(beside_i[1:P, 0:1], dst_d[0:P - 1, L - 1:L]).then_inc(edges_in, 16)
            sp.dma_start(beside_i[0:P - 1, 1:2], dst_d[1:P, 0:1]).then_inc(edges_in, 16)
            sp.dma_start(beside_i[0:1, 0:1], a["none"]).then_inc(edges_in, 16)
            sp.dma_start(beside_i[P - 1:P, 1:2], a["none"]).then_inc(edges_in, 16)
            sp.dma_start(xN[:], x_d.rearrange("(t p) d -> p t d", p=P)).then_inc(x_in, 16)
            for dst, s in weight_loads:
                sp.dma_start(dst, s).then_inc(weights_in, 16)

            def store_sums(k, start, end):
                with sp.Fori(start, end) as i:
                    for s in range(SLOTS):
                        sp.wait_ge(summed, i * SLOTS + k * NG + s + 1)
                        sp.dma_start(sums_g[:, bass.ds((i * SLOTS + s) * COLS * D, COLS * D)],
                                     ringG[:, s, 0:COLS * D]).then_inc(slot_open[s], 16)

            store_sums(0, 0, COUNT_TO)
            sp.wait_ge(first_ready, 1)
            sp.dma_start(first_d[0:NP].rearrange("(t p) o -> p (t o)", p=P), first[:]).then_inc(first_out, 16)
            sp.dma_start(first_d[NP:NP + 1], tail[P - 1:P, 1:2]).then_inc(first_out, 16)
            sp.wait_ge(first_out, 32)
            sp.dma_start(nxt[:], first_d[1:NP + 1].rearrange("(t p) o -> p (t o)", p=P)).then_inc(first_in, 16)
            row = first_d.rearrange("n o -> (n o)")
            sp.dma_start(FM[1], row[0:NP].partition_broadcast(P)).then_inc(first_in, 16)
            sp.dma_start(FM[2], row[1:NP + 1].partition_broadcast(P)).then_inc(first_in, 16)
            store_sums(0, COUNT_TO, TRIPS)

            for c in range(NC):
                sp.wait_ge(*done("l0_norm", c))
                sp.dma_start(chunk_of(tab[1], c), chunk(xN, c)).then_inc(table_out, 16)
            store_sums(1, 0, TRIPS)
            for l in range(NLAYER):
                for c in range(NC):
                    sp.wait_ge(*done(f"pq{l}", c))
                    sp.dma_start(chunk_of(tab[2 + l], c), chunk(pq, c)).then_inc(table_out, 16)
                    sp.dma_start(chunk_of(qtab[l], c), chunk(pq, c, 2 * D)[:, :, D:]).then_inc(qtable_out, 16)
                sp.wait_ge(q_row_in, 16 * (l + 1))
                sp.wait_ge(q_scattered, 16 * NT * (l + 1))
                sp.dma_start(q_at_start.rearrange("(p l) d -> p l d", p=P)[:, 0, :], q_row[:, l, :]
                             ).then_inc(q_row_out, 16)
                store_sums(2 + l, 0, TRIPS)
            for l in range(2):
                for c in range(NC):
                    sp.wait_ge(*done(f"gh{l}", c))
                    sp.dma_start(chunk_of(tab[5 + l], c), chunk(gN, c, WG)).then_inc(table_out, 16)
                    sp.dma_start(chunk_of(adtab[l], c), chunk(adN, c, 2)).then_inc(adtab_out, 16)
                sp.wait_ge(ad_scattered, 16 * NT * (l + 1))
                sp.dma_start(ad_e[:].rearrange("p l o -> p (l o)"), ad_g).then_inc(ad_in, 16)
                for q in range(PARTS):
                    sp.wait_ge(scanned, W * (l * PARTS + q + 1))
                    at = slice(q * LP * WG, (q + 1) * LP * WG)
                    sp.dma_start(sums_wg[:, at], big[:, at]).then_inc(weighted_out, 16)
            full = N // P
            for c in range(NC):
                sp.wait_ge(*done("l3_norm", c))
                t = range(tiles(c).start, min(tiles(c).stop, full))
                if len(t):
                    sp.dma_start(out[t.start * P:t.stop * P].rearrange("(t p) d -> p t d", p=P),
                                 yN[:, t.start:t.stop, 0:D]).then_inc(out_done, 16)
            sp.dma_start(out[full * P:N], yN[0:N - full * P, full, 0:D]).then_inc(out_done, 16)
            sp.wait_ge(out_done, 16 * (-(-full * P // CH) + 1))

        @block.gpsimd
        def _(pool):
            def made(ins, n):
                ins.then_inc(consts_made, 1)
                pool.wait_ge(consts_made, n)

            made(pool.memset(ident[:], 0.0), 1)
            made(pool.affine_select(out=ident[:], in_=ident[:], compare_op=ALU.not_equal, fill=1.0, base=0,
                                    pattern=[[-1, P]], channel_multiplier=1), 2)
            made(pool.memset(ones[:], 1.0), 3)
            made(pool.iota(node_i[:], pattern=[[P, NTP]], base=0, channel_multiplier=1), 4)
            made(pool.iota(tail_i[:], pattern=[[1, 2]], base=L - 1, channel_multiplier=L), 5)
            made(pool.iota(FM[1].bitcast(I32), pattern=[[1, NP]], base=0, channel_multiplier=0), 6)

            def gather(out_ap, table, index):
                return pool.indirect_dma_start(out=out_ap, out_offset=None, in_=table,
                                               in_offset=bass.IndirectOffsetOnAxis(ap=index, axis=0))

            def scatter(table, index, in_ap):
                return pool.indirect_dma_start(out=table, out_offset=bass.IndirectOffsetOnAxis(ap=index, axis=0),
                                               in_=in_ap, in_offset=None, bounds_check=EP - 1, oob_is_err=False)

            def gather_pass(k, width, start=0, end=TRIPS):
                table = x_d if k == 0 else tab[k][:, :]
                if k:
                    pool.wait_ge(table_out, 16 * NC * k)
                with pool.Fori(start, end) as i:
                    for s in range(SLOTS):
                        pool.wait_ge(staged, i * SLOTS + k * NG + s + 1)
                        pool.sem_inc(turn, 1)
                        for u in range(COLS):
                            gather(ringG[:, s, u * width:(u + 1) * width], table,
                                   idx_s[:, s, u:u + 1]).then_inc(gathered[s], 16)

            def gather_sums(k):
                if k < 5:
                    for s in range(SLOTS):
                        pool.wait_ge(slot_open[s], 16 * ((k + 1) * TRIPS + 1))
                else:
                    pool.wait_ge(weighted_out, 16 * PARTS * (k - 4))
                source, width = (sums, D) if k < 5 else (sums_w, WG)
                for c in range(NC):
                    for t in tiles(c):
                        gather(gN[:, t, 0:width], source[:, :], end_i[:, t:t + 1]).then_inc(sums_in[c], 16)

            gather_pass(0, D, 0, COUNT_FROM)
            pool.wait_ge(edge_rows_ready, 1)
            for t in range(NTP):
                gather(edge_rows[:, t * L:(t + 1) * L], dst_d, edge_row_i[:, t:t + 1]).then_inc(edge_rows_in, 16)
            gather_pass(0, D, COUNT_FROM, TRIPS)
            pool.wait_ge(zeros_out, 16 * ZERO_STORES)
            pool.wait_ge(prep_done, 1)
            gather_sums(0)
            gather_pass(1, D)
            gather_sums(1)
            for l in range(NLAYER):
                for c in range(NC):
                    pool.wait_ge(*done(f"pq{l}", c))
                    for t in tiles(c):
                        scatter(q_at_start[:, :], start_i[:, t:t + 1], pq[:, t, D:]).then_inc(q_scattered, 16)
                pool.wait_ge(qtable_out, 16 * NC * (l + 1))
                gather(q_row[:, l, :], qtab[l][:, :], dst_i[:, 0:1]).then_inc(q_row_in, 16)
                gather_pass(2 + l, D)
                gather_sums(2 + l)
            for l in range(2):
                if l:
                    pool.wait_ge(ad_in, 16 * l)
                for c in range(NC):
                    pool.wait_ge(*done(f"gh{l}", c))
                    for t in tiles(c):
                        scatter(ad_at_start[:, :], start_i[:, t:t + 1], adN[:, t, :]).then_inc(ad_scattered, 16)
                pool.wait_ge(adtab_out, 16 * NC * (l + 1))
                gather(ad_row[:, l, :], adtab[l][:, :], dst_i[:, 0:1]).then_inc(ad_row_in, 16)
                gather_pass(5 + l, WG)
                pool.wait_ge(weights_ready, l + 1)
                for q in range(1, PARTS):
                    part = every[:, q * LP:(q + 1) * LP, 1:WG]
                    nc.gpsimd.tensor_tensor(part, part, wgt[:, q * LP:(q + 1) * LP].unsqueeze(2).to_broadcast(
                        [P, LP, W]), ALU.mult).then_inc(multiplied, 1)
                gather_sums(5 + l)

        @block.scalar
        def _(act):
            def stage_indices(k, i, s):
                act.wait_ge(slot_open[s], (i + (k * TRIPS + 1)) * 16)
                act.sem_inc(turn_a, 1)
                nc.scalar.copy(idx_s[:, s, :], src_i[:, bass.ds((i * SLOTS + s) * COLS, COLS)]).then_inc(staged, 1)

            def load_edges(l, i, s):
                act.wait_ge(edge_summed, i * SLOTS + l * NG + s + 1)
                act.dma_start(ringQ[:, s, :], q_g[:, bass.ds((i * SLOTS + s) * COLS * D, COLS * D)]
                              ).then_inc(q_in[s], 16)
                act.dma_start(ringE[:, s, :], ef_d[:, bass.ds((i * SLOTS + s) * COLS * P, COLS * P)]
                              ).then_inc(ef_in[s], 16)

            def drain(out_ap, in_ap, fn, bias=0.0):
                return nc.scalar.activation(out_ap, in_ap, fn, bias=bias)

            def run_wave(phase, work):
                for name, c in wave(phase):
                    if WHO[name] == "A":
                        if is_filled(name):
                            act.wait_ge(*FILL(name, c))
                        work[name](c, cols(c)).then_inc(done_a, 1)

            def bank(c, lo=0, hi=D):
                n = cols(c)
                return ps[lo:hi, c, 0:n.stop - n.start]

            def turn_to(array, rows=D):
                return lambda c, n: drain(array[0:rows, n], bank(c, 0, rows), ACT.Copy)

            def std(prev):
                def go(c, n):
                    act.wait_ge(*done(prev, c))
                    t = tiles(c)
                    return drain(rstd[:, t.start:t.stop], stat[:, t.start:t.stop], ACT.Sqrt)
                return go

            for s in range(SLOTS):
                act.sem_inc(slot_open[s], 16)
            act.sem_inc(edge_summed, SLOTS)
            act.wait_ge(src_in, 16)
            for s in range(SLOTS):
                stage_indices(0, 0, s)
            act.wait_ge(zero_made, 1)
            act.dma_start(ad_g, FM[0][:, 0:2 * L]).then_inc(zeros_out, 16)
            act.dma_start(sums[EP:EP + 1, :], FM[0][0:1, 0:D]).then_inc(zeros_out, 16)
            act.dma_start(sums_w[EP:EP + 1, :], FM[0][0:1, 0:WG]).then_inc(zeros_out, 16)
            act.dma_start(q_g[:, 0:ZERO_W], FM[0][:, 0:ZERO_W]).then_inc(zeros_out, 16)
            with act.Fori(1, TRIPS) as i:
                for s in range(SLOTS):
                    stage_indices(0, i, s)
                act.dma_start(q_g[:, bass.ds(i * ZERO_W, ZERO_W)], FM[0][:, 0:ZERO_W]).then_inc(zeros_out, 16)
            act.wait_ge(weights_in, 16 * len(weight_loads))
            act.wait_ge(zeros_out, 16 * ZERO_STORES)
            run_wave("gin0", {
                "l0_T": turn_to(FM[0]),
                "l0_w1": lambda c, n: drain(FM[1][0:D, n], bank(c), ACT.Relu, c0[:, 0:1]),
                "l0_w2": lambda c, n: drain(FM[2][0:D, n], bank(c), ACT.Identity, c0[:, 1:2])})
            act.wait_ge(bn_scale_ready, 1)
            nc.scalar.activation(bn[:, 3:4], bn[:, 2:3], ACT.Sqrt).then_inc(bn_done, 1)
            act.wait_ge(bn_scale_ready, 2)
            nc.scalar.activation(FM[1][0:D, :], FM[2][0:D, :], ACT.Relu, bias=c0[:, 3:4],
                                 scale=bn[:, 5:6]).then_inc(bn_done, 1)
            run_wave("gin0_end", {"l0_std": std("l0_back")})
            with act.Fori(0, TRIPS) as i:
                for s in range(SLOTS):
                    stage_indices(1, i, s)
            run_wave("gin1", {
                "l1_T": turn_to(FM[0]),
                "l1_w1a": lambda c, n: drain(FM[1][:, n], bank(c, 0, P), ACT.Relu, c1[:, 0:1]),
                "l1_w1b": lambda c, n: drain(FM[2][:, n], bank(c, 0, P), ACT.Relu, c1[:, 1:2]),
                "l1_w2a": lambda c, n: drain(FM[3][:, n], bank(c, 0, P), ACT.Relu, c1[:, 2:3]),
                "l1_w2b": lambda c, n: drain(FM[4][:, n], bank(c, 0, P), ACT.Relu, c1[:, 3:4]),
                "l1_w3": lambda c, n: drain(FM[5][0:D, n], bank(c), ACT.Identity, c13[:]),
                "l1_std": std("l1_back"),
                "l2_T": turn_to(FM[0]),
                "enc": lambda c, n: drain(STATE[:, n], bank(c, D, P), ACT.Identity, enc_b[D:P])})
            for l in range(NLAYER):
                for s in range(SLOTS):
                    stage_indices(2 + l, 0, s)
                act.wait_ge(q_row_out, 16 * (l + 1))
                for s in range(SLOTS):
                    load_edges(l, 0, s)
                with act.Fori(1, TRIPS) as i:
                    for s in range(SLOTS):
                        stage_indices(2 + l, i, s)
                        load_edges(l, i, s)

                def gates(c, n, l=l):
                    drain(FM[4][D:P, n], bank(c), ACT.Sigmoid, b_z[0:D, l, 0:1])
                    return drain(FM[3][D:P, n], bank(c, D, P), ACT.Sigmoid, b_r[D:P, l, 0:1])

                def new_value(c, n, l=l):
                    act.wait_ge(*done(f"cell{l}", c))
                    return drain(FM[5][D:P, n], FM[5][D:P, n], ACT.Tanh, b_n[D:P, l, 0:1])

                run_wave(f"gru{l}", {
                    f"T{l}": turn_to(FM[0], W), f"agg{l}": lambda c, n: drain(FM[1][0:D, n], bank(c), ACT.Copy),
                    f"rz{l}": gates, f"tanh{l}": new_value,
                    "ro1": lambda c, n: drain(FM[2][0:D, n], bank(c), ACT.Relu, c_ro[:, 0:1]),
                    "ro2": lambda c, n: drain(FM[3][0:D, n], bank(c), ACT.Identity, c_ro[:, 1:2]),
                    "l2_std": std("l2_back"), "gT0": turn_to(FM[0])})
            for l in range(2):
                with act.Fori(0, TRIPS) as i:
                    for s in range(SLOTS):
                        stage_indices(5 + l, i, s)
                act.wait_ge(gap_ready, l + 1)
                nc.scalar.activation(wgt[:], wgt[:], ACT.Exp).then_inc(weights_ready, 1)

                def self_weight(c, n, l=l):
                    act.wait_ge(*done(f"gself{l}", c))
                    t = tiles(c)
                    return drain(self_w[:, t.start:t.stop], self_w[:, t.start:t.stop], ACT.Exp)

                run_wave(f"gat{l}", {f"gexp{l}": self_weight, "gT1": turn_to(FM[0]), "l3_std": std("gcarry1")})

        @block.vector
        def _(v):
            chain = Chain(v, vchain)
            link = chain.link

            def wide(value, width=D):
                return value.unsqueeze(2).to_broadcast([P, value.shape[1], width])

            def leaky(out_ap, in_ap):
                return v.scalar_tensor_tensor(out_ap, in_ap, SLOPE, in_ap, ALU.mult, ALU.max)

            def banked(c, width=D):
                return ps[:, c, :].rearrange("p (t d) -> p t d", d=P)[:, 0:len(tiles(c)), 0:width]

            def run_wave(phase, work):
                for name, c in wave(phase):
                    if WHO[name] == "V":
                        work[name](c).then_inc(done_v, 1)
                        v.wait_ge(*done(name, c))

            v.memset(FM[0], 0.0).then_inc(zero_made, 1)
            link(v.memset(carry[:], 0.0))
            link(v.memset(carry_q[:], 0.0))
            v.wait_ge(edges_in, 5 * 16)
            link(v.tensor_copy(dst_f[:], dst_i[:]))
            link(v.memset(same[:, 0:1], 0.0))
            link(v.tensor_tensor(same[:, 1:L], dst_f[:, 1:L], dst_f[:, 0:L - 1], ALU.is_equal))
            v.wait_ge(consts_made, 6)
            link(v.tensor_copy(FM[2], FM[1].bitcast(I32)))
            v.tensor_scalar(spans[:], FM[2], dst_f[:, 0:1], None, ALU.is_gt).then_inc(rows_before, 1)
            link(v.tensor_copy(node_f[:], node_i[:]))
            link(v.tensor_copy(tail[:], tail_i[:]))
            link(v.tensor_copy(beside[:], beside_i[:]))
            link(v.memset(b_pq[:, :, 0:D], 0.0))
            link(v.memset(enc_w[:, 0:D], 0.0))
            link(v.memset(w_n[0:D, :, D:P], 0.0))
            link(v.memset(w_n[D:P, :, 0:D], 0.0))
            link(v.memset(edge_row[:], 0.0))
            v.wait_ge(counts_ready, 1)
            link(v.tensor_scalar(edge_row[:, 0:NT], ps[:, 7, 0:NT], -1.0, 0.0, ALU.add, ALU.max))
            v.tensor_copy(edge_row_i[:], edge_row[:]).then_inc(edge_rows_ready, 1)

            def sum_columns(s, i, rows):
                for u in range(COLS):
                    now = rows[:, u * D:(u + 1) * D]
                    prev = carry[:] if u == 0 else rows[:, (u - 1) * D:u * D]
                    link(v.scalar_tensor_tensor(now, prev, same[:, bass.ds((i * SLOTS + s) * COLS + u, 1)], now,
                                                ALU.mult, ALU.add))

            def sum_group(k, s, i):
                rows = ringG[:, s, 0:COLS * D]
                sum_columns(s, i, rows)
                v.tensor_copy(carry[:], rows[:, (COLS - 1) * D:]).then_inc(summed, 1)
                v.wait_ge(summed, i * SLOTS + k * NG + s + 1)

            def sum_pass(k, start=0, end=TRIPS, counting=False):
                with v.Fori(start, end) as i:
                    chain.loop(i - start, SLOTS * (COLS + 2 * counting))
                    for s in range(SLOTS):
                        v.wait_ge(gathered[s], (i + (k * TRIPS + 1)) * 16 * COLS)
                        sum_group(k, s, i)
                        if counting:
                            t = (i - start) * SLOTS + s
                            link(v.tensor_scalar(logit[:], edge_rows[:, bass.ds(t * L, L)], 1.0, None, ALU.mult))
                            link(v.tensor_scalar(wgt[:], logit[:], node_f[:, bass.ds(t, 1)], 0.0, ALU.is_lt, ALU.add,
                                                 accum_out=count[:, bass.ds(t, 1)]))
                    chain.end(end - start)

            def message_pass(k, l):
                with v.Fori(0, TRIPS) as i:
                    chain.loop(i, SLOTS * (2 * COLS + 3))
                    for s in range(SLOTS):
                        v.wait_ge(q_in[s], (i + (l * TRIPS + 1)) * 16)
                        q, rows = ringQ[:, s, :], ringG[:, s, 0:COLS * D]
                        for u in range(COLS):
                            now = q[:, u * D:(u + 1) * D]
                            prev = carry_q[:] if u == 0 else q[:, (u - 1) * D:u * D]
                            link(v.scalar_tensor_tensor(now, prev, same[:, bass.ds((i * SLOTS + s) * COLS + u, 1)],
                                                        now, ALU.mult, ALU.add))
                        link(v.tensor_copy(carry_q[:], q[:, (COLS - 1) * D:]))
                        v.wait_ge(edge_product, i * SLOTS + l * NG + s + 1)
                        link(v.tensor_tensor(q, ps[:, 6 + s, :], q, ALU.add))
                        v.wait_ge(gathered[s], (i + (k * TRIPS + 1)) * 16 * COLS)
                        v.tensor_tensor(rows, rows, q, ALU.add).then_inc(edge_summed, 1)
                        v.wait_ge(edge_summed, i * SLOTS + l * NG + SLOTS + s + 1)
                        link(v.tensor_scalar(rows, rows, 0.0, None, ALU.max))
                        sum_group(k, s, i)
                    chain.end(TRIPS)

            def variance(c):
                y, t = chunk(yN, c), tiles(c)
                sq = chunk(FM[7][:, 0:NT * D].rearrange("p (t d) -> p t d", d=D), c)
                st = stat[:, t.start:t.stop]
                link(v.tensor_reduce(st, y, AX.X, ALU.add))
                link(v.tensor_scalar(st, st, 1.0 / D, None, ALU.mult))
                link(v.tensor_tensor(y, y, wide(st), ALU.subtract))
                link(v.tensor_tensor(sq, y, y, ALU.mult))
                link(v.tensor_reduce(st, sq, AX.X, ALU.add))
                return v.tensor_scalar(st, st, 1.0 / D, LN_EPS, ALU.mult, ALU.add)

            def norm(prefix, dst):
                def go(c):
                    t = tiles(c)
                    v.wait_ge(*done(prefix + "_std", c))
                    r = rstd[:, t.start:t.stop]
                    link(v.reciprocal(r, r))
                    return v.tensor_tensor(chunk(dst, c), chunk(yN, c), wide(r), ALU.mult)
                return go

            def back(name):
                def go(c):
                    v.wait_ge(*FILL(name, c))
                    link(v.tensor_tensor(chunk(yN, c), chunk(xN, c), banked(c), ALU.add))
                    return variance(c)
                return go

            def node_sums(name, k, extra):
                def go(c):
                    v.wait_ge(sums_in[c], 16 * len(tiles(c)) * (k + 1))
                    v.wait_ge(*FILL(name, c))
                    link(v.tensor_tensor(chunk(yN, c), chunk(gN, c), banked(c), ALU.add))
                    return extra(c)
                return go

            def add_x(c):
                return v.tensor_tensor(chunk(yN, c), chunk(yN, c), chunk(xN, c), ALU.add)

            def message_table(l):
                def go(c):
                    v.wait_ge(*FILL(f"pq{l}", c))
                    return v.tensor_tensor(chunk(pq, c, P), banked(c, P), b_pq[:, l, :].unsqueeze(1).to_broadcast(
                        [P, len(tiles(c)), P]), ALU.add)
                return go

            sum_pass(0, 0, COUNT_FROM)
            v.wait_ge(edge_rows_in, 16 * NTP)
            sum_pass(0, COUNT_FROM, COUNT_TO, counting=True)
            v.scalar_tensor_tensor(first[:], edge_row[:, 0:NT], float(L), count[:, 0:NT], ALU.mult, ALU.add
                                   ).then_inc(first_ready, 1)
            v.wait_ge(first_in, 48)
            link(v.tensor_tensor(has[:], nxt[:], first[:], ALU.is_gt))
            link(v.tensor_tensor(deg[:], nxt[:], first[:], ALU.subtract))
            link(v.tensor_scalar(tmp[:], nxt[:], -1.0 - EP, None, ALU.add))
            link(v.tensor_tensor(tmp[:], tmp[:], has[:], ALU.mult))
            link(v.tensor_scalar(tmp[:], tmp[:], float(EP), None, ALU.add))
            link(v.tensor_copy(end_i[:], tmp[:]))
            link(v.tensor_scalar(tmp[:], has[:], float(-SKIP), float(SKIP), ALU.mult, ALU.add))
            link(v.tensor_tensor(tmp[:], tmp[:], first[:], ALU.add))
            link(v.tensor_copy(start_i[:], tmp[:]))
            link(v.tensor_scalar(FM[1], FM[1], tail[:, 0:1], None, ALU.is_le))
            link(v.scalar_tensor_tensor(spans[:], FM[2], tail[:, 1:2], FM[1], ALU.is_gt, ALU.mult))
            link(v.tensor_scalar(pen_f[:, 1:L], same[:, 1:L], BIG, -BIG, ALU.mult, ALU.add))
            link(v.tensor_scalar(pen_b[:, 0:L - 1], same[:, 1:L], BIG, -BIG, ALU.mult, ALU.add))
            link(v.tensor_tensor(flag[:, 0:1], beside[:, 0:1], dst_f[:, 0:1], ALU.is_equal))
            link(v.tensor_tensor(flag[:, 1:2], beside[:, 1:2], dst_f[:, L - 1:L], ALU.is_equal))
            link(v.tensor_scalar(pen_f[:, 0:1], flag[:, 0:1], BIG, -BIG, ALU.mult, ALU.add))
            link(v.tensor_scalar(pen_b[:, L - 1:L], flag[:, 1:2], BIG, -BIG, ALU.mult, ALU.add))
            link(v.tensor_tensor(flag[:, 2:3], dst_f[:, 0:1], dst_f[:, L - 1:L], ALU.is_equal))
            link(v.tensor_scalar(flag[:, 0:2], flag[:, 0:2], flag[:, 2:3], None, ALU.mult))
            v.tensor_scalar(flag[:, 4:6], flag[:, 0:2], BIG, -BIG, ALU.mult, ALU.add).then_inc(pens_ready, 1)
            v.wait_ge(pens_turned, 1)
            link(v.tensor_copy(pen_row[:], ps[0:1, 7, 0:2 * P].rearrange("p (a b) -> p a b", a=2)))
            link(v.memset(car_row[:], -BIG))
            v.wait_ge(weights_in, 16 * len(weight_loads))
            link(v.tensor_tensor(b_z[0:D, :, 0], b_z[0:D, :, 0], b_z[0:D, :, 1], ALU.add))
            v.tensor_tensor(b_r[D:P, :, 0], b_r[D:P, :, 0], b_r[D:P, :, 1], ALU.add).then_inc(prep_done, 1)
            sum_pass(0, COUNT_TO, TRIPS)
            v.wait_ge(x_in, 16)
            run_wave("gin0", {"l0_carry": node_sums("l0_carry", 0, add_x)})
            for c in range(NC):
                v.wait_ge(*done("l0_w2", c))
            h = FM[2][0:D, 0:N]
            link(v.tensor_reduce(bn[:, 0:1], h, AX.X, ALU.add))
            link(v.tensor_scalar(bn[:, 0:1], bn[:, 0:1], 1.0 / N, None, ALU.mult))
            link(v.tensor_scalar(FM[2][0:D, :], FM[2][0:D, :], bn[:, 0:1], None, ALU.subtract))
            link(v.tensor_tensor(FM[3][0:D, 0:N], h, h, ALU.mult))
            link(v.tensor_reduce(bn[:, 1:2], FM[3][0:D, 0:N], AX.X, ALU.add))
            v.tensor_scalar(bn[:, 2:3], bn[:, 1:2], 1.0 / N, BN_EPS, ALU.mult, ALU.add).then_inc(bn_scale_ready, 1)
            v.wait_ge(bn_done, 1)
            link(v.reciprocal(bn[:, 4:5], bn[:, 3:4]))
            v.tensor_tensor(bn[:, 5:6], bn[:, 4:5], c0[:, 2:3], ALU.mult).then_inc(bn_scale_ready, 1)
            run_wave("gin0_end", {"l0_back": back("l0_back"), "l0_norm": norm("l0", xN)})

            sum_pass(1)
            v.wait_ge(table_out, 16 * NC)
            run_wave("gin1", {"l1_carry": node_sums("l1_carry", 1, add_x), "l1_back": back("l1_back"),
                              "l1_norm": norm("l1", xN), "pq0": message_table(0)})

            def attention_table(l):
                def go(c):
                    v.wait_ge(*FILL(f"gh{l}", c))
                    t = tiles(c)
                    y, g, logits = chunk(yN, c), chunk(gN, c, WG), chunk(adN, c, 2)
                    prod = chunk(FM[7][:, 0:NT * D].rearrange("p (t d) -> p t d", d=D), c)
                    link(v.tensor_copy(y, banked(c)))
                    link(v.tensor_copy(g[:, :, 1:W], y))
                    link(v.memset(g[:, :, W:WG], 1.0))
                    for o, vec in ((1, g_src), (0, g_dst)):
                        link(v.tensor_tensor(prod, y, vec[:, l, :].unsqueeze(1).to_broadcast([P, len(t), D]),
                                             ALU.mult))
                        link(v.tensor_reduce(logits[:, :, o], prod, AX.X, ALU.add))
                    return v.tensor_copy(g[:, :, 0], logits[:, :, 1])
                return go

            for l in range(NLAYER):
                message_pass(2 + l, l)

                def count_edges(c):
                    t = tiles(c)
                    return v.tensor_copy(yN[:, t.start:t.stop, D], deg[:, t.start:t.stop])

                def cell(c, l=l):
                    v.wait_ge(*FILL(f"cell{l}", c))
                    v.wait_ge(*done(f"rz{l}", c))
                    n = cols(c)
                    w, x = n.stop - n.start, FM[5][D:P, n]
                    link(v.scalar_tensor_tensor(x, ps[D:P, c, 0:w], b_n[D:P, l, 1:2], FM[3][D:P, n], ALU.add,
                                                ALU.mult))
                    return v.tensor_tensor(x, x, ps[0:D, c, 0:w], ALU.add)

                def state(c, l=l):
                    v.wait_ge(*done(f"tanh{l}", c))
                    n = cols(c)
                    h, x = STATE[:, n], FM[5][D:P, n]
                    link(v.tensor_tensor(h, h, x, ALU.subtract))
                    link(v.tensor_tensor(h, h, FM[4][D:P, n], ALU.mult))
                    return v.tensor_tensor(h, h, x, ALU.add)

                run_wave(f"gru{l}", {f"carry{l}": node_sums(f"carry{l}", 2 + l, count_edges), f"cell{l}": cell,
                                     f"state{l}": state, f"pq{l + 1}": message_table(l + 1),
                                     "l2_back": back("l2_back"), "l2_norm": norm("l2", xN),
                                     "gh0": attention_table(0)})

            for l in range(2):
                k = 5 + l
                with v.Fori(0, TRIPS) as i:
                    for s in range(SLOTS):
                        v.wait_ge(gathered[s], (i + (k * TRIPS + 1)) * 16 * COLS)
                        v.tensor_scalar(big[:, bass.ds((i * SLOTS + s) * COLS * WG, COLS * WG)], ringG[:, s, :], 1.0,
                                        None, ALU.mult).then_inc(slot_open[s], 16)
                for s in range(SLOTS):
                    v.wait_ge(slot_open[s], 16 * ((k + 1) * TRIPS + 1))
                link(v.tensor_copy(logit[:], every[:, :, 0]))
                v.wait_ge(ad_in, 16 * (l + 1))
                v.wait_ge(ad_row_in, 16 * (l + 1))
                link(v.tensor_copy(ad_e[:, 0, :], ad_row[:, l, :]))
                for o in range(2):
                    link(v.tensor_tensor_scan(ad_e[:, :, o], same[:], ad_e[:, :, o], 0.0, ALU.mult, ALU.add))
                link(v.tensor_tensor_scan(mx_f[:], pen_f[:], logit[:], -BIG, ALU.add, ALU.max))
                v.tensor_tensor_scan(mx_b[:, ::-1], pen_b[:, ::-1], logit[:, ::-1], -BIG, ALU.add,
                                     ALU.max).then_inc(maxima_ready, 1)
                v.wait_ge(maxima_turned, l + 1)
                link(v.tensor_copy(val_row[:], ps[0:1, 7, 0:2 * P].rearrange("p (a b) -> p a b", a=2)))
                link(v.tensor_tensor_scan(car_row[:, 0, 1:P + 1], pen_row[:, 0, :], val_row[:, 0, :], -BIG,
                                          ALU.add, ALU.max))
                v.tensor_tensor_scan(car_row[:, 1, 0:P][:, ::-1], pen_row[:, 1, ::-1], val_row[:, 1, ::-1], -BIG,
                                     ALU.add, ALU.max).then_inc(carries_ready, 1)
                v.wait_ge(carries_turned, l + 1)
                link(v.tensor_copy(edge_carry[:], ps[:, 7, 0:2]))
                link(v.tensor_tensor_scan(mx_f[:], pen_f[:], logit[:], edge_carry[:, 0:1], ALU.add, ALU.max))
                link(v.tensor_tensor_scan(mx_b[:, ::-1], pen_b[:, ::-1], logit[:, ::-1], edge_carry[:, 1:2],
                                          ALU.add, ALU.max))
                link(v.tensor_tensor(mx_f[:], mx_f[:], mx_b[:], ALU.max))
                link(v.tensor_tensor(mx_f[:], mx_f[:], ad_e[:, :, 1], ALU.max))
                link(v.tensor_tensor(mx_f[:], mx_f[:], ad_e[:, :, 0], ALU.add))
                link(leaky(mx_f[:], mx_f[:]))
                link(v.tensor_tensor(logit[:], logit[:], ad_e[:, :, 0], ALU.add))
                link(leaky(logit[:], logit[:]))
                v.tensor_tensor(wgt[:], logit[:], mx_f[:], ALU.subtract).then_inc(gap_ready, 1)
                link(v.tensor_copy(every[:, :, 0], mx_f[:]))
                v.wait_ge(weights_ready, l + 1)
                part = every[:, 0:LP, 1:WG]
                link(v.tensor_tensor(part, part, wgt[:, 0:LP].unsqueeze(2).to_broadcast([P, LP, W]), ALU.mult))
                for q in range(PARTS):
                    if q:
                        v.wait_ge(multiplied, l * (PARTS - 1) + q)
                    b = slice(q * LP, (q + 1) * LP)
                    with v.Fori(0, W // UNROLL) as i:
                        for u in range(UNROLL):
                            f = i * UNROLL + u + 1
                            one = big[:, bass.ds(f + q * LP * WG, LP, WG)]
                            start = big[:, bass.ds(f + (q * LP - 1) * WG, 1)] if q else 0.0
                            v.tensor_tensor_scan(one, same[:, b], one, start, ALU.mult, ALU.add).then_inc(scanned, 1)
                    v.wait_ge(scanned, W * (l * PARTS + q + 1))
                link(v.tensor_tensor(self_s[:], adN[:, :, 0], adN[:, :, 1], ALU.add))
                link(leaky(self_s[:], self_s[:]))

                def self_gap(c, k=k):
                    v.wait_ge(sums_in[c], 16 * len(tiles(c)) * (k + 1))
                    t = slice(tiles(c).start, tiles(c).stop)
                    link(v.tensor_scalar(tmp[:, t], has[:, t], BIG, -BIG, ALU.mult, ALU.add))
                    link(v.tensor_tensor(tmp[:, t], tmp[:, t], gN[:, t, 0], ALU.add))
                    link(v.tensor_tensor(tmp[:, t], tmp[:, t], self_s[:, t], ALU.max))
                    return v.tensor_tensor(self_w[:, t], self_s[:, t], tmp[:, t], ALU.subtract)

                def attend(c, l=l):
                    v.wait_ge(*FILL(f"gcarry{l}", c))
                    v.wait_ge(*done(f"gexp{l}", c))
                    t = slice(tiles(c).start, tiles(c).stop)
                    y, rows = chunk(yN, c), gN[:, t, 1:WG]
                    link(v.tensor_tensor(rows, rows, banked(c, W), ALU.add))
                    link(v.tensor_tensor(y, y, wide(self_w[:, t]), ALU.mult))
                    link(v.tensor_tensor(y, y, gN[:, t, 1:W], ALU.add))
                    link(v.tensor_tensor(tmp[:, t], gN[:, t, W], self_w[:, t], ALU.add))
                    link(v.tensor_scalar(tmp[:, t], tmp[:, t], 1e-16, None, ALU.add))
                    link(v.reciprocal(tmp[:, t], tmp[:, t]))
                    link(v.tensor_tensor(y, y, wide(tmp[:, t]), ALU.mult))
                    link(v.tensor_tensor(y, y, g_b[:, l, :].unsqueeze(1).to_broadcast([P, len(tiles(c)), D]),
                                         ALU.add))
                    if l == 0:
                        return v.tensor_scalar(y, y, 0.0, None, ALU.max)
                    link(add_x(c))
                    return variance(c)

                run_wave(f"gat{l}", {f"gself{l}": self_gap, f"gcarry{l}": attend, "gh1": attention_table(1),
                                     "l3_norm": norm("l3", yN)})

        @block.tensor
        def _(pe):
            pe.wait_ge(consts_made, 6)
            pe.wait_ge(rows_before, 1)
            for t in range(NT):
                mm = pe.matmul(ps[:, 7, t:t + 1], spans[:, t * P:(t + 1) * P], ones[:], start=True, stop=True)
            mm.then_inc(counts_ready, 1)
            pe.wait_ge(pens_ready, 1)
            pe.transpose(ps[0:1, 7, 0:P], flag[:, 4:5], ident[:])
            pe.transpose(ps[0:1, 7, P:2 * P], flag[:, 5:6], ident[:]).then_inc(pens_turned, 1)
            pe.wait_ge(weights_in, 16 * len(weight_loads))

            def run_wave(phase, work):
                names = [name for name, _ in PHASES[phase]]
                for name, c in wave(phase):
                    if is_filled(name):
                        k = names.index(name)
                        if k:
                            pe.wait_ge(*done(names[k - 1], c))
                        work[name](c).then_inc(filled, 1)

            def carries(tails, width=D):
                def go(c):
                    for j, t in enumerate(tiles(c)):
                        mm = pe.matmul(ps[:, c, j * P:j * P + width], spans[:, t * P:(t + 1) * P], tails,
                                       start=True, stop=True)
                    return mm
                return go

            def turn(source, width=D):
                def go(c):
                    for j, t in enumerate(tiles(c)):
                        mm = pe.transpose(ps[0:width, c, j * P:(j + 1) * P], source[:, t, 0:width], ident[:])
                    return mm
                return go

            def turn_back(source):
                def go(c):
                    for j, t in enumerate(tiles(c)):
                        mm = pe.transpose(ps[:, c, j * P:j * P + D], source[0:D, t * P:(t + 1) * P], ident[0:D, 0:D])
                    return mm
                return go

            def product(pairs, rows=D):
                def go(c):
                    n = cols(c)
                    for q, (wt, x) in enumerate(pairs):
                        mm = pe.matmul(ps[0:rows, c, 0:n.stop - n.start], wt, x[:, n], start=(q == 0),
                                       stop=(q == len(pairs) - 1))
                    return mm
                return go

            def node_product(x, wt, width):
                def go(c):
                    for j, t in enumerate(tiles(c)):
                        mm = pe.matmul(ps[:, c, j * P:j * P + width], x[:, t * P:(t + 1) * P], wt, start=True,
                                       stop=True)
                    return mm
                return go

            pe.wait_ge(summed, NG)
            run_wave("gin0", {"l0_carry": carries(carry[:]), "l0_T": turn(yN),
                              "l0_w1": product([(w01[:], FM[0][0:D])]), "l0_w2": product([(w02[:], FM[1][0:D])])})
            pe.wait_ge(bn_done, 2)
            run_wave("gin0_end", {"l0_back": turn_back(FM[1])})
            pe.wait_ge(summed, 2 * NG)
            run_wave("gin1", {
                "l1_carry": carries(carry[:]), "l1_T": turn(yN),
                "l1_w1a": product([(w11[:, 0:P], FM[0][0:D])], P), "l1_w1b": product([(w11[:, P:HID], FM[0][0:D])], P),
                "l1_w2a": product([(w12[:, 0, 0:P], FM[1]), (w12[:, 1, 0:P], FM[2])], P),
                "l1_w2b": product([(w12[:, 0, P:HID], FM[1]), (w12[:, 1, P:HID], FM[2])], P),
                "l1_w3": product([(w13[:, 0, :], FM[3]), (w13[:, 1, :], FM[4])]), "l1_back": turn_back(FM[5]),
                "l2_T": turn(xN), "enc": product([(enc_w[:], FM[0][0:D])], P),
                "pq0": node_product(STATE, w_pq[D:P, 0, :], 2 * D)})
            for l in range(NLAYER):
                pe.wait_ge(*done(f"pq{l}", NC - 1))
                with pe.Fori(0, TRIPS) as i:
                    for s in range(SLOTS):
                        pe.wait_ge(ef_in[s], (i + (l * TRIPS + 1)) * 16)
                        for u in range(COLS):
                            mm = pe.matmul(ps[:, 6 + s, u * D:(u + 1) * D], ringE[:, s, u * P:(u + 1) * P],
                                           w_e[:, l, :], start=True, stop=True)
                        mm.then_inc(edge_product, 1)
                pe.wait_ge(summed, (3 + l) * NG)
                work = {f"carry{l}": carries(carry[:]), f"T{l}": turn(yN, W),
                        f"agg{l}": product([(w_m2[:, l, :], FM[0][0:W])]),
                        f"rz{l}": product([(w_rz[:, l, :], FM[1])], P), f"cell{l}": product([(w_n[:, l, :], FM[1])], P),
                        "ro1": product([(ro1[D:P], STATE)]), "ro2": product([(ro2[:], FM[2][0:D])]),
                        "l2_back": turn_back(FM[3]), "gT0": turn(xN),
                        "gh0": node_product(FM[0][0:D], gw[:, 0, :], D)}
                if l < NLAYER - 1:
                    work[f"pq{l + 1}"] = node_product(STATE, w_pq[D:P, l + 1, :], 2 * D)
                run_wave(f"gru{l}", work)
            for l in range(2):
                pe.wait_ge(maxima_ready, l + 1)
                pe.transpose(ps[0:1, 7, 0:P], mx_f[:, L - 1:L], ident[:])
                pe.transpose(ps[0:1, 7, P:2 * P], mx_b[:, 0:1], ident[:]).then_inc(maxima_turned, 1)
                pe.wait_ge(carries_ready, l + 1)
                pe.transpose(ps[:, 7, 0:1], car_row[:, 0, 0:P], ones[0:1, :])
                pe.transpose(ps[:, 7, 1:2], car_row[:, 1, 1:P + 1], ones[0:1, :]).then_inc(carries_turned, 1)
                pe.wait_ge(scanned, (l + 1) * PARTS * W)
                run_wave(f"gat{l}", {f"gcarry{l}": carries(every[:, L - 1, 1:WG], W), "gT1": turn(yN),
                                     "gh1": node_product(FM[0][0:D], gw[:, 1, :], D)})


_LAID_OUT = ("x", "src", "dst", "edge_attr_16")


def kernel(**inputs):
    import numpy as np
    import concourse.bacc as bacc
    from concourse.bass_utils import run_bass_kernel_spmd as run

    nc = bacc.Bacc("TRN2", target_bir_lowering=False, num_devices=1)
    arrays = {k: np.ascontiguousarray(v) for k, v in inputs.items() if k not in _LAID_OUT}
    x, src, dst, ef = (np.asarray(inputs[k]) for k in _LAID_OUT)
    arrays["x"] = np.concatenate([x, np.zeros((NP - N, D), x.dtype)])
    arrays["src"] = np.concatenate([src, np.zeros(EP - E, src.dtype)]).reshape(P, L)
    arrays["dst"] = np.concatenate([dst, np.full(EP - E, N, dst.dtype)]).reshape(P, L)
    arrays["none"] = np.full((1, 1), -1, dst.dtype)
    padded = np.concatenate([ef, np.zeros((EP - E, EF), ef.dtype)]).reshape(P, L, EF)
    arrays["edge_attr_16"] = np.ascontiguousarray(padded.transpose(2, 1, 0)).reshape(EF, L * P)
    aps = {k: nc.dram_tensor(f"in_{k}", v.shape, mybir.dt.from_np(v.dtype), kind="ExternalInput").ap()
           for k, v in arrays.items()}
    out = nc.dram_tensor("out_nodes", (N, D), F32, kind="ExternalOutput").ap()
    build(nc, aps, out)
    r = run(nc, [{f"in_{k}": v for k, v in arrays.items()}], core_ids=[0])
    return r.results[0]["out_nodes"]
```

```python
from contextlib import ExitStack

import concourse.bass as bass
from concourse import mybir

F32 = mybir.dt.float32
I32 = mybir.dt.int32
I16 = mybir.dt.int16
BF16 = mybir.dt.bfloat16
ALU = mybir.AluOpType
ACT = mybir.ActivationFunctionType
AX = mybir.AxisListType

P = 128
N, E, D = 3125, 53125, 64
NT = -(-N // P)
NP = NT * P
L = -(-E // P)
COLS, SLOTS = 8, 2
RING = 4
L = -(-L // (COLS * RING)) * COLS * RING
EP = P * L
NG = L // COLS
TURNS = NG // SLOTS
TRIPS = NG // RING
COUNT_FROM = 3
COUNT_TO = COUNT_FROM + -(-NT // RING)
NTP = -(-NT // RING) * RING
W = D + 1
WG = D + 2
HID = 256
EF = 16
CH = 512
NC = -(-NP // CH)
BN_EPS = LN_EPS = 1e-5
SLOPE = 0.2
BIG = 1e30
NLAYER = 3
PIECES = RING
HOT = 7
ZERO_W = L * D // TRIPS
ZERO_STORES = TRIPS + 3
BOUNDS = [0, 9 * L // 52, 23 * L // 52, 40 * L // 52, L]
PARTS = len(BOUNDS) - 1
UNROLL = 13
SKIP = 1 << 20

NORM = [("std", "A"), ("norm", "V")]
PHASES = {
    "gin0": [("l0_carry", "V"), ("l0_T", "A"), ("l0_w1", "A"), ("l0_w2", "A"), ("l0_stats", "V")],
    "gin0_end": [("l0_bn", "A"), ("l0_back", "V")] + [("l0_" + n, w) for n, w in NORM],
    "gin1": [("l1_carry", "V"), ("l1_T", "A"), ("l1_w1a", "A"), ("l1_w1b", "A"), ("l1_w2a", "A"), ("l1_w2b", "A"),
             ("l1_w3", "A"), ("l1_back", "V")] + [("l1_" + n, w) for n, w in NORM]
            + [("l2_T", "A"), ("enc", "A"), ("pq0", "V")],
}
for _l in range(NLAYER):
    PHASES[f"gru{_l}"] = [(f"carry{_l}", "V"), (f"T{_l}", "A"), (f"agg{_l}", "A"), (f"rz{_l}", "A"),
                          (f"cell{_l}", "V"), (f"tanh{_l}", "A"), (f"state{_l}", "V")]
    PHASES[f"gru{_l}"] += ([(f"pq{_l + 1}", "V")] if _l < NLAYER - 1 else
                           [("ro1", "A"), ("ro2", "A"), ("l2_back", "V")] + [("l2_" + n, w) for n, w in NORM]
                           + [("gT0", "A"), ("gh0", "V")])
PHASES["gat0"] = [("gself0", "V"), ("gexp0", "A"), ("gcarry0", "V"), ("gT1", "A"), ("gh1", "V")]
PHASES["gat1"] = [("gself1", "V"), ("gexp1", "A"), ("gcarry1", "V")] + [("l3_" + n, w) for n, w in NORM]
UNFILLED = ("std", "norm", "tanh", "state", "gself", "gexp", "stats", "bn")


def is_filled(name):
    return not any(u in name for u in UNFILLED)


def wave(phase):
    names = [name for name, _ in PHASES[phase]]
    return [(names[k], step - k) for step in range(NC + len(names) - 1) for k in reversed(range(len(names)))
            if 0 <= step - k < NC]


ORDER = [item for phase in PHASES for item in wave(phase)]
WHO = {name: who for stages in PHASES.values() for name, who in stages}
FILLED_AT, DONE_AT, _count = {}, {}, {"A": 0, "V": 0, "P": 0}
for _name, _c in ORDER:
    if is_filled(_name):
        _count["P"] += 1
        FILLED_AT[_name, _c] = _count["P"]
    _count[WHO[_name]] += 1
    DONE_AT[_name, _c] = _count[WHO[_name]]


class Pass:

    span = RING * COLS

    def __init__(self, k, step=0, most=0, width=D, last=TRIPS - 1):
        self.k, self.width, self.last = k, width, last
        self.hot = list(range(step - 1, self.span, step))[:most] if step else []
        self.step, self.u = step, len(self.hot)

    def hot_in(self, j):
        return [(b - j * COLS, n) for n, b in enumerate(self.hot) if b // COLS == j]

    def gathers(self, j, use):
        return COLS - (len(self.hot_in(j)) if use else 0)

    def turn(self, i, j):
        return i * (RING // SLOTS) + j // SLOTS

    def opened(self, i):
        return i + (self.k * TRIPS + 1)

    def gathered(self, i, j, use):
        before = sum(p.total(j) for p in PASSES[:self.k])
        if use:
            return (i - 1) * self.gathers(j, True) + (before + COLS + self.gathers(j, True))
        spared = self.last * (COLS - self.gathers(j, True)) if not isinstance(i, int) else 0
        return i * COLS + (before + COLS - spared)

    def total(self, j):
        return COLS * TRIPS - self.last * (COLS - self.gathers(j, True))

    def unit(self, i):
        return i - 1 + sum(p.last for p in PASSES[:self.k] if p.hot)

    def run(self, eng, body):
        if not self.hot:
            with eng.Fori(0, TRIPS) as i:
                body(i, False, False)
            return
        body(0, False, True)
        with eng.Fori(1, self.last) as i:
            body(i, True, True)
        body(self.last, True, False)
        if self.last < TRIPS - 1:
            with eng.Fori(self.last + 1, TRIPS) as i:
                body(i, False, False)


GAT_HOT = 5
GAT_SCRATCH = NT * GAT_HOT * P // 2 + -(-NT * 3 * WG // 2) + GAT_HOT * P * 3 // 2 + GAT_HOT * WG
GAT_LAST = (L * WG - GAT_SCRATCH) // (RING * COLS * WG)
PASSES = ([Pass(0), Pass(1, 4, HOT)] + [Pass(2 + l, COLS, RING) for l in range(NLAYER)]
          + [Pass(5 + l, 6, GAT_HOT, WG, GAT_LAST) for l in range(2)])
LAST = 3
AHEAD = 2
PIECE_TILES = [range(0, COLS), range(COLS, 2 * COLS), range(2 * COLS, NT - LAST), range(NT - LAST, NT)]
assert len(PIECE_TILES) == PIECES and 0 < len(PIECE_TILES[2]) <= COLS


def tiles(c):
    return range(c * CH // P, min(NT, (c + 1) * CH // P))


def cols(c):
    return slice(c * CH, min(NP, (c + 1) * CH))


class Chain:

    def __init__(self, eng, sem):
        self.eng, self.sem, self.n, self.base = eng, sem, 0, None

    def value(self):
        return self.n if self.base is None else self.base + self.n

    def link(self, ins):
        ins.then_inc(self.sem, 1)
        self.n += 1
        self.eng.wait_ge(self.sem, self.value())

    def mark(self, ins):
        ins.then_inc(self.sem, 1)
        self.n += 1
        return self.value()

    def loop(self, i, per_trip):
        self.start, self.per_trip = self.n, per_trip
        self.base, self.n = i * per_trip, self.start

    def end(self, trips):
        assert self.n == self.start + self.per_trip, self.n - self.start
        self.base, self.n = None, self.start + trips * self.per_trip


def build(nc, a, out):
    with ExitStack() as ctx:
        ctx.enter_context(nc.allow_non_contiguous_dma(reason="a few columns of one value per partition"))

        def sb(name, shape, dt=F32):
            return ctx.enter_context(nc.sbuf_tensor(name, shape, dt))

        def sem(name):
            return ctx.enter_context(nc.semaphore(name))

        def dram(name, shape, dt=F32):
            return nc.dram_tensor(name, shape, dt, kind="Internal").ap()

        tab = [dram(f"tab{k}", (NP, WG if k >= 5 else D)) for k in range(7)]
        qtab = [dram(f"qtab{l}", (NP, D)) for l in range(NLAYER)]
        adtab = [dram(f"adtab{l}", (NP, 2)) for l in range(2)]
        q_at_start = dram("q_at_start", (EP, D))
        ad_at_start = dram("ad_at_start", (EP, 2))
        sums = dram("sums", (EP + 1, D))
        sums_w = dram("sums_w", (EP + 1, WG))
        first_d = dram("first_d", (NP + 1, 1))

        big = sb("big", [P, L * WG])
        FM = [big[:, k * NP:(k + 1) * NP] for k in range(8)]
        spans = sb("spans", [P, NP])
        src_i = sb("src_i", [P, L], I32)
        dst_i = sb("dst_i", [P, L], I32)
        dst_f = sb("dst_f", [P, L])
        same = sb("same", [P, L])
        pen_f = sb("pen_f", [P, L])
        pen_b = sb("pen_b", [P, L])
        logit = sb("logit", [P, L])
        ad_e = sb("ad_e", [P, L, 2])
        mx_f = sb("mx_f", [P, L])
        mx_b = sb("mx_b", [P, L])
        wgt = sb("wgt", [P, L])
        xN = sb("xN", [P, NT, D])
        yN = sb("yN", [P, NT, W])
        gN = sb("gN", [P, NT, WG])
        ringG = sb("ringG", [P, RING, COLS * WG])
        ringQ = sb("ringQ", [P, SLOTS, COLS * D])
        ringE = sb("ringE", [EF, SLOTS, COLS * P])
        idx_s = sb("idx_s", [P, RING, COLS], I32)
        carry = sb("carry", [P, D])
        carry_q = sb("carry_q", [P, D])
        q_row = sb("q_row", [P, NLAYER, D])
        ad_row = sb("ad_row", [P, 2, 2])
        ident = sb("ident", [P, P])
        ones = sb("ones", [P, 1])
        node_i = sb("node_i", [P, NTP], I32)
        node_f = sb("node_f", [P, NTP])
        edge_row_i = sb("edge_row_i", [P, NTP], I32)
        edge_row = sb("edge_row", [P, NTP])
        count = sb("count", [P, NTP])
        first = sb("first", [P, NT])
        nxt = sb("nxt", [P, NT])
        has = sb("has", [P, NT])
        deg = sb("deg", [P, NT])
        tmp = sb("tmp", [P, NT])
        start_i = sb("start_i", [P, NT], I32)
        end_i = sb("end_i", [P, NT], I32)
        tail = sb("tail", [P, 2])
        tail_i = sb("tail_i", [P, 2], I32)
        beside_i = sb("beside_i", [P, 2], I32)
        beside = sb("beside", [P, 2])
        flag = sb("flag", [P, 6])
        stat = sb("stat", [P, NT])
        rstd = sb("rstd", [P, NT])
        adN = sb("adN", [P, NT, 2])
        self_w = sb("self_w", [P, NT])
        self_s = sb("self_s", [P, NT])
        edge_carry = sb("edge_carry", [P, 2])
        pen_row = sb("pen_row", [1, 2, P])
        val_row = sb("val_row", [1, 2, P])
        car_row = sb("car_row", [1, 2, P + 1])
        edge_end = sb("edge_end", [1, 1])
        bn = sb("bn", [D, 8])
        bn_chunk = sb("bn_chunk", [D, 4, NC])
        w01, w02 = sb("w01", [D, D]), sb("w02", [D, D])
        c0 = sb("c0", [D, 4])
        w11 = sb("w11", [D, HID])
        w12 = sb("w12", [P, 2, HID])
        w13 = sb("w13", [P, 2, D])
        c1 = sb("c1", [P, 4])
        c13 = sb("c13", [D, 1])
        enc_w, enc_b = sb("enc_w", [D, P]), sb("enc_b", [P, 1])
        w_pq = sb("w_pq", [P, NLAYER, 2 * D])
        w_e = sb("w_e", [EF, NLAYER, D])
        b_pq = sb("b_pq", [P, NLAYER, 2 * D])
        w_m2 = sb("w_m2", [W, NLAYER, D])
        w_rz = sb("w_rz", [P, NLAYER, P])
        w_n = sb("w_n", [P, NLAYER, P])
        b_z, b_r = sb("b_z", [P, NLAYER, 2]), sb("b_r", [P, NLAYER, 2])
        b_n = sb("b_n", [P, NLAYER, 2])
        ro1, ro2, c_ro = sb("ro1", [P, D]), sb("ro2", [D, D]), sb("c_ro", [D, 2])
        gw = sb("gw", [D, 2, D])
        g_src, g_dst, g_b = sb("g_src", [P, 2, D]), sb("g_dst", [P, 2, D]), sb("g_b", [P, 2, D])

        class Scratch:

            def __init__(self, way, split, hot, src_all, src_hot, parts, part_sum, rest):
                w = way.width
                self.split = split.bitcast(BF16).rearrange("p (t j) -> p t j", t=NT)[:, :, 0:3 * w]
                self.hot = hot.bitcast(BF16).rearrange("p (t e) -> p t e", t=NT)
                self.src_all, self.src_hot = src_all.bitcast(I32), src_hot.bitcast(I16)
                self.parts = parts.rearrange("p (u k d) -> p u k d", k=3, d=w)
                self.part_sum = part_sum.rearrange("p (u d) -> p u d", d=w)
                self.rest = rest.rearrange("p (t d) -> p t d", d=w)

        def side_by_side(start, sizes):
            ends = [start + sum(sizes[:n + 1]) for n in range(len(sizes))]
            return [big[:, end - n:end] for end, n in zip(ends, sizes)]

        def scratch(way):
            u, w = way.u, way.width
            hot_size, sources = NT * u * P // 2, [u * P, u * P // 2]
            if w == D:
                hot = big[:, 2 * NP:2 * NP + hot_size]
                src_all, src_hot, parts, part_sum = side_by_side(7 * NP, sources + [u * 3 * w, u * w])
                return Scratch(way, FM[0], hot, src_all, src_hot, parts, part_sum, FM[5][:, NT * D:2 * NT * D])
            split, hot, src_all, src_hot, part_sum = side_by_side(
                L * WG - GAT_SCRATCH, [NT * 3 * w // 2, hot_size] + sources + [u * w])
            parts = ringQ[:].rearrange("p s n -> p (s n)")[:, 0:u * 3 * w]
            return Scratch(way, split, hot, src_all, src_hot, parts, part_sum, hot[:, 0:NT * w])

        of = [scratch(way) if way.hot else None for way in PASSES]

        ps = ctx.enter_context(nc.psum_tensor("ps", [P, 8, 512], F32))

        src_in, edges_in, x_in, weights_in = sem("src_in"), sem("edges_in"), sem("x_in"), sem("weights_in")
        consts_made = sem("consts_made")
        zero_made, zeros_out = sem("zero_made"), sem("zeros_out")
        act_slots_open = sem("act_slots_open")
        rows_before = sem("rows_before")
        counts_ready = sem("counts_ready")
        edge_rows_ready, edge_rows_in = sem("edge_rows_ready"), sem("edge_rows_in")
        first_ready, first_out, first_in = sem("first_ready"), sem("first_out"), sem("first_in")
        prep_done = sem("prep_done")
        pens_ready, pens_turned = sem("pens_ready"), sem("pens_turned")
        filled, done_a, done_v = sem("filled"), sem("done_a"), sem("done_v")
        vchain = sem("vchain")
        split_ready = sem("split_ready")
        src_all_in, src_hot_ready = sem("src_all_in"), sem("src_hot_ready")
        hot_ready, hot_used = sem("hot_ready"), sem("hot_used")
        parts_ready, parts_used = sem("parts_ready"), sem("parts_used")
        staged = sem("staged")
        turn, turn_a = sem("turn"), sem("turn_a")
        gathered = [sem(f"gathered{s}") for s in range(RING)]
        slot_open = [sem(f"slot_open{s}") for s in range(RING)]
        q_in = [sem(f"q_in{s}") for s in range(SLOTS)]
        ef_in = [sem(f"ef_in{s}") for s in range(SLOTS)]
        edge_product = sem("edge_product")
        clipped = sem("clipped")
        edge_summed = sem("edge_summed")
        summed = sem("summed")
        weighted_out = sem("weighted_out")
        multiplied, scanned = sem("multiplied"), sem("scanned")
        sums_in = [sem(f"sums_in{c}") for c in range(NC)]
        table_out, qtable_out = sem("table_out"), sem("qtable_out")
        q_scattered, q_row_in, q_row_out = sem("q_scattered"), sem("q_row_in"), sem("q_row_out")
        adtab_out, ad_scattered = sem("adtab_out"), sem("ad_scattered")
        ad_row_in, ad_in = sem("ad_row_in"), sem("ad_in")
        maxima_ready, maxima_turned = sem("maxima_ready"), sem("maxima_turned")
        carries_ready, carries_turned = sem("carries_ready"), sem("carries_turned")
        gap_ready, weights_ready = sem("gap_ready"), sem("weights_ready")
        bn_scale_ready, bn_done = sem("bn_scale_ready"), sem("bn_done")
        out_done = sem("out_done")

        def done(name, c):
            return (done_a if WHO[name] == "A" else done_v), DONE_AT[name, c]

        src_d, dst_d, x_d, ef_d = a["src"], a["dst"], a["x"], a["edge_attr_16"]

        FILL = lambda name, c: (filled, FILLED_AT[name, c])
        STATE = FM[1][D:P]
        pq = FM[6].rearrange("p (t d) -> p t d", t=NT)
        edge_rows = big[:, 3 * NP:3 * NP + NTP * L].bitcast(I32)

        def chunk_of(table, c):
            return table.rearrange("(t p) d -> p t d", p=P)[:, tiles(c).start:tiles(c).stop]

        def chunk(x, c, width=D):
            return x[:, tiles(c).start:tiles(c).stop, 0:width]

        sums_g = sums[0:EP].rearrange("(p l) d -> p (l d)", p=P)
        sums_wg = sums_w[0:EP].rearrange("(p l) d -> p (l d)", p=P)
        q_g = q_at_start.rearrange("(p l) d -> p (l d)", p=P)
        every = big[:].rearrange("p (b w) -> p b w", w=WG)
        ad_g = ad_at_start.rearrange("(p l) d -> p (l d)", p=P)

        wih, whh = (a[f"L2_gnn_gru_W{n}"].rearrange("l k n -> k l n") for n in ("ih", "hh"))
        bih, bhh = (a[f"L2_gnn_gru_b{n}"].rearrange("l (g d) -> d l g", g=3) for n in ("ih", "hh"))
        weight_loads = [
            (w01[:], a["L0_gnn_W1"]), (w02[:], a["L0_gnn_W2"]),
            (c0[:, 0:1], a["L0_gnn_b1"].unsqueeze(1)), (c0[:, 1:2], a["L0_gnn_b2"].unsqueeze(1)),
            (c0[:, 2:3], a["L0_gnn_gamma"].unsqueeze(1)), (c0[:, 3:4], a["L0_gnn_beta"].unsqueeze(1)),
            (w11[:], a["L1_gnn_W1"]), (w12[:], a["L1_gnn_W2"].rearrange("(k p) n -> p k n", p=P)),
            (w13[:], a["L1_gnn_W3"].rearrange("(k p) n -> p k n", p=P)),
            (c1[:, 0:1], a["L1_gnn_b1"][0:P].unsqueeze(1)), (c1[:, 1:2], a["L1_gnn_b1"][P:HID].unsqueeze(1)),
            (c1[:, 2:3], a["L1_gnn_b2"][0:P].unsqueeze(1)), (c1[:, 3:4], a["L1_gnn_b2"][P:HID].unsqueeze(1)),
            (c13[:], a["L1_gnn_b3"].unsqueeze(1)),
            (enc_w[:, D:P], a["L2_gnn_enc_W"]), (enc_b[D:P], a["L2_gnn_enc_b"].unsqueeze(1)),
            (w_pq[D:P, :, 0:D], a["L2_gnn_msg_W1"][:, 0:D, :].rearrange("l k n -> k l n")),
            (w_pq[D:P, :, D:2 * D], a["L2_gnn_msg_W1"][:, D:2 * D, :].rearrange("l k n -> k l n")),
            (w_e[:], a["L2_gnn_msg_W1"][:, 2 * D:, :].rearrange("l k n -> k l n")),
            (w_m2[0:D], a["L2_gnn_msg_W2"].rearrange("l k n -> k l n")),
            (w_m2[D:W], a["L2_gnn_msg_b2"].unsqueeze(0)),
            (w_rz[0:D, :, 0:D], wih[:, :, D:2 * D]), (w_rz[0:D, :, D:P], wih[:, :, 0:D]),
            (w_rz[D:P, :, 0:D], whh[:, :, D:2 * D]), (w_rz[D:P, :, D:P], whh[:, :, 0:D]),
            (w_n[0:D, :, 0:D], wih[:, :, 2 * D:]), (w_n[D:P, :, D:P], whh[:, :, 2 * D:]),
            (b_r[D:P, :, 0], bih[:, :, 0]), (b_r[D:P, :, 1], bhh[:, :, 0]),
            (b_z[0:D, :, 0], bih[:, :, 1]), (b_z[0:D, :, 1], bhh[:, :, 1]),
            (b_n[D:P, :, 0], bih[:, :, 2]), (b_n[D:P, :, 1], bhh[:, :, 2]),
            (ro1[D:P], a["L2_gnn_ro_W1"]), (ro2[:], a["L2_gnn_ro_W2"]),
            (c_ro[:, 0:1], a["L2_gnn_ro_b1"].unsqueeze(1)), (c_ro[:, 1:2], a["L2_gnn_ro_b2"].unsqueeze(1)),
            (b_pq[:, :, D:2 * D], a["L2_gnn_msg_b1"].partition_broadcast(P)),
        ]
        for l in range(2):
            weight_loads += [
                (gw[:, l, :], a[f"L3_gnn_W{l + 1}"]),
                (g_src[:, l, :], a[f"L3_gnn_a_src{l + 1}"].partition_broadcast(P)),
                (g_dst[:, l, :], a[f"L3_gnn_a_dst{l + 1}"].partition_broadcast(P)),
                (g_b[:, l, :], a[f"L3_gnn_b{l + 1}"].partition_broadcast(P))]

        block = ctx.enter_context(nc.Block())

        @block.sync
        def _(sp):
            sp.dma_start(src_i[:], src_d).then_inc(src_in, 16)
            sp.dma_start(dst_i[:], dst_d).then_inc(edges_in, 16)
            sp.dma_start(beside_i[1:P, 0:1], dst_d[0:P - 1, L - 1:L]).then_inc(edges_in, 16)
            sp.dma_start(beside_i[0:P - 1, 1:2], dst_d[1:P, 0:1]).then_inc(edges_in, 16)
            sp.dma_start(beside_i[0:1, 0:1], a["none"]).then_inc(edges_in, 16)
            sp.dma_start(beside_i[P - 1:P, 1:2], a["none"]).then_inc(edges_in, 16)
            sp.dma_start(xN[:], x_d.rearrange("(t p) d -> p t d", p=P)).then_inc(x_in, 16)
            for dst, s in weight_loads:
                sp.dma_start(dst, s).then_inc(weights_in, 16)

            def store_sums(k, start=0, end=TRIPS):
                with sp.Fori(start, end) as i:
                    for s in range(RING):
                        sp.wait_ge(summed, i * RING + k * NG + s + 1)
                        sp.dma_start(sums_g[:, bass.ds((i * RING + s) * COLS * D, COLS * D)],
                                     ringG[:, s, 0:COLS * D]).then_inc(slot_open[s], 16)

            store_sums(0, 0, COUNT_TO)
            sp.wait_ge(first_ready, 1)
            sp.dma_start(first_d[0:NP].rearrange("(t p) o -> p (t o)", p=P), first[:]).then_inc(first_out, 16)
            sp.dma_start(first_d[NP:NP + 1], tail[P - 1:P, 1:2]).then_inc(first_out, 16)
            sp.wait_ge(first_out, 32)
            sp.dma_start(nxt[:], first_d[1:NP + 1].rearrange("(t p) o -> p (t o)", p=P)).then_inc(first_in, 16)
            row = first_d.rearrange("n o -> (n o)")
            sp.dma_start(FM[1], row[0:NP].partition_broadcast(P)).then_inc(first_in, 16)
            sp.dma_start(FM[2], row[1:NP + 1].partition_broadcast(P)).then_inc(first_in, 16)
            store_sums(0, COUNT_TO, TRIPS)

            for c in range(NC):
                sp.wait_ge(*done("l0_norm", c))
                sp.dma_start(chunk_of(tab[1], c), chunk(xN, c)).then_inc(table_out, 16)
            store_sums(1)
            for l in range(NLAYER):
                for c in range(NC):
                    sp.wait_ge(*done(f"pq{l}", c))
                    sp.dma_start(chunk_of(tab[2 + l], c), chunk(pq, c)).then_inc(table_out, 16)
                    sp.dma_start(chunk_of(qtab[l], c), chunk(pq, c, 2 * D)[:, :, D:]).then_inc(qtable_out, 16)
                sp.wait_ge(q_row_in, 16 * (l + 1))
                sp.wait_ge(q_scattered, 16 * NT * (l + 1))
                sp.dma_start(q_at_start.rearrange("(p l) d -> p l d", p=P)[:, 0, :], q_row[:, l, :]
                             ).then_inc(q_row_out, 16)
                store_sums(2 + l)
            for l in range(2):
                for c in range(NC):
                    sp.wait_ge(*done(f"gh{l}", c))
                    sp.dma_start(chunk_of(tab[5 + l], c), chunk(gN, c, WG)).then_inc(table_out, 16)
                    sp.dma_start(chunk_of(adtab[l], c), chunk(adN, c, 2)).then_inc(adtab_out, 16)
                sp.wait_ge(ad_scattered, 16 * NT * (l + 1))
                sp.dma_start(ad_e[:].rearrange("p l o -> p (l o)"), ad_g).then_inc(ad_in, 16)
                for q in range(PARTS):
                    sp.wait_ge(scanned, W * (l * PARTS + q + 1))
                    at = slice(max(0, BOUNDS[q] - 1) * WG, (BOUNDS[q + 1] - (q < PARTS - 1)) * WG)
                    sp.dma_start(sums_wg[:, at], big[:, at]).then_inc(weighted_out, 16)
            full = N // P
            for c in range(NC):
                sp.wait_ge(*done("l3_norm", c))
                t = range(tiles(c).start, min(tiles(c).stop, full))
                if len(t):
                    sp.dma_start(out[t.start * P:t.stop * P].rearrange("(t p) d -> p t d", p=P),
                                 yN[:, t.start:t.stop, 0:D]).then_inc(out_done, 16)
            sp.dma_start(out[full * P:N], yN[0:N - full * P, full, 0:D]).then_inc(out_done, 16)
            sp.wait_ge(out_done, 16 * (-(-full * P // CH) + 1))

        @block.gpsimd
        def _(pool):
            def made(ins, n):
                ins.then_inc(consts_made, 1)
                pool.wait_ge(consts_made, n)

            made(pool.memset(ident[:], 0.0), 1)
            made(pool.affine_select(out=ident[:], in_=ident[:], compare_op=ALU.not_equal, fill=1.0, base=0,
                                    pattern=[[-1, P]], channel_multiplier=1), 2)
            made(pool.memset(ones[:], 1.0), 3)
            made(pool.iota(node_i[:], pattern=[[P, NTP]], base=0, channel_multiplier=1), 4)
            made(pool.iota(tail_i[:], pattern=[[1, 2]], base=L - 1, channel_multiplier=L), 5)
            made(pool.iota(FM[1].bitcast(I32), pattern=[[1, NP]], base=0, channel_multiplier=0), 6)

            def gather(out_ap, table, index):
                return pool.indirect_dma_start(out=out_ap, out_offset=None, in_=table,
                                               in_offset=bass.IndirectOffsetOnAxis(ap=index, axis=0))

            def scatter(table, index, in_ap):
                return pool.indirect_dma_start(out=table, out_offset=bass.IndirectOffsetOnAxis(ap=index, axis=0),
                                               in_=in_ap, in_offset=None, bounds_check=EP - 1, oob_is_err=False)

            def gather_pass(k, width, start=0, end=TRIPS):
                table = x_d if k == 0 else tab[k][:, :]
                if k:
                    pool.wait_ge(table_out, 16 * NC * k)
                way = PASSES[k]

                def body(i, use, make):
                    for j in range(RING):
                        s = j
                        pool.wait_ge(staged, i * RING + k * NG + j + 1)
                        pool.sem_inc(turn, 1)
                        for u in range(COLS):
                            if not (use and j * COLS + u in way.hot):
                                gather(ringG[:, s, u * width:(u + 1) * width], table,
                                       idx_s[:, s, u:u + 1]).then_inc(gathered[s], 16)

                if k:
                    way.run(pool, body)
                else:
                    with pool.Fori(start, end) as i:
                        body(i, False, False)

            def gather_sums(k):
                if k < 5:
                    for s in range(RING):
                        pool.wait_ge(slot_open[s], 16 * PASSES[k].opened(TRIPS))
                else:
                    pool.wait_ge(weighted_out, 16 * PARTS * (k - 4))
                source, width = (sums, D) if k < 5 else (sums_w, WG)
                for c in range(NC):
                    for t in tiles(c):
                        gather(gN[:, t, 0:width], source[:, :], end_i[:, t:t + 1]).then_inc(sums_in[c], 16)

            gather_pass(0, D, 0, COUNT_FROM)
            pool.wait_ge(edge_rows_ready, 1)
            for t in range(NTP):
                gather(edge_rows[:, t * L:(t + 1) * L], dst_d, edge_row_i[:, t:t + 1]).then_inc(edge_rows_in, 16)
            gather_pass(0, D, COUNT_FROM, TRIPS)
            pool.wait_ge(zeros_out, 16 * ZERO_STORES)
            pool.wait_ge(prep_done, 1)
            gather_sums(0)
            gather_pass(1, D)
            gather_sums(1)
            for l in range(NLAYER):
                for c in range(NC):
                    pool.wait_ge(*done(f"pq{l}", c))
                    for t in tiles(c):
                        scatter(q_at_start[:, :], start_i[:, t:t + 1], pq[:, t, D:]).then_inc(q_scattered, 16)
                pool.wait_ge(qtable_out, 16 * NC * (l + 1))
                gather(q_row[:, l, :], qtab[l][:, :], dst_i[:, 0:1]).then_inc(q_row_in, 16)
                gather_pass(2 + l, D)
                gather_sums(2 + l)
            for l in range(2):
                if l:
                    pool.wait_ge(ad_in, 16 * l)
                for c in range(NC):
                    pool.wait_ge(*done(f"gh{l}", c))
                    for t in tiles(c):
                        scatter(ad_at_start[:, :], start_i[:, t:t + 1], adN[:, t, :]).then_inc(ad_scattered, 16)
                pool.wait_ge(adtab_out, 16 * NC * (l + 1))
                gather(ad_row[:, l, :], adtab[l][:, :], dst_i[:, 0:1]).then_inc(ad_row_in, 16)
                gather_pass(5 + l, WG)
                pool.wait_ge(weights_ready, l + 1)
                for q in range(1, PARTS):
                    b = slice(BOUNDS[q], BOUNDS[q + 1])
                    nc.gpsimd.tensor_tensor(every[:, b, 1:WG], every[:, b, 1:WG], wgt[:, b].unsqueeze(2).to_broadcast(
                        [P, b.stop - b.start, W]), ALU.mult).then_inc(multiplied, 1)
                gather_sums(5 + l)

        @block.scalar
        def _(act):
            def stage_indices(k, i, s):
                act.wait_ge(slot_open[s], PASSES[k].opened(i) * 16)
                act.sem_inc(turn_a, 1)
                nc.scalar.copy(idx_s[:, s, :], src_i[:, bass.ds((i * RING + s) * COLS, COLS)]).then_inc(staged, 1)

            def load_edges(l, i, s):
                act.wait_ge(edge_summed, i * SLOTS + l * NG + s + 1)
                act.dma_start(ringQ[:, s, :], q_g[:, bass.ds((i * SLOTS + s) * COLS * D, COLS * D)]
                              ).then_inc(q_in[s], 16)
                act.dma_start(ringE[:, s, :], ef_d[:, bass.ds((i * SLOTS + s) * COLS * P, COLS * P)]
                              ).then_inc(ef_in[s], 16)

            def load_sources(way, i):
                act.wait_ge(src_hot_ready, way.unit(i) + 1)
                act.dma_start(of[way.k].src_all.rearrange("p (b e) -> p b e", e=P),
                              a["src_columns"][bass.ds(i * way.span + way.step - 1, way.u, way.step), :]
                              .partition_broadcast(P)).then_inc(src_all_in, 16)

            def unit_work(way, i, use, make):
                if make:
                    n = way.unit(i + 1)
                    act.wait_ge(src_all_in, (n + 1) * 16)
                    act.wait_ge(hot_ready, (n + 1) * PIECES)
                    act.sem_inc(turn_a, 1)
                    nc.scalar.copy(of[way.k].src_hot, of[way.k].src_all).then_inc(src_hot_ready, 1)
                if use:
                    n = way.unit(i)
                    act.wait_ge(hot_used, (n + 2) * PIECES)
                    act.wait_ge(parts_used, n + 1)
                    nc.scalar.copy(of[way.k].parts.rearrange("p u k d -> p u (k d)"),
                                   ps[:, 0:way.u, 0:3 * way.width]).then_inc(parts_ready, 1)

            def act_pass(k, edges=None):
                way = PASSES[k]

                def clip(group, s):
                    act.wait_ge(edge_summed, group + (edges * NG + SLOTS + 1))
                    nc.scalar.activation(ringG[:, s, 0:COLS * D], ringG[:, s, 0:COLS * D], ACT.Relu
                                         ).then_inc(clipped, 1)

                def body(i, use, make):
                    if make:
                        load_sources(way, i + 1)
                    for j in range(RING):
                        if edges is not None and (not isinstance(i, int) or i or j >= SLOTS):
                            clip(i * RING + j - SLOTS, (j - SLOTS) % RING)
                        if j != 2:
                            stage_indices(k, i, j)
                        if edges is not None:
                            load_edges(edges, way.turn(i, j), j % SLOTS)
                        if j == 1:
                            stage_indices(k, i, 2)
                            unit_work(way, i, use, make)

                way.run(act, body)
                if edges is not None:
                    for j in range(RING - SLOTS, RING):
                        clip((TRIPS - 1) * RING + j, j)

            def drain(out_ap, in_ap, fn, bias=0.0):
                return nc.scalar.activation(out_ap, in_ap, fn, bias=bias)

            def run_wave(phase, work):
                for name, c in wave(phase):
                    if WHO[name] == "A":
                        if is_filled(name):
                            act.wait_ge(*FILL(name, c))
                        work[name](c, cols(c)).then_inc(done_a, 1)

            def bank(c, lo=0, hi=D):
                n = cols(c)
                return ps[lo:hi, c, 0:n.stop - n.start]

            def turn_to(array, rows=D):
                return lambda c, n: drain(array[0:rows, n], bank(c, 0, rows), ACT.Copy)

            def std(prev):
                def go(c, n):
                    act.wait_ge(*done(prev, c))
                    t = tiles(c)
                    return drain(rstd[:, t.start:t.stop], stat[:, t.start:t.stop], ACT.Sqrt)
                return go

            for s in range(RING):
                act.sem_inc(slot_open[s], 16)
            act.sem_inc(edge_summed, SLOTS)
            act.sem_inc(src_hot_ready, 1)
            act.sem_inc(parts_ready, 1)
            act.wait_ge(src_in, 16)
            for s in range(RING):
                stage_indices(0, 0, s)
            act.wait_ge(zero_made, 1)
            act.dma_start(ad_g, FM[0][:, 0:2 * L]).then_inc(zeros_out, 16)
            act.dma_start(sums[EP:EP + 1, :], FM[0][0:1, 0:D]).then_inc(zeros_out, 16)
            act.dma_start(sums_w[EP:EP + 1, :], FM[0][0:1, 0:WG]).then_inc(zeros_out, 16)
            act.dma_start(q_g[:, 0:ZERO_W], FM[0][:, 0:ZERO_W]).then_inc(zeros_out, 16)
            with act.Fori(1, TRIPS) as i:
                for s in range(RING):
                    stage_indices(0, i, s)
                act.dma_start(q_g[:, bass.ds(i * ZERO_W, ZERO_W)], FM[0][:, 0:ZERO_W]).then_inc(zeros_out, 16)
            act.wait_ge(weights_in, 16 * len(weight_loads))
            act.wait_ge(zeros_out, 16 * ZERO_STORES)
            run_wave("gin0", {
                "l0_T": turn_to(FM[0]),
                "l0_w1": lambda c, n: drain(FM[1][0:D, n], bank(c), ACT.Relu, c0[:, 0:1]),
                "l0_w2": lambda c, n: drain(FM[2][0:D, n], bank(c), ACT.Identity, c0[:, 1:2])})
            act.wait_ge(bn_scale_ready, 1)
            nc.scalar.activation(bn[:, 3:4], bn[:, 2:3], ACT.Sqrt).then_inc(bn_done, 1)
            act.wait_ge(bn_scale_ready, 2)
            run_wave("gin0_end", {
                "l0_bn": lambda c, n: nc.scalar.activation(FM[1][0:D, n], FM[2][0:D, n], ACT.Relu, bias=bn[:, 7:8],
                                                           scale=bn[:, 5:6]),
                "l0_std": std("l0_back")})
            act_pass(1)
            run_wave("gin1", {
                "l1_T": turn_to(FM[0]),
                "l1_w1a": lambda c, n: drain(FM[1][:, n], bank(c, 0, P), ACT.Relu, c1[:, 0:1]),
                "l1_w1b": lambda c, n: drain(FM[2][:, n], bank(c, 0, P), ACT.Relu, c1[:, 1:2]),
                "l1_w2a": lambda c, n: drain(FM[3][:, n], bank(c, 0, P), ACT.Relu, c1[:, 2:3]),
                "l1_w2b": lambda c, n: drain(FM[4][:, n], bank(c, 0, P), ACT.Relu, c1[:, 3:4]),
                "l1_w3": lambda c, n: drain(FM[5][0:D, n], bank(c), ACT.Identity, c13[:]),
                "l1_std": std("l1_back"),
                "l2_T": turn_to(FM[0]),
                "enc": lambda c, n: drain(STATE[:, n], bank(c, D, P), ACT.Identity, enc_b[D:P])})
            for l in range(NLAYER):
                act.wait_ge(q_row_out, 16 * (l + 1))
                act_pass(2 + l, l)

                def gates(c, n, l=l):
                    drain(FM[4][D:P, n], bank(c), ACT.Sigmoid, b_z[0:D, l, 0:1])
                    return drain(FM[3][D:P, n], bank(c, D, P), ACT.Sigmoid, b_r[D:P, l, 0:1])

                def new_value(c, n, l=l):
                    act.wait_ge(*done(f"cell{l}", c))
                    return drain(FM[5][D:P, n], FM[5][D:P, n], ACT.Tanh, b_n[D:P, l, 0:1])

                run_wave(f"gru{l}", {
                    f"T{l}": turn_to(FM[0], W), f"agg{l}": lambda c, n: drain(FM[1][0:D, n], bank(c), ACT.Copy),
                    f"rz{l}": gates, f"tanh{l}": new_value,
                    "ro1": lambda c, n: drain(FM[2][0:D, n], bank(c), ACT.Relu, c_ro[:, 0:1]),
                    "ro2": lambda c, n: drain(FM[3][0:D, n], bank(c), ACT.Identity, c_ro[:, 1:2]),
                    "l2_std": std("l2_back"), "gT0": turn_to(FM[0])})
            for l in range(2):
                act_pass(5 + l)
                act.wait_ge(gap_ready, l + 1)
                nc.scalar.activation(wgt[:], wgt[:], ACT.Exp).then_inc(weights_ready, 1)

                def self_weight(c, n, l=l):
                    act.wait_ge(*done(f"gself{l}", c))
                    t = tiles(c)
                    return drain(self_w[:, t.start:t.stop], self_w[:, t.start:t.stop], ACT.Exp)

                run_wave(f"gat{l}", {f"gexp{l}": self_weight, "gT1": turn_to(FM[0]), "l3_std": std("gcarry1")})

        @block.vector
        def _(v):
            chain = Chain(v, vchain)
            link = chain.link

            def wide(value, width=D):
                return value.unsqueeze(2).to_broadcast([P, value.shape[1], width])

            def leaky(out_ap, in_ap):
                return v.scalar_tensor_tensor(out_ap, in_ap, SLOPE, in_ap, ALU.mult, ALU.max)

            def banked(c, width=D):
                return ps[:, c, :].rearrange("p (t d) -> p t d", d=P)[:, 0:len(tiles(c)), 0:width]

            def run_wave(phase, work):
                for name, c in wave(phase):
                    if WHO[name] == "V":
                        work[name](c).then_inc(done_v, 1)
                        v.wait_ge(*done(name, c))

            v.memset(FM[0], 0.0).then_inc(zero_made, 1)
            link(v.memset(carry[:], 0.0))
            link(v.memset(carry_q[:], 0.0))
            v.sem_inc(hot_ready, PIECES)
            v.sem_inc(parts_used, 1)
            v.wait_ge(edges_in, 5 * 16)
            link(v.tensor_copy(dst_f[:], dst_i[:]))
            link(v.memset(same[:, 0:1], 0.0))
            link(v.tensor_tensor(same[:, 1:L], dst_f[:, 1:L], dst_f[:, 0:L - 1], ALU.is_equal))
            v.wait_ge(consts_made, 6)
            link(v.tensor_copy(FM[2], FM[1].bitcast(I32)))
            v.tensor_scalar(spans[:], FM[2], dst_f[:, 0:1], None, ALU.is_gt).then_inc(rows_before, 1)
            link(v.tensor_copy(node_f[:], node_i[:]))
            link(v.tensor_copy(tail[:], tail_i[:]))
            link(v.tensor_copy(beside[:], beside_i[:]))
            link(v.memset(b_pq[:, :, 0:D], 0.0))
            link(v.memset(enc_w[:, 0:D], 0.0))
            link(v.memset(w_n[0:D, :, D:P], 0.0))
            link(v.memset(w_n[D:P, :, 0:D], 0.0))
            link(v.memset(edge_row[:], 0.0))
            v.wait_ge(counts_ready, 1)
            link(v.tensor_scalar(edge_row[:, 0:NT], ps[:, 7, 0:NT], -1.0, 0.0, ALU.add, ALU.max))
            v.tensor_copy(edge_row_i[:], edge_row[:]).then_inc(edge_rows_ready, 1)

            def running(group, u, rows, before):
                now = rows[:, u * D:(u + 1) * D]
                prev = before[:] if u == 0 else rows[:, (u - 1) * D:u * D]
                return v.scalar_tensor_tensor(now, prev, same[:, bass.ds(group * COLS + u, 1)], now, ALU.mult,
                                              ALU.add)

            def split_table(k, table):
                w, split, rest = PASSES[k].width, of[k].split, of[k].rest
                link(v.tensor_copy(split[:, :, 0:w], table))
                link(v.tensor_tensor(rest, table, split[:, :, 0:w], ALU.subtract))
                link(v.tensor_copy(split[:, :, w:2 * w], rest))
                v.tensor_tensor(split[:, :, 2 * w:], rest, split[:, :, w:2 * w], ALU.subtract).then_inc(split_ready, 1)
                v.wait_ge(split_ready, k)

            def start_piece(way, i, j):
                v.wait_ge(src_hot_ready, way.unit(i) + 2)
                v.wait_ge(hot_used, way.unit(i) * PIECES + j + 1)

            def make_tile(way, j, u):
                if u < len(PIECE_TILES[j]):
                    t = PIECE_TILES[j][u]
                    ins = v.tensor_scalar(of[way.k].hot[:, t], of[way.k].src_hot, node_f[:, t:t + 1], None, ALU.is_equal)
                    if t == PIECE_TILES[j][-1]:
                        ins.then_inc(hot_ready, 1)

            def take_products(way, i, j):
                part, both, w = of[way.k].parts, of[way.k].part_sum, way.width
                if way.hot_in(j) and way.hot_in(j)[0][1] == 0:
                    v.wait_ge(parts_ready, way.unit(i) + 2)
                    link(v.tensor_tensor(both, part[:, :, 2], part[:, :, 1], ALU.add))
                for u, n in way.hot_in(j):
                    link(v.tensor_tensor(ringG[:, j, u * w:(u + 1) * w], both[:, n], part[:, n, 0], ALU.add))
                if way.hot_in(j) and way.hot_in(j)[-1][1] == way.u - 1:
                    v.sem_inc(parts_used, 1)

            def sum_group(k, s, group, between=None):
                rows = ringG[:, s, 0:COLS * D]
                for u in range(COLS):
                    row_done = chain.mark(running(group, u, rows, carry))
                    if between is not None:
                        between(u)
                    v.wait_ge(vchain, row_done)
                v.tensor_copy(carry[:], rows[:, (COLS - 1) * D:]).then_inc(summed, 1)
                v.wait_ge(summed, group + (k * NG + 1))

            def sum_pass(k, start=0, end=TRIPS, counting=False):
                with v.Fori(start, end) as i:
                    chain.loop(i - start, RING * (COLS + 2 * counting))
                    for s in range(RING):
                        v.wait_ge(gathered[s], (i + (k * TRIPS + 1)) * 16 * COLS)
                        sum_group(k, s, i * RING + s)
                        if counting:
                            t = (i - start) * RING + s
                            link(v.tensor_scalar(logit[:], edge_rows[:, bass.ds(t * L, L)], 1.0, None, ALU.mult))
                            link(v.tensor_scalar(wgt[:], logit[:], node_f[:, bass.ds(t, 1)], 0.0, ALU.is_lt, ALU.add,
                                                 accum_out=count[:, bass.ds(t, 1)]))
                    chain.end(end - start)

            def pooled_pass(k):
                way = PASSES[k]

                def body(i, use, make):
                    links = RING * COLS + (1 + way.u if use else 0)
                    if not isinstance(i, int):
                        chain.loop(i - 1, links)
                    for j in range(RING):
                        v.wait_ge(gathered[j], way.gathered(i, j, use) * 16)
                        if use:
                            take_products(way, i, j)
                        if make:
                            start_piece(way, i + 1, j)
                        sum_group(k, j, i * RING + j, (lambda u, j=j: make_tile(way, j, u)) if make else None)
                    if not isinstance(i, int):
                        chain.end(way.last - 1)

                way.run(v, body)

            def message_pass(k, l):
                way = PASSES[k]

                def add_edge_product(group, s):
                    v.wait_ge(edge_product, group + (l * NG + 1))
                    return v.tensor_tensor(ringQ[:, s, :], ps[:, 6 + s, :], ringQ[:, s, :], ALU.add)

                def body(i, use, make):
                    looped = not isinstance(i, int)
                    if looped:
                        chain.loop(i - 1, RING * (2 * COLS + 2) + 1 + way.u)
                    for j in range(RING):
                        s, group = j % SLOTS, i * RING + j
                        q, rows = ringQ[:, s, :], ringG[:, j, 0:COLS * D]
                        after = (j + 1) % SLOTS if make or j < RING - 1 else None
                        v.wait_ge(gathered[j], way.gathered(i, j, use) * 16)
                        if use:
                            take_products(way, i, j)
                        if make:
                            start_piece(way, i + 1, j)

                        def tile(u, j=j):
                            if make:
                                make_tile(way, j, u)

                        v.tensor_tensor(rows, rows, q, ALU.add).then_inc(edge_summed, 1)
                        if after is not None:
                            v.wait_ge(q_in[after], (way.turn(i, j + 1) + (l * TURNS + 1)) * 16)
                        row_done = q_done = None
                        for x in range(COLS + AHEAD):
                            if x < COLS and after is not None:
                                if q_done is not None:
                                    v.wait_ge(vchain, q_done)
                                q_done = chain.mark(running(group + 1, x, ringQ[:, after, :], carry_q))
                            if x < AHEAD:
                                tile(x)
                            else:
                                if row_done is None:
                                    v.wait_ge(clipped, group + (l * NG + 1))
                                else:
                                    v.wait_ge(vchain, row_done)
                                row_done = chain.mark(running(group, x - AHEAD, rows, carry))
                                if AHEAD <= x < 2 * AHEAD or x >= COLS:
                                    tile(x if x < COLS else x - COLS + 2 * AHEAD)
                        v.wait_ge(vchain, chain.value())
                        v.tensor_copy(carry[:], rows[:, (COLS - 1) * D:]).then_inc(summed, 1)
                        if after is not None:
                            q_done = chain.mark(v.tensor_copy(carry_q[:], ringQ[:, after, (COLS - 1) * D:]))
                            tile(COLS - 2)
                            v.wait_ge(vchain, q_done)
                            q_done = chain.mark(add_edge_product(group + 1, after))
                            tile(COLS - 1)
                            v.wait_ge(vchain, q_done)
                        v.wait_ge(summed, group + (k * NG + 1))
                    if looped:
                        chain.end(way.last - 1)

                v.wait_ge(q_in[0], (l * TURNS + 1) * 16)
                for u in range(COLS):
                    link(running(0, u, ringQ[:, 0, :], carry_q))
                link(v.tensor_copy(carry_q[:], ringQ[:, 0, (COLS - 1) * D:]))
                link(add_edge_product(0, 0))
                way.run(v, body)

            def variance(c):
                y, t = chunk(yN, c), tiles(c)
                sq = chunk(FM[7][:, 0:NT * D].rearrange("p (t d) -> p t d", d=D), c)
                st = stat[:, t.start:t.stop]
                link(v.tensor_reduce(st, y, AX.X, ALU.add))
                link(v.tensor_scalar(st, st, 1.0 / D, None, ALU.mult))
                link(v.tensor_tensor(y, y, wide(st), ALU.subtract))
                link(v.tensor_tensor(sq, y, y, ALU.mult))
                link(v.tensor_reduce(st, sq, AX.X, ALU.add))
                return v.tensor_scalar(st, st, 1.0 / D, LN_EPS, ALU.mult, ALU.add)

            def norm(prefix, dst):
                def go(c):
                    t = tiles(c)
                    v.wait_ge(*done(prefix + "_std", c))
                    r = rstd[:, t.start:t.stop]
                    link(v.reciprocal(r, r))
                    return v.tensor_tensor(chunk(dst, c), chunk(yN, c), wide(r), ALU.mult)
                return go

            def back(name):
                def go(c):
                    v.wait_ge(*FILL(name, c))
                    link(v.tensor_tensor(chunk(yN, c), chunk(xN, c), banked(c), ALU.add))
                    return variance(c)
                return go

            def node_sums(name, k, extra):
                def go(c):
                    v.wait_ge(sums_in[c], 16 * len(tiles(c)) * (k + 1))
                    v.wait_ge(*FILL(name, c))
                    link(v.tensor_tensor(chunk(yN, c), chunk(gN, c), banked(c), ALU.add))
                    return extra(c)
                return go

            def add_x(c):
                return v.tensor_tensor(chunk(yN, c), chunk(yN, c), chunk(xN, c), ALU.add)

            def message_table(l):
                def go(c):
                    v.wait_ge(*FILL(f"pq{l}", c))
                    return v.tensor_tensor(chunk(pq, c, P), banked(c, P), b_pq[:, l, :].unsqueeze(1).to_broadcast(
                        [P, len(tiles(c)), P]), ALU.add)
                return go

            sum_pass(0, 0, COUNT_FROM)
            v.wait_ge(edge_rows_in, 16 * NTP)
            sum_pass(0, COUNT_FROM, COUNT_TO, counting=True)
            v.scalar_tensor_tensor(first[:], edge_row[:, 0:NT], float(L), count[:, 0:NT], ALU.mult, ALU.add
                                   ).then_inc(first_ready, 1)
            v.wait_ge(first_in, 48)
            link(v.tensor_tensor(has[:], nxt[:], first[:], ALU.is_gt))
            link(v.tensor_tensor(deg[:], nxt[:], first[:], ALU.subtract))
            link(v.tensor_scalar(tmp[:], nxt[:], -1.0 - EP, None, ALU.add))
            link(v.tensor_tensor(tmp[:], tmp[:], has[:], ALU.mult))
            link(v.tensor_scalar(tmp[:], tmp[:], float(EP), None, ALU.add))
            link(v.tensor_copy(end_i[:], tmp[:]))
            link(v.tensor_scalar(tmp[:], has[:], float(-SKIP), float(SKIP), ALU.mult, ALU.add))
            link(v.tensor_tensor(tmp[:], tmp[:], first[:], ALU.add))
            link(v.tensor_copy(start_i[:], tmp[:]))
            link(v.tensor_scalar(FM[1], FM[1], tail[:, 0:1], None, ALU.is_le))
            link(v.scalar_tensor_tensor(spans[:], FM[2], tail[:, 1:2], FM[1], ALU.is_gt, ALU.mult))
            link(v.tensor_scalar(pen_f[:, 1:L], same[:, 1:L], BIG, -BIG, ALU.mult, ALU.add))
            link(v.tensor_scalar(pen_b[:, 0:L - 1], same[:, 1:L], BIG, -BIG, ALU.mult, ALU.add))
            link(v.tensor_tensor(flag[:, 0:1], beside[:, 0:1], dst_f[:, 0:1], ALU.is_equal))
            link(v.tensor_tensor(flag[:, 1:2], beside[:, 1:2], dst_f[:, L - 1:L], ALU.is_equal))
            link(v.tensor_scalar(pen_f[:, 0:1], flag[:, 0:1], BIG, -BIG, ALU.mult, ALU.add))
            link(v.tensor_scalar(pen_b[:, L - 1:L], flag[:, 1:2], BIG, -BIG, ALU.mult, ALU.add))
            link(v.tensor_tensor(flag[:, 2:3], dst_f[:, 0:1], dst_f[:, L - 1:L], ALU.is_equal))
            link(v.tensor_scalar(flag[:, 0:2], flag[:, 0:2], flag[:, 2:3], None, ALU.mult))
            v.tensor_scalar(flag[:, 4:6], flag[:, 0:2], BIG, -BIG, ALU.mult, ALU.add).then_inc(pens_ready, 1)
            v.wait_ge(pens_turned, 1)
            link(v.tensor_copy(pen_row[:], ps[0:1, 7, 0:2 * P].rearrange("p (a b) -> p a b", a=2)))
            link(v.memset(car_row[:], -BIG))
            v.wait_ge(weights_in, 16 * len(weight_loads))
            link(v.tensor_tensor(b_z[0:D, :, 0], b_z[0:D, :, 0], b_z[0:D, :, 1], ALU.add))
            v.tensor_tensor(b_r[D:P, :, 0], b_r[D:P, :, 0], b_r[D:P, :, 1], ALU.add).then_inc(prep_done, 1)
            sum_pass(0, COUNT_TO, TRIPS)
            v.wait_ge(x_in, 16)

            def chunk_stats(c):
                v.wait_ge(*done("l0_w2", c))
                n = slice(c * CH, min(N, (c + 1) * CH))
                h, off = FM[2][0:D, n], FM[3][0:D, n]
                link(v.tensor_reduce(bn_chunk[:, 0, c:c + 1], h, AX.X, ALU.add))
                link(v.tensor_scalar(bn_chunk[:, 1, c:c + 1], bn_chunk[:, 0, c:c + 1], 1.0 / (n.stop - n.start), None,
                                     ALU.mult))
                link(v.tensor_scalar(off, h, bn_chunk[:, 1, c:c + 1], None, ALU.subtract))
                link(v.tensor_tensor(off, off, off, ALU.mult))
                return v.tensor_reduce(bn_chunk[:, 2, c:c + 1], off, AX.X, ALU.add)

            link(v.memset(bn_chunk[:, 3, 0:NC - 1], float(CH)))
            link(v.memset(bn_chunk[:, 3, NC - 1:NC], float(N - (NC - 1) * CH)))
            run_wave("gin0", {"l0_carry": node_sums("l0_carry", 0, add_x), "l0_stats": chunk_stats})
            link(v.tensor_reduce(bn[:, 0:1], bn_chunk[:, 0, :], AX.X, ALU.add))
            link(v.tensor_scalar(bn[:, 0:1], bn[:, 0:1], 1.0 / N, None, ALU.mult))
            off = bn_chunk[:, 1, :]
            link(v.tensor_scalar(off, off, bn[:, 0:1], None, ALU.subtract))
            link(v.tensor_tensor(off, off, off, ALU.mult))
            link(v.tensor_tensor(off, off, bn_chunk[:, 3, :], ALU.mult))
            link(v.tensor_tensor(off, off, bn_chunk[:, 2, :], ALU.add))
            link(v.tensor_reduce(bn[:, 1:2], off, AX.X, ALU.add))
            v.tensor_scalar(bn[:, 2:3], bn[:, 1:2], 1.0 / N, BN_EPS, ALU.mult, ALU.add).then_inc(bn_scale_ready, 1)
            v.wait_ge(bn_done, 1)
            link(v.reciprocal(bn[:, 4:5], bn[:, 3:4]))
            link(v.tensor_tensor(bn[:, 5:6], bn[:, 4:5], c0[:, 2:3], ALU.mult))
            link(v.tensor_tensor(bn[:, 6:7], bn[:, 0:1], bn[:, 5:6], ALU.mult))
            v.tensor_tensor(bn[:, 7:8], c0[:, 3:4], bn[:, 6:7], ALU.subtract).then_inc(bn_scale_ready, 1)
            run_wave("gin0_end", {"l0_back": back("l0_back"), "l0_norm": norm("l0", xN)})

            split_table(1, xN[:])
            pooled_pass(1)
            v.wait_ge(table_out, 16 * NC)
            run_wave("gin1", {"l1_carry": node_sums("l1_carry", 1, add_x), "l1_back": back("l1_back"),
                              "l1_norm": norm("l1", xN), "pq0": message_table(0)})

            def attention_table(l):
                def go(c):
                    v.wait_ge(*FILL(f"gh{l}", c))
                    t = tiles(c)
                    y, g, logits = chunk(yN, c), chunk(gN, c, WG), chunk(adN, c, 2)
                    prod = chunk(FM[7][:, 0:NT * D].rearrange("p (t d) -> p t d", d=D), c)
                    link(v.tensor_copy(y, banked(c)))
                    link(v.tensor_copy(g[:, :, 1:W], y))
                    link(v.memset(g[:, :, W:WG], 1.0))
                    for o, vec in ((1, g_src), (0, g_dst)):
                        link(v.tensor_tensor(prod, y, vec[:, l, :].unsqueeze(1).to_broadcast([P, len(t), D]),
                                             ALU.mult))
                        link(v.tensor_reduce(logits[:, :, o], prod, AX.X, ALU.add))
                    return v.tensor_copy(g[:, :, 0], logits[:, :, 1])
                return go

            for l in range(NLAYER):
                split_table(2 + l, pq[:, :, 0:D])
                message_pass(2 + l, l)

                def count_edges(c):
                    t = tiles(c)
                    return v.tensor_copy(yN[:, t.start:t.stop, D], deg[:, t.start:t.stop])

                def cell(c, l=l):
                    v.wait_ge(*FILL(f"cell{l}", c))
                    v.wait_ge(*done(f"rz{l}", c))
                    n = cols(c)
                    w, x = n.stop - n.start, FM[5][D:P, n]
                    link(v.scalar_tensor_tensor(x, ps[D:P, c, 0:w], b_n[D:P, l, 1:2], FM[3][D:P, n], ALU.add,
                                                ALU.mult))
                    return v.tensor_tensor(x, x, ps[0:D, c, 0:w], ALU.add)

                def state(c, l=l):
                    v.wait_ge(*done(f"tanh{l}", c))
                    n = cols(c)
                    h, x = STATE[:, n], FM[5][D:P, n]
                    link(v.tensor_tensor(h, h, x, ALU.subtract))
                    link(v.tensor_tensor(h, h, FM[4][D:P, n], ALU.mult))
                    return v.tensor_tensor(h, h, x, ALU.add)

                run_wave(f"gru{l}", {f"carry{l}": node_sums(f"carry{l}", 2 + l, count_edges), f"cell{l}": cell,
                                     f"state{l}": state, f"pq{l + 1}": message_table(l + 1),
                                     "l2_back": back("l2_back"), "l2_norm": norm("l2", xN),
                                     "gh0": attention_table(0)})

            for l in range(2):
                k = 5 + l
                way = PASSES[k]
                split_table(k, gN[:])
                v.wait_ge(ad_in, 16 * (l + 1))
                v.wait_ge(ad_row_in, 16 * (l + 1))
                link(v.tensor_copy(ad_e[:, 0, :], ad_row[:, l, :]))
                for o in range(2):
                    link(v.tensor_tensor_scan(ad_e[:, :, o], same[:], ad_e[:, :, o], 0.0, ALU.mult, ALU.add))

                def body(i, use, make, way=way):
                    looped = use and not isinstance(i, int)
                    if looped:
                        chain.loop(i - 1, 1 + way.u)
                    for j in range(RING):
                        v.wait_ge(gathered[j], way.gathered(i, j, use) * 16)
                        if use:
                            take_products(way, i, j)
                        v.tensor_scalar(big[:, bass.ds((i * RING + j) * COLS * WG, COLS * WG)], ringG[:, j, :], 1.0,
                                        None, ALU.mult).then_inc(slot_open[j], 16)
                        if make:
                            start_piece(way, i + 1, j)
                            for u in range(COLS):
                                make_tile(way, j, u)
                    if looped:
                        chain.end(way.last - 1)

                way.run(v, body)
                for s in range(RING):
                    v.wait_ge(slot_open[s], 16 * PASSES[k].opened(TRIPS))
                link(v.tensor_copy(logit[:], every[:, :, 0]))
                link(v.tensor_tensor_scan(mx_f[:], pen_f[:], logit[:], -BIG, ALU.add, ALU.max))
                v.tensor_tensor_scan(mx_b[:, ::-1], pen_b[:, ::-1], logit[:, ::-1], -BIG, ALU.add,
                                     ALU.max).then_inc(maxima_ready, 1)
                v.wait_ge(maxima_turned, l + 1)
                link(v.tensor_copy(val_row[:], ps[0:1, 7, 0:2 * P].rearrange("p (a b) -> p a b", a=2)))
                link(v.tensor_tensor_scan(car_row[:, 0, 1:P + 1], pen_row[:, 0, :], val_row[:, 0, :], -BIG,
                                          ALU.add, ALU.max))
                v.tensor_tensor_scan(car_row[:, 1, 0:P][:, ::-1], pen_row[:, 1, ::-1], val_row[:, 1, ::-1], -BIG,
                                     ALU.add, ALU.max).then_inc(carries_ready, 1)
                v.wait_ge(carries_turned, l + 1)
                link(v.tensor_copy(edge_carry[:], ps[:, 7, 0:2]))
                link(v.tensor_tensor_scan(mx_f[:], pen_f[:], logit[:], edge_carry[:, 0:1], ALU.add, ALU.max))
                link(v.tensor_tensor_scan(mx_b[:, ::-1], pen_b[:, ::-1], logit[:, ::-1], edge_carry[:, 1:2],
                                          ALU.add, ALU.max))
                link(v.tensor_tensor(mx_f[:], mx_f[:], mx_b[:], ALU.max))
                link(v.tensor_tensor(mx_f[:], mx_f[:], ad_e[:, :, 1], ALU.max))
                link(v.tensor_tensor(mx_f[:], mx_f[:], ad_e[:, :, 0], ALU.add))
                link(leaky(mx_f[:], mx_f[:]))
                link(v.tensor_tensor(logit[:], logit[:], ad_e[:, :, 0], ALU.add))
                link(leaky(logit[:], logit[:]))
                v.tensor_tensor(wgt[:], logit[:], mx_f[:], ALU.subtract).then_inc(gap_ready, 1)
                link(v.tensor_copy(every[:, :, 0], mx_f[:]))
                v.wait_ge(weights_ready, l + 1)
                n = BOUNDS[1]
                part = every[:, 0:n, 1:WG]
                link(v.tensor_tensor(part, part, wgt[:, 0:n].unsqueeze(2).to_broadcast([P, n, W]), ALU.mult))
                for q in range(PARTS):
                    if q:
                        v.wait_ge(multiplied, l * (PARTS - 1) + q)
                    b = slice(max(0, BOUNDS[q] - 1), BOUNDS[q + 1])
                    with v.Fori(0, W // UNROLL) as i:
                        for u in range(UNROLL):
                            f = i * UNROLL + u + 1
                            one = big[:, bass.ds(f + b.start * WG, b.stop - b.start, WG)]
                            v.tensor_tensor_scan(one, same[:, b], one, 0.0, ALU.mult, ALU.add).then_inc(scanned, 1)
                    v.wait_ge(scanned, W * (l * PARTS + q + 1))
                link(v.tensor_tensor(self_s[:], adN[:, :, 0], adN[:, :, 1], ALU.add))
                link(leaky(self_s[:], self_s[:]))

                def self_gap(c, k=k):
                    v.wait_ge(sums_in[c], 16 * len(tiles(c)) * (k + 1))
                    t = slice(tiles(c).start, tiles(c).stop)
                    link(v.tensor_scalar(tmp[:, t], has[:, t], BIG, -BIG, ALU.mult, ALU.add))
                    link(v.tensor_tensor(tmp[:, t], tmp[:, t], gN[:, t, 0], ALU.add))
                    link(v.tensor_tensor(tmp[:, t], tmp[:, t], self_s[:, t], ALU.max))
                    return v.tensor_tensor(self_w[:, t], self_s[:, t], tmp[:, t], ALU.subtract)

                def attend(c, l=l):
                    v.wait_ge(*FILL(f"gcarry{l}", c))
                    v.wait_ge(*done(f"gexp{l}", c))
                    t = slice(tiles(c).start, tiles(c).stop)
                    y, rows = chunk(yN, c), gN[:, t, 1:WG]
                    link(v.tensor_tensor(rows, rows, banked(c, W), ALU.add))
                    link(v.tensor_tensor(y, y, wide(self_w[:, t]), ALU.mult))
                    link(v.tensor_tensor(y, y, gN[:, t, 1:W], ALU.add))
                    link(v.tensor_tensor(tmp[:, t], gN[:, t, W], self_w[:, t], ALU.add))
                    link(v.tensor_scalar(tmp[:, t], tmp[:, t], 1e-16, None, ALU.add))
                    link(v.reciprocal(tmp[:, t], tmp[:, t]))
                    link(v.tensor_tensor(y, y, wide(tmp[:, t]), ALU.mult))
                    link(v.tensor_tensor(y, y, g_b[:, l, :].unsqueeze(1).to_broadcast([P, len(tiles(c)), D]),
                                         ALU.add))
                    if l == 0:
                        return v.tensor_scalar(y, y, 0.0, None, ALU.max)
                    link(add_x(c))
                    return variance(c)

                run_wave(f"gat{l}", {f"gself{l}": self_gap, f"gcarry{l}": attend, "gh1": attention_table(1),
                                     "l3_norm": norm("l3", yN)})

        @block.tensor
        def _(pe):
            pe.wait_ge(consts_made, 6)
            pe.wait_ge(rows_before, 1)
            for t in range(NT):
                mm = pe.matmul(ps[:, 7, t:t + 1], spans[:, t * P:(t + 1) * P], ones[:], start=True, stop=True)
            mm.then_inc(counts_ready, 1)
            pe.wait_ge(pens_ready, 1)
            pe.transpose(ps[0:1, 7, 0:P], flag[:, 4:5], ident[:])
            pe.transpose(ps[0:1, 7, P:2 * P], flag[:, 5:6], ident[:]).then_inc(pens_turned, 1)
            pe.wait_ge(weights_in, 16 * len(weight_loads))

            def run_wave(phase, work):
                names = [name for name, _ in PHASES[phase]]
                for name, c in wave(phase):
                    if is_filled(name):
                        k = names.index(name)
                        if k:
                            pe.wait_ge(*done(names[k - 1], c))
                        work[name](c).then_inc(filled, 1)

            def carries(tails, width=D):
                def go(c):
                    for j, t in enumerate(tiles(c)):
                        mm = pe.matmul(ps[:, c, j * P:j * P + width], spans[:, t * P:(t + 1) * P], tails,
                                       start=True, stop=True)
                    return mm
                return go

            def turn(source, width=D):
                def go(c):
                    for j, t in enumerate(tiles(c)):
                        mm = pe.transpose(ps[0:width, c, j * P:(j + 1) * P], source[:, t, 0:width], ident[:])
                    return mm
                return go

            def turn_back(source):
                def go(c):
                    for j, t in enumerate(tiles(c)):
                        mm = pe.transpose(ps[:, c, j * P:j * P + D], source[0:D, t * P:(t + 1) * P], ident[0:D, 0:D])
                    return mm
                return go

            def product(pairs, rows=D):
                def go(c):
                    n = cols(c)
                    for q, (wt, x) in enumerate(pairs):
                        mm = pe.matmul(ps[0:rows, c, 0:n.stop - n.start], wt, x[:, n], start=(q == 0),
                                       stop=(q == len(pairs) - 1))
                    return mm
                return go

            def node_product(x, wt, width):
                def go(c):
                    for j, t in enumerate(tiles(c)):
                        mm = pe.matmul(ps[:, c, j * P:j * P + width], x[:, t * P:(t + 1) * P], wt, start=True,
                                       stop=True)
                    return mm
                return go

            def multiply_piece(way, i, q):
                n = way.unit(i)
                if q == 0:
                    pe.wait_ge(parts_ready, n + 1)
                pe.wait_ge(hot_ready, (n + 1) * PIECES + q + 1)
                for t in PIECE_TILES[q]:
                    for u in range(way.u):
                        mm = pe.matmul(ps[:, u, 0:3 * way.width], of[way.k].hot[:, t, u * P:(u + 1) * P],
                                       of[way.k].split[:, t], start=(t == 0), stop=(t == NT - 1))
                mm.then_inc(hot_used, 1)

            def pe_pass(k, l=None):
                way = PASSES[k]
                if way.hot:
                    pe.wait_ge(split_ready, k)

                def edge_products(i, j):
                    s = j % SLOTS
                    pe.wait_ge(ef_in[s], (way.turn(i, j) + (l * TURNS + 1)) * 16)
                    for u in range(COLS):
                        mm = pe.matmul(ps[:, 6 + s, u * D:(u + 1) * D], ringE[:, s, u * P:(u + 1) * P],
                                       w_e[:, l, :], start=True, stop=True)
                    mm.then_inc(edge_product, 1)

                def body(i, use, make):
                    for j in range(RING):
                        if make and j == RING - 1:
                            multiply_piece(way, i + 1, j)
                        if l is not None and (make or j < RING - SLOTS):
                            edge_products(i, j + SLOTS)
                        if make and j < RING - 1:
                            multiply_piece(way, i + 1, j)

                if l is not None:
                    for j in range(SLOTS):
                        edge_products(0, j)
                way.run(pe, body)
                if way.hot:
                    pe.wait_ge(parts_ready, way.unit(way.last) + 2)

            pe.sem_inc(hot_used, PIECES)
            pe.wait_ge(summed, NG)
            run_wave("gin0", {"l0_carry": carries(carry[:]), "l0_T": turn(yN),
                              "l0_w1": product([(w01[:], FM[0][0:D])]), "l0_w2": product([(w02[:], FM[1][0:D])])})
            run_wave("gin0_end", {"l0_back": turn_back(FM[1])})
            pe_pass(1)
            pe.wait_ge(summed, 2 * NG)
            run_wave("gin1", {
                "l1_carry": carries(carry[:]), "l1_T": turn(yN),
                "l1_w1a": product([(w11[:, 0:P], FM[0][0:D])], P), "l1_w1b": product([(w11[:, P:HID], FM[0][0:D])], P),
                "l1_w2a": product([(w12[:, 0, 0:P], FM[1]), (w12[:, 1, 0:P], FM[2])], P),
                "l1_w2b": product([(w12[:, 0, P:HID], FM[1]), (w12[:, 1, P:HID], FM[2])], P),
                "l1_w3": product([(w13[:, 0, :], FM[3]), (w13[:, 1, :], FM[4])]), "l1_back": turn_back(FM[5]),
                "l2_T": turn(xN), "enc": product([(enc_w[:], FM[0][0:D])], P),
                "pq0": node_product(STATE, w_pq[D:P, 0, :], 2 * D)})
            for l in range(NLAYER):
                pe.wait_ge(*done(f"pq{l}", NC - 1))
                pe_pass(2 + l, l)
                pe.wait_ge(summed, (3 + l) * NG)
                work = {f"carry{l}": carries(carry[:]), f"T{l}": turn(yN, W),
                        f"agg{l}": product([(w_m2[:, l, :], FM[0][0:W])]),
                        f"rz{l}": product([(w_rz[:, l, :], FM[1])], P), f"cell{l}": product([(w_n[:, l, :], FM[1])], P),
                        "ro1": product([(ro1[D:P], STATE)]), "ro2": product([(ro2[:], FM[2][0:D])]),
                        "l2_back": turn_back(FM[3]), "gT0": turn(xN),
                        "gh0": node_product(FM[0][0:D], gw[:, 0, :], D)}
                if l < NLAYER - 1:
                    work[f"pq{l + 1}"] = node_product(STATE, w_pq[D:P, l + 1, :], 2 * D)
                run_wave(f"gru{l}", work)
            for l in range(2):
                pe_pass(5 + l)
                pe.wait_ge(maxima_ready, l + 1)
                pe.transpose(ps[0:1, 7, 0:P], mx_f[:, L - 1:L], ident[:])
                pe.transpose(ps[0:1, 7, P:2 * P], mx_b[:, 0:1], ident[:]).then_inc(maxima_turned, 1)
                pe.wait_ge(carries_ready, l + 1)
                pe.transpose(ps[:, 7, 0:1], car_row[:, 0, 0:P], ones[0:1, :])
                pe.transpose(ps[:, 7, 1:2], car_row[:, 1, 1:P + 1], ones[0:1, :]).then_inc(carries_turned, 1)
                pe.wait_ge(scanned, (l + 1) * PARTS * W)
                run_wave(f"gat{l}", {f"gcarry{l}": carries(every[:, L - 1, 1:WG], W), "gT1": turn(yN),
                                     "gh1": node_product(FM[0][0:D], gw[:, 1, :], D)})


_LAID_OUT = ("x", "src", "dst", "edge_attr_16")


def kernel(**inputs):
    import numpy as np
    import concourse.bacc as bacc
    from concourse.bass_utils import run_bass_kernel_spmd as run

    nc = bacc.Bacc("TRN2", target_bir_lowering=False, num_devices=1)
    arrays = {k: np.ascontiguousarray(v) for k, v in inputs.items() if k not in _LAID_OUT}
    x, src, dst, ef = (np.asarray(inputs[k]) for k in _LAID_OUT)
    arrays["x"] = np.concatenate([x, np.zeros((NP - N, D), x.dtype)])
    arrays["src"] = np.concatenate([src, np.zeros(EP - E, src.dtype)]).reshape(P, L)
    arrays["dst"] = np.concatenate([dst, np.full(EP - E, N, dst.dtype)]).reshape(P, L)
    arrays["none"] = np.full((1, 1), -1, dst.dtype)
    arrays["src_columns"] = np.ascontiguousarray(arrays["src"].T)
    padded = np.concatenate([ef, np.zeros((EP - E, EF), ef.dtype)]).reshape(P, L, EF)
    arrays["edge_attr_16"] = np.ascontiguousarray(padded.transpose(2, 1, 0)).reshape(EF, L * P)
    aps = {k: nc.dram_tensor(f"in_{k}", v.shape, mybir.dt.from_np(v.dtype), kind="ExternalInput").ap()
           for k, v in arrays.items()}
    out = nc.dram_tensor("out_nodes", (N, D), F32, kind="ExternalOutput").ap()
    build(nc, aps, out)
    r = run(nc, [{f"in_{k}": v for k, v in arrays.items()}], core_ids=[0])
    return r.results[0]["out_nodes"]
```
